# Optimizing a Trainium2 kernel written in Bass

```python
import numpy as np
import jax
import jax.numpy as jnp

def _softmax(x, axis=-1):
    return jax.nn.softmax(x, axis=axis)

def _gelu(x):
    return jax.nn.gelu(x, approximate=True)

def _silu(x):
    return jax.nn.silu(x)

def _sigmoid(x):
    return jax.nn.sigmoid(x)

def _layernorm(x, axis=-1, eps=1e-05):
    m = jnp.mean(x, axis=axis, keepdims=True)
    v = jnp.var(x, axis=axis, keepdims=True)
    return (x - m) / jnp.sqrt(v + eps)

def _scatter_add(tgt, idx, src, axis=0):
    return tgt.at[idx].add(src)

def _segment_sum(src, seg, n):
    return jax.ops.segment_sum(src, seg, n)
kernel_name = 'mk_vit_tower_cls_d1_tok_img1024_r4_618f38'

def setup_inputs(seed: int=0):
    np.random.seed(seed)
    _w = jnp.asarray

    def _rec_inputs():
        import jax
        import jax.numpy as jnp
        _rk = jax.random.key(seed)
        x = -0.00016672 + 0.999947 * jax.random.normal(jax.random.fold_in(_rk, 1), (32, 3, 96, 96), jnp.float32)
        cls_tok = 0.02 * jax.random.normal(jax.random.fold_in(_rk, 5), (1, 1, 256), jnp.float32)
        return (x, cls_tok)
    x, cls_tok = _rec_inputs()

    def _L0_tok_setup():
        import jax, jax.numpy as jnp
        import numpy as np
        PATCH = 16
        EPS = 1e-05

        def _patchify(x, p):
            B, C, H, W = x.shape
            hp, wp = (H // p, W // p)
            x = x.reshape(B, C, hp, p, wp, p)
            x = x.transpose(0, 2, 4, 1, 3, 5)
            return x.reshape(B, hp * wp, C * p * p)
        key = jax.random.key(seed)
        ks = jax.random.split(key, 6)
        B, C, H = (64, 3, 96)
        E = 256
        P = PATCH
        N = (H // P) ** 2
        D = C * P * P
        x = jax.random.normal(ks[0], (B, C, H, H), dtype=jnp.float32)
        W = jax.random.normal(ks[1], (D, E), dtype=jnp.float32) * (1.0 / np.sqrt(D))
        b = jnp.zeros((E,), dtype=jnp.float32)
        cls_token = jax.random.normal(ks[2], (1, 1, E), dtype=jnp.float32) * 0.02
        pos_embedding = jax.random.normal(ks[3], (1, N + 1, E), dtype=jnp.float32) * 0.02
        gamma = jnp.ones((E,), dtype=jnp.float32)
        beta = jnp.zeros((E,), dtype=jnp.float32)
        return {'x': x, 'W': W, 'b': b, 'cls_token': cls_token, 'pos_embedding': pos_embedding, 'gamma': gamma, 'beta': beta}
    _L0_tok_all = _L0_tok_setup()
    _L0_tok_in = {k: v for k, v in _L0_tok_all.items() if k in ('W', 'b', 'cls_token', 'pos_embedding', 'gamma', 'beta')}
    del _L0_tok_all

    def _L0_attn_setup():
        import jax, jax.numpy as jnp
        import numpy as np
        HIDDEN, HEADS, HDIM = (256, 8, 64)
        B, S = (4, 2048)
        LN_EPS = 1e-06
        key = jax.random.key(seed)
        ks = jax.random.split(key, 12)
        inner = HEADS * HDIM
        sd = HIDDEN ** (-0.5)
        return {'x': jax.random.normal(ks[0], (B, S, HIDDEN), jnp.float32), 'Wq': jax.random.normal(ks[1], (HIDDEN, inner), jnp.float32) * sd, 'bq': jnp.zeros((inner,), jnp.float32), 'Wk': jax.random.normal(ks[2], (HIDDEN, inner), jnp.float32) * sd, 'bk': jnp.zeros((inner,), jnp.float32), 'Wv': jax.random.normal(ks[3], (HIDDEN, inner), jnp.float32) * sd, 'bv': jnp.zeros((inner,), jnp.float32), 'Wo': jax.random.normal(ks[4], (inner, HIDDEN), jnp.float32) * inner ** (-0.5), 'bo': jnp.zeros((HIDDEN,), jnp.float32), 'alpha': jnp.ones((HEADS, HDIM), jnp.float32), 'aug_param': jax.random.normal(ks[5], (1, HEADS, HDIM), jnp.float32), 'ln_scale': jnp.ones((HIDDEN,), jnp.float32), 'ln_bias': jnp.zeros((HIDDEN,), jnp.float32)}
    _L0_attn_all = _L0_attn_setup()
    _L0_attn_in = {k: v for k, v in _L0_attn_all.items() if k in ('Wq', 'bq', 'Wk', 'bk', 'Wv', 'bv', 'Wo', 'bo', 'alpha', 'aug_param', 'ln_scale', 'ln_bias')}
    del _L0_attn_all

    def _L0_ffn_setup():
        import jax, jax.numpy as jnp
        import numpy as np
        NUM_EXPERTS = 8
        CAPACITY = 1024
        key = jax.random.key(seed)
        ks = jax.random.split(key, 5)
        dim, hidden = (256, 512)
        x = jax.random.normal(ks[0], (4, 1024, dim), dtype=jnp.float32)
        wg = jax.random.normal(ks[1], (dim, NUM_EXPERTS), dtype=jnp.float32) * 0.02
        w1 = jax.random.normal(ks[2], (NUM_EXPERTS, dim, hidden), dtype=jnp.float32) * 0.02
        w3 = jax.random.normal(ks[3], (NUM_EXPERTS, dim, hidden), dtype=jnp.float32) * 0.02
        w2 = jax.random.normal(ks[4], (NUM_EXPERTS, hidden, dim), dtype=jnp.float32) * 0.02
        return {'x': x, 'wg': wg, 'w1': w1, 'w3': w3, 'w2': w2}
    _L0_ffn_all = _L0_ffn_setup()
    _L0_ffn_in = {k: v for k, v in _L0_ffn_all.items() if k in ('wg', 'w1', 'w3', 'w2')}
    del _L0_ffn_all
    return {'x': x, 'cls_tok': cls_tok, 'L0_tok_W': _L0_tok_in['W'], 'L0_tok_b': _L0_tok_in['b'], 'L0_tok_cls_token': _L0_tok_in['cls_token'], 'L0_tok_pos_embedding': _L0_tok_in['pos_embedding'], 'L0_tok_gamma': _L0_tok_in['gamma'], 'L0_tok_beta': _L0_tok_in['beta'], 'L0_attn_Wq': _L0_attn_in['Wq'], 'L0_attn_bq': _L0_attn_in['bq'], 'L0_attn_Wk': _L0_attn_in['Wk'], 'L0_attn_bk': _L0_attn_in['bk'], 'L0_attn_Wv': _L0_attn_in['Wv'], 'L0_attn_bv': _L0_attn_in['bv'], 'L0_attn_Wo': _L0_attn_in['Wo'], 'L0_attn_bo': _L0_attn_in['bo'], 'L0_attn_alpha': _L0_attn_in['alpha'], 'L0_attn_aug_param': _L0_attn_in['aug_param'], 'L0_attn_ln_scale': _L0_attn_in['ln_scale'], 'L0_attn_ln_bias': _L0_attn_in['ln_bias'], 'L0_ffn_wg': _L0_ffn_in['wg'], 'L0_ffn_w1': _L0_ffn_in['w1'], 'L0_ffn_w3': _L0_ffn_in['w3'], 'L0_ffn_w2': _L0_ffn_in['w2']}

def reference(x, cls_tok, L0_tok_W, L0_tok_b, L0_tok_cls_token, L0_tok_pos_embedding, L0_tok_gamma, L0_tok_beta, L0_attn_Wq, L0_attn_bq, L0_attn_Wk, L0_attn_bk, L0_attn_Wv, L0_attn_bv, L0_attn_Wo, L0_attn_bo, L0_attn_alpha, L0_attn_aug_param, L0_attn_ln_scale, L0_attn_ln_bias, L0_ffn_wg, L0_ffn_w1, L0_ffn_w3, L0_ffn_w2):
    import jax
    import jax.numpy as jnp

    def _L0_tok_ref(x, W, b, cls_token, pos_embedding, gamma, beta):
        import jax, jax.numpy as jnp
        import numpy as np
        PATCH = 16
        EPS = 1e-05

        def _patchify(x, p):
            B, C, H, W = x.shape
            hp, wp = (H // p, W // p)
            x = x.reshape(B, C, hp, p, wp, p)
            x = x.transpose(0, 2, 4, 1, 3, 5)
            return x.reshape(B, hp * wp, C * p * p)
        B = x.shape[0]
        patches = _patchify(x, PATCH)
        tok = jnp.einsum('bnd,de->bne', patches, W) + b
        cls = jnp.broadcast_to(cls_token, (B, 1, tok.shape[-1]))
        h = jnp.concatenate([cls, tok], axis=1) + pos_embedding
        mu = jnp.mean(h, axis=-1, keepdims=True)
        var = jnp.mean(jnp.square(h - mu), axis=-1, keepdims=True)
        out = (h - mu) * jax.lax.rsqrt(var + EPS) * gamma + beta
        return out

    def _L0_attn_ref(x, Wq, bq, Wk, bk, Wv, bv, Wo, bo, alpha, aug_param, ln_scale, ln_bias):
        import jax, jax.numpy as jnp
        import numpy as np
        HIDDEN, HEADS, HDIM = (256, 8, 64)
        B, S = (4, 2048)
        LN_EPS = 1e-06
        b, s, _ = x.shape
        h, d = alpha.shape
        scale = d ** (-0.5)
        q = (x @ Wq + bq).reshape(b, s, h, d)
        k = (x @ Wk + bk).reshape(b, s, h, d)
        v = (x @ Wv + bv).reshape(b, s, h, d)
        decay = jax.nn.sigmoid(alpha)

        def step(state, qkv):
            q_t, k_t, v_t = qkv
            attn = jax.nn.softmax(jnp.einsum('bhd,bhd->bh', q_t, k_t) * scale, axis=-1)
            new_state = decay * state + (1.0 - decay) * attn[..., None] * v_t
            return (new_state, new_state)
        qs = jnp.moveaxis(q, 1, 0)
        ks_ = jnp.moveaxis(k, 1, 0)
        vs = jnp.moveaxis(v, 1, 0)
        init = jnp.zeros((b, h, d), x.dtype)
        _, states = jax.lax.scan(step, init, (qs, ks_, vs))
        states = jnp.moveaxis(states, 0, 1)
        aug = jax.nn.sigmoid(q * aug_param)
        out = (q * states + aug).reshape(b, s, h * d)
        out = out @ Wo + bo
        mean = jnp.mean(out, axis=-1, keepdims=True)
        var = jnp.var(out, axis=-1, keepdims=True)
        return (out - mean) * jax.lax.rsqrt(var + LN_EPS) * ln_scale + ln_bias

    def _L0_ffn_ref(x, wg, w1, w3, w2):
        import jax, jax.numpy as jnp
        import numpy as np
        NUM_EXPERTS = 8
        CAPACITY = 1024
        bz, slen, dim = x.shape
        xt = x.reshape(bz * slen, dim)
        scores = jax.nn.softmax(xt @ wg, axis=-1)
        top_scores, sel = jax.lax.top_k(scores.T, CAPACITY)
        token_idx = sel.reshape(-1)
        routed = xt[token_idx] * top_scores.reshape(-1, 1)
        routed = routed.reshape(NUM_EXPERTS, CAPACITY, dim)
        h = jax.nn.silu(jnp.einsum('ecd,edh->ech', routed, w1)) * jnp.einsum('ecd,edh->ech', routed, w3)
        routed_out = jnp.einsum('ech,ehd->ecd', h, w2).reshape(-1, dim)
        out = jnp.zeros_like(xt).at[token_idx].add(routed_out)
        return out.reshape(bz, slen, dim)
    h = _L0_tok_ref(x, L0_tok_W, L0_tok_b, L0_tok_cls_token, L0_tok_pos_embedding, L0_tok_gamma, L0_tok_beta)
    h = jnp.concatenate([jnp.broadcast_to(cls_tok, (h.shape[0], 1, h.shape[2])), h], axis=1)
    h = h + _L0_attn_ref(_layernorm(h, axis=-1), L0_attn_Wq, L0_attn_bq, L0_attn_Wk, L0_attn_bk, L0_attn_Wv, L0_attn_bv, L0_attn_Wo, L0_attn_bo, L0_attn_alpha, L0_attn_aug_param, L0_attn_ln_scale, L0_attn_ln_bias)
    h = h + _L0_ffn_ref(_layernorm(h, axis=-1), L0_ffn_wg, L0_ffn_w1, L0_ffn_w3, L0_ffn_w2)
    return h

_drawn_inputs = setup_inputs


def setup_inputs(seed=0):
    import zlib

    import numpy as np

    out = dict(_drawn_inputs(seed))
    spreads = {'L0_tok_b': (0.0, 0.1),
     'L0_tok_gamma': (1.0, 0.2),
     'L0_tok_beta': (0.0, 0.1),
     'L0_attn_bq': (0.0, 0.31),
     'L0_attn_bk': (0.0, 0.8),
     'L0_attn_bv': (0.0, 0.557),
     'L0_attn_bo': (0.0, 0.1),
     'L0_attn_alpha': (1.0, 0.6),
     'L0_attn_ln_scale': (1.0, 0.2),
     'L0_attn_ln_bias': (0.0, 0.1)}
    factors = {'L0_ffn_wg': 8.0, 'L0_ffn_w1': 8.0, 'L0_ffn_w3': 8.0, 'L0_ffn_w2': 8.0}
    for name, (base, spread) in spreads.items():
        noise = np.random.default_rng([zlib.crc32(name.encode()), seed]).standard_normal(out[name].shape)
        drawn = base * np.exp(spread * noise) if base else spread * noise
        out[name] = jnp.asarray(drawn.astype(out[name].dtype))
    for name, factor in factors.items():
        out[name] = (out[name] * factor).astype(out[name].dtype)
    return out
```

```python
from contextlib import ExitStack

import concourse.bass as bass
from concourse import mybir

F32 = mybir.dt.float32
F16 = mybir.dt.float16
I32 = mybir.dt.int32
ALU = mybir.AluOpType
ACT = mybir.ActivationFunctionType
AX = mybir.AxisListType.X

P = 128
B = 32
C, SIDE, PATCH = 3, 96, 16
NPATCH = (SIDE // PATCH) ** 2
T = B * NPATCH
NSP = 2
S = NPATCH + NSP
E = 256
EK = E // P
D = C * PATCH * PATCH
DK = D // P
HEADS, HDIM = 8, 64
INNER = HEADS * HDIM
MK = INNER // P
NEXP = 8
HID = 512
HK = HID // P
CAP = 1024

TILES = T // P
SLOTS = TILES + 1
NCH = 3
TPC = TILES // NCH
CW = TPC * P
TC = NPATCH // NCH
COLS = NSP + T
SEG = TC + 1
BANK = 512

SX, SW, SY, SO, SXS, ST_ = 64.0, 256.0, 256.0, 64.0, 1024.0, 16.0
SA = 4096.0
MAGIC = float(0x5F3759DF)
TIE_BIG = 2048.0
ROUNDS = 15
NCAND = 3

K_ONES, K_W32, K_EARLIER, K_SAME, K_LOWER, K_SPEC = (i * P for i in range(6))
K_TRI = 6 * P
K_COEF = K_TRI + B
K_SPSEL = K_COEF + 2 * B
K_ID16 = K_SPSEL + 2
K_SPREAD = K_ID16 + P
K16 = K_SPREAD + INNER
K_IDENT, K_BLK, K_BIT = 0, P, P + MK * HEADS
K32 = K_BIT + 1


def slots_of(c):
    return list(range(0 if c == 0 else 1 + TPC * c, 1 + TPC * (c + 1)))


def col0(c):
    return 0 if c == 0 else NSP + CW * c


def width(c):
    return CW + (NSP if c == 0 else 0)


def slot_cols(s, c):
    if s == 0:
        return 0, NSP
    return (NSP if c == 0 else 0) + (s - 1 - TPC * c) * P, P


def vit_tower(nc, xT, cls_tok, tok_w, tok_b, cls_token, pos, gamma, beta, wqkv, bqkv, wo, bo, alpha, aug,
              ln_scale, ln_bias, wg, w13, w2, k16_in, k32_in, cand_in, out_patch, out_spec):
    with ExitStack() as ctx:
        def sb(name, shape, dt=F32):
            return ctx.enter_context(nc.sbuf_tensor(name, shape, dt))

        def sem(name):
            return ctx.enter_context(nc.semaphore(name))

        bank = [ctx.enter_context(nc.psum_tensor(f"bank{i}", [P, BANK], F32)) for i in range(8)]
        score_rows = nc.dram_tensor("score_rows", (NEXP, COLS), F32, kind="Internal").ap()

        k16 = sb("k16", [P, K16], F16)
        k32 = sb("k32", [P, K32])
        cand = sb("cand", [P, NCAND], I32)
        ident = k32[:, K_IDENT:K_IDENT + P]
        blk = k32[:, K_BLK:K_BLK + MK * HEADS].rearrange("p (m h) -> p m h", m=MK)
        bit = k32[:, K_BIT:K_BIT + 1]
        gam, bet, tokb, bob, lns, lnb = (sb(n, [P, E]) for n in ("gam", "bet", "tokb", "bob", "lns", "lnb"))
        chan = sb("chan", [P, 5, MK])
        bk_s = sb("bk_s", [P, MK])
        v_scale = sb("v_scale", [P, MK])
        v_bias = sb("v_bias", [P, MK])
        decay = sb("decay", [P, MK])
        ez = sb("ez", [P, MK])
        half32 = sb("half32", [P, 1])
        zero16 = sb("zero16", [P, P], F16)
        cls_sb = sb("cls_sb", [1, E])
        wg_sb = sb("wg_sb", [P, EK, NEXP])

        tw, twh, twl = sb("tw", [P, DK, E]), sb("twh", [P, DK, E], F16), sb("twl", [P, DK, E], F16)
        qw, qwh, qwl = (sb(n, [P, 3, EK, INNER], d) for n, d in (("qw", F32), ("qwh", F16), ("qwl", F16)))
        ow, owh, owl = (sb(n, [P, MK, E], d) for n, d in (("ow", F32), ("owh", F16), ("owl", F16)))

        H = sb("H", [P, SLOTS, E])
        Y = sb("Y", [P, SLOTS, E])
        y2T = sb("y2T", [P, EK, COLS])

        LATE = 16384
        front = sb("front", [P, LATE])
        place = [0]

        def at(shape, dt=F32):
            n = 1
            for x in shape:
                n *= x
            words = n if dt != F16 else (n + 1) // 2
            v = front[:, place[0]:place[0] + words]
            place[0] += words
            assert place[0] <= LATE, place[0]
            if dt == F16:
                v = v.bitcast(F16)
            names = [f"a{i}" for i in range(len(shape))]
            if len(shape) == 1:
                return v
            return v.rearrange(f"p ({' '.join(names)}) -> p {' '.join(names)}",
                               **{a: x for a, x in zip(names[1:], shape[1:])})

        px = at([NCH, DK, CW])
        pxh, pxl = at([NCH, DK, CW], F16), at([NCH, DK, CW], F16)
        yTh, yTl = at([EK, CW + NSP], F16), at([EK, CW + NSP], F16)
        oTh, oTl = at([MK, CW + NSP], F16), at([MK, CW + NSP], F16)
        place[0] = 0
        q = at([MK, CW + NSP])
        qk = at([MK, CW + NSP])
        vp = at([MK, CW + NSP])
        th = at([MK, CW + NSP])
        assert place[0] <= NCH * DK * CW
        place[0] = NCH * DK * CW
        U = at([MK * B * SEG])
        STt = at([MK * B * SEG])
        DEC = at([MK * B * SEG])
        assert place[0] <= 2 * NCH * DK * CW
        Us = U.rearrange("p (m b t) -> p m b t", m=MK, b=B)
        STs = STt.rearrange("p (m b t) -> p m b t", m=MK, b=B)
        DECs = DEC.rearrange("p (m b t) -> p m b t", m=MK, b=B)

        place[0] = 0
        X32 = at([EK, COLS])
        sB = at([2, COLS])
        xh, xl = at([2, EK, COLS], F16), at([2, EK, COLS], F16)
        sg = at([2, CW + NSP])
        Tt = at([2, CW + NSP])
        Hh, Hl = at([2, HK, CW + NSP], F16), at([2, HK, CW + NSP], F16)
        OUT = at([TILES, E])

        wst = sb("wst", [P, 2, 3 * EK * HID])
        wh = sb("wh", [P, 2, 3 * EK * HID], F16)
        wl = sb("wl", [P, 2, 3 * EK * HID], F16)

        def w13_of(w, par, which, k, m):
            o = (which * EK + k) * HID + m * P
            return w[:, par, o:o + P]

        def w2_of(w, par, m):
            o = 2 * EK * HID + m * E
            return w[:, par, o:o + E]

        stats = sb("stats", [P, 4, 6])
        mv = sb("mv", [P, 4, 2])
        ve, ri, na, nb_ = (sb(n, [P, 4]) for n in ("ve", "ri", "na", "nb_"))
        sh = sb("sh", [P, 4], I32)
        mx = sb("mx", [P, 4])
        dd = sb("dd", [P, 4, HEADS])
        ex = sb("ex", [P, 4, HEADS])
        sm = sb("sm", [P, 4])
        attn = sb("attn", [P, 4, HEADS])
        attn_hl = sb("attn_hl", [P, 4, 2, HEADS], F16)
        attn_T = sb("attn_T", [2 * HEADS, CW + NSP], F16)
        us2 = sb("us2", [P, MK, NSP])
        sp_state = sb("sp_state", [P, MK, NSP])
        sp_tmp = sb("sp_tmp", [P, MK])
        SC = sb("SC", [P, SLOTS, NEXP])
        SM = sb("SM", [P, SLOTS, NEXP])
        lo = sb("lo", [P, NEXP], I32)
        mid = sb("mid", [P, NCAND, NEXP], I32)
        ge = sb("ge", [P, SLOTS, NCAND, NEXP], F16)
        fl = sb("fl", [P, NCAND, NEXP])
        inc = sb("inc", [P, NEXP], I32)
        gt = sb("gt", [P, SLOTS, NEXP], F16)
        eq = sb("eq", [P, SLOTS, NEXP], F16)
        esum = sb("esum", [P, NEXP], F16)
        room = sb("room", [P, NEXP])
        allow = sb("allow", [P, SLOTS, NEXP])
        allow_sp = sb("allow_sp", [P, 2, NEXP], F16)
        tri_e = sb("tri_e", [P, B, 2, NEXP], F16)
        sp_e = sb("sp_e", [P, B, 2, NEXP], F16)
        asp = sb("asp", [P, 2, NEXP])
        msp = sb("msp", [P, B, 2, NEXP])
        keep = sb("keep", [P, TILES, NEXP])
        rows = sb("rows", [P, P])
        rows_sp = sb("rows_sp", [NEXP, NSP])
        ysp = sb("ysp", [P, EK, NEXP, NSP])
        h2sp = sb("h2sp", [P, EK, NSP])
        prod = sb("prod", [P, B, NEXP])
        osp = sb("osp", [P, EK, NSP, B])

        px_in = [sem(f"px_in{c}") for c in range(NCH)]
        tokw_in, slot0_in, vec_in, const_in = sem("tokw_in"), sem("slot0_in"), sem("vec_in"), sem("const_in")
        qkvw_in, wo_in, cls_in = sem("qkvw_in"), sem("wo_in"), sem("cls_in")
        ew_in = [sem("ew_in0"), sem("ew_in1")]
        sB_in = [sem("sB_in0"), sem("sB_in1")]
        rows_out, out_done = sem("rows_out"), sem("out_done")
        zeroed, posb_ready = sem("zeroed"), sem("posb_ready")
        tokw_hi, qkvw_hi, wo_hi = sem("tokw_hi"), sem("qkvw_hi"), sem("wo_hi")
        tokw_lo, qkvw_lo, wo_lo = sem("tokw_lo"), sem("qkvw_lo"), sem("wo_lo")
        px_hi, px_lo = sem("px_hi"), sem("px_lo")
        dve_step, act_step, pool_step = sem("dve_step"), sem("act_step"), sem("pool_step")
        tok_mm, tok_read = sem("tok_mm"), sem("tok_read")
        y_ready, yT_mm, yT_hi, yT_lo = sem("y_ready"), sem("yT_mm"), sem("yT_hi"), sem("yT_lo")
        q_mm, k_mm, v_mm = sem("q_mm"), sem("k_mm"), sem("v_mm")
        q_read, qk_ready, v_read = sem("q_read"), sem("qk_ready"), sem("v_read")
        chan_ready, chan_e = sem("chan_ready"), sem("chan_e")
        logit_mm, logit_sub, exp_ready, attn_ready = (sem("logit_mm"), sem("logit_sub"), sem("exp_ready"),
                                                      sem("attn_ready"))
        attn_T_mm, attn_T_ready = sem("attn_T_mm"), sem("attn_T_ready")
        aB_mm, u_ready = sem("aB_mm"), sem("u_ready")
        th_ready, o_ready, o_hi, o_lo = sem("th_ready"), sem("o_ready"), sem("o_hi"), sem("o_lo")
        wo_mm, wo_read = sem("wo_mm"), sem("wo_read")
        y2_ready, y2T_mm, y2T_ready = sem("y2_ready"), sem("y2T_mm"), sem("y2T_ready")
        gate_mm, gate_sub, gexp_ready, gate_free = (sem("gate_mm"), sem("gate_sub"), sem("gexp_ready"),
                                                    sem("gate_free"))
        ge_ready, count_mm, cut_ready = sem("ge_ready"), sem("count_mm"), sem("cut_ready")
        tie_ready, rank_mm, sm_ready, rows_mm, rows_ready = (sem("tie_ready"), sem("rank_mm"), sem("sm_ready"),
                                                             sem("rows_mm"), sem("rows_ready"))
        ew_hi, ew_lo = sem("ew_hi"), sem("ew_lo")
        xs_ready, xs_hi, xs_lo = sem("xs_ready"), sem("xs_hi"), sem("xs_lo")
        g_mm, u_mm, silu_ready, t_ready = sem("g_mm"), sem("u_mm"), sem("silu_ready"), sem("t_ready")
        h_hi, h_lo, dn_mm = sem("h_hi"), sem("h_lo"), sem("dn_mm")
        out_ready, osp_ready = sem("out_ready"), sem("osp_ready")

        block = ctx.enter_context(nc.Block())

        class Steps:

            def __init__(self, eng, s):
                self.eng, self.s, self.n = eng, s, 0

            def did(self, ins):
                self.n += 1
                ins.then_inc(self.s, 1)

            def wait(self):
                self.eng.wait_ge(self.s, self.n)

            def then(self, ins):
                self.did(ins)
                self.wait()

        ORDER = [("tok", 0), ("tok", 1), ("tok", 2), ("yT", 0), ("qkv", 0), ("yT", 1), ("soft", 0), ("state", 0),
                 ("qkv", 1), ("out", 0), ("yT", 2), ("soft", 1), ("state", 1), ("qkv", 2), ("out", 1),
                 ("y2T", 0), ("soft", 2), ("state", 2), ("y2T", 1), ("out", 2), ("y2T", 2)]

        def units(unit, loop):
            unit(0, 0, 0)
            unit(0, 0, 1)
            with loop(0, NEXP // 2 - 1) as pair:
                for par in range(2):
                    e = pair * 2 + par
                    unit(e, par, 2)
                    unit(e + 1, 1 - par, 0)
                    unit(e + 1, 1 - par, 1)
            for e, c in ((NEXP - 2, 2), (NEXP - 1, 0), (NEXP - 1, 1), (NEXP - 1, 2)):
                unit(e, e % 2, c)

        @block.sync
        def _(sp):
            sp.dma_start(tw[:], tok_w).then_inc(tokw_in, 16)
            for c in range(NCH):
                sp.dma_start(px[:, c], xT[:, c]).then_inc(px_in[c], 16)
            sp.dma_start(gam[:], gamma.to_broadcast([P, E])).then_inc(vec_in, 16)
            sp.dma_start(bet[:], beta.to_broadcast([P, E])).then_inc(vec_in, 16)
            sp.dma_start(bob[:], bo.to_broadcast([P, E])).then_inc(vec_in, 16)
            sp.dma_start(lns[:], ln_scale.to_broadcast([P, E])).then_inc(vec_in, 16)
            sp.dma_start(lnb[:], ln_bias.to_broadcast([P, E])).then_inc(vec_in, 16)
            sp.dma_start(qw[:], wqkv).then_inc(qkvw_in, 16)
            sp.dma_start(ow[:], wo).then_inc(wo_in, 16)
            sp.dma_start(wg_sb[:], wg).then_inc(wo_in, 16)

            def load_expert(e, par):
                sp.dma_start(wst[:, par, 0:2 * EK * HID], w13[e]).then_inc(ew_in[par], 16)
                sp.dma_start(wst[:, par, 2 * EK * HID:], w2[e]).then_inc(ew_in[par], 16)

            def load_scores(e, par):
                sp.dma_start(sB[:, par], score_rows[bass.ds(e, 1), :].to_broadcast([P, COLS])).then_inc(sB_in[par], 16)

            load_expert(0, 0)
            load_expert(1, 1)
            sp.wait_ge(rows_ready, 2)
            sp.dma_start(score_rows[:, NSP:COLS].rearrange("e (s n) -> s e n", n=P),
                         rows[0:TILES * NEXP, :]).then_inc(rows_out, 16)
            sp.dma_start(score_rows[:, 0:NSP], rows_sp[:]).then_inc(rows_out, 16)
            sp.wait_ge(rows_out, 32)
            load_scores(0, 0)
            load_scores(1, 1)
            with sp.Fori(1, NEXP // 2) as pair:
                for par in range(2):
                    e = pair * 2 + par
                    sp.wait_ge(ew_lo, (e - 1) * 6)
                    sp.dma_start(wst[:, par, 0:2 * EK * HID], w13[e]).then_inc(ew_in[par], 16)
                    sp.dma_start(wst[:, par, 2 * EK * HID:], w2[e]).then_inc(ew_in[par], 16)
                    sp.wait_ge(xs_ready, e - 1)
                    sp.dma_start(sB[:, par], score_rows[bass.ds(e, 1), :].to_broadcast([P, COLS])
                                 ).then_inc(sB_in[par], 16)
            sp.wait_ge(osp_ready, EK * NSP)
            sp.dma_start(out_spec, osp[:]).then_inc(out_done, 16)
            for i in range(TILES // 3):
                sp.wait_ge(out_ready, 3 * (i + 1))
                sp.dma_start(out_patch[:, 3 * i:3 * i + 3], OUT[:, 3 * i:3 * i + 3]).then_inc(out_done, 16)
            sp.wait_ge(out_done, 16 * (1 + TILES // 3))

        @block.gpsimd
        def _(pool):
            steps = Steps(pool, pool_step)
            nc.gpsimd.memset(H[:, 0, :], 0.0).then_inc(zeroed, 1)
            nc.gpsimd.memset(Y[:, 0, :], 0.0).then_inc(zeroed, 1)
            nc.gpsimd.memset(lo[:], 0).then_inc(zeroed, 1)
            nc.gpsimd.memset(half32[:], SO / 2).then_inc(zeroed, 1)
            nc.gpsimd.memset(zero16[:], 0.0).then_inc(zeroed, 1)
            pool.wait_ge(zeroed, 2)
            pool.dma_start(H[1:2, 0, :], cls_token).then_inc(slot0_in, 16)
            pool.dma_start(Y[1:2, 0, :], pos[0:1, :]).then_inc(slot0_in, 16)
            pool.dma_start(tokb[:], tok_b.to_broadcast([P, E])).then_inc(slot0_in, 16)
            pool.dma_start(cls_sb[:], cls_tok).then_inc(slot0_in, 16)
            for j in range(P // B):
                pool.dma_start(Y[B * j:B * (j + 1), 1:, :],
                               pos[1 + j:1 + j + (P // B) * (TILES - 1) + 1:P // B, :].unsqueeze(0)
                               .to_broadcast([B, TILES, E])).then_inc(slot0_in, 16)
            pool.dma_start(k16[:], k16_in).then_inc(const_in, 16)
            pool.dma_start(k32[:], k32_in).then_inc(const_in, 16)
            pool.dma_start(cand[:], cand_in).then_inc(const_in, 16)
            for i, v in enumerate((bqkv, alpha, aug)):
                n = 3 if i == 0 else 1
                a = 0 if i == 0 else 2 + i
                pool.dma_start(chan[:, a:a + n, :], v).then_inc(cls_in, 16)
            pool.wait_ge(slot0_in, 16 * 8)
            for s in range(1, SLOTS):
                nc.gpsimd.tensor_tensor(Y[:, s, :], Y[:, s, :], tokb[:], ALU.add).then_inc(posb_ready, 1)

            pool.wait_ge(qkvw_in, 16)
            nc.gpsimd.tensor_scalar(qwh[:], qw[:], SW, 0.0, ALU.mult, ALU.add).then_inc(qkvw_hi, 1)
            pool.wait_ge(wo_in, 32)
            nc.gpsimd.tensor_scalar(owh[:], ow[:], SW, 0.0, ALU.mult, ALU.add).then_inc(wo_hi, 1)

            def weights_hi(e, par):
                if not isinstance(e, int):
                    pool.wait_ge(ew_in[par], (e - par) * 16 + 32)
                    pool.sem_inc(pool_step, 1)
                else:
                    pool.wait_ge(ew_in[par], 32)
                nc.gpsimd.tensor_scalar(wh[:, par], wst[:, par], SW, 0.0, ALU.mult, ALU.add).then_inc(ew_hi, 1)

            def scaled_tokens(e, par):
                pool.wait_ge(sB_in[par], (e // 2 + 1) * 16 if isinstance(e, int) else (e - par) * 8 + 16)
                for k in range(EK):
                    ins = nc.gpsimd.tensor_tensor(X32[:, k], y2T[:, k], sB[:, par], ALU.mult)
                ins.then_inc(xs_ready, 1)

            weights_hi(0, 0)
            weights_hi(1, 1)
            pool.wait_ge(y2T_ready, NCH)
            scaled_tokens(0, 0)
            pool.wait_ge(xs_hi, NCH * EK)
            pool.wait_ge(xs_lo, NCH * EK)
            scaled_tokens(1, 1)
            with pool.Fori(1, NEXP // 2) as pair:
                for par in range(2):
                    e = pair * 2 + par
                    pool.wait_ge(xs_hi, e * (NCH * EK))
                    pool.wait_ge(xs_lo, e * (NCH * EK))
                    scaled_tokens(e, par)
                    pool.wait_ge(dn_mm, (e - 1) * NCH)
                    weights_hi(e, par)

        @block.scalar
        def _(act):
            steps = Steps(act, act_step)
            act.wait_ge(cls_in, 48)
            nc.scalar.activation(ez[:], chan[:, 3, :], ACT.Tanh, scale=0.5).then_inc(chan_e, 1)
            act.wait_ge(tokw_in, 16)
            nc.scalar.activation(twh[:], tw[:], ACT.Copy, scale=SW).then_inc(tokw_hi, 1)
            for c in range(NCH):
                act.wait_ge(px_in[c], 16)
                nc.scalar.activation(pxh[:, c], px[:, c], ACT.Copy, scale=SX).then_inc(px_hi, 1)
            act.wait_ge(zeroed, 5)

            for stage, c in ORDER:
                w, ns = width(c), len(slots_of(c))
                if stage == "yT":
                    for k in range(EK):
                        act.wait_ge(yT_mm, EK * c + k + 1)
                        if c:
                            act.wait_ge(v_mm, MK * c)
                        nc.scalar.activation(yTh[:, k, 0:w], bank[6 + k][:, 0:w], ACT.Copy, scale=SY
                                             ).then_inc(yT_hi, 1)
                elif stage == "qkv":
                    if c == 0:
                        act.wait_ge(chan_ready, 1)
                        act.wait_ge(tok_mm, TILES)
                        act.wait_ge(px_lo, NCH)
                        act.wait_ge(px_hi, NCH)
                    for m in range(MK):
                        n = MK * c + m
                        act.wait_ge(q_mm, n + 1)
                        if c and m == 0:
                            act.wait_ge(o_ready, c)
                        nc.scalar.activation(q[:, m, 0:w], bank[(3 * m) % 3][:, 0:w], ACT.Identity,
                                             bias=chan[:, 0, m:m + 1], scale=1.0 / (SY * SW)).then_inc(q_read, 1)
                        act.wait_ge(v_mm, n + 1)
                        nc.scalar.activation(vp[:, m, 0:w], bank[2][:, 0:w], ACT.Identity,
                                             bias=v_bias[:, m:m + 1], scale=v_scale[:, m:m + 1]).then_inc(v_read, 1)
                        act.wait_ge(q_read, n + 1)
                        nc.scalar.activation(th[:, m, 0:w], q[:, m, 0:w], ACT.Tanh,
                                             scale=chan[:, 4, m:m + 1]).then_inc(th_ready, 1)
                elif stage == "soft":
                    act.wait_ge(logit_sub, c + 1)
                    nc.scalar.activation(ex[:, 0:ns], dd[:, 0:ns], ACT.Exp,
                                         scale=HDIM ** -0.5 / (SY * SW)).then_inc(exp_ready, 1)
                elif stage == "state":
                    act.wait_ge(attn_T_mm, c + 1)
                    if c:
                        act.wait_ge(aB_mm, MK * c)
                    nc.scalar.activation(attn_T[:, 0:w], bank[5][0:2 * HEADS, :].bitcast(F16)[:, 0:w], ACT.Copy
                                         ).then_inc(attn_T_ready, 1)
                    act.wait_ge(o_ready, c + 1)
                    if c:
                        act.wait_ge(wo_mm, slots_of(c)[0])
                    nc.scalar.activation(oTh[:, :, 0:w], qk[:, :, 0:w], ACT.Identity, bias=half32[:]
                                         ).then_inc(o_hi, 1)
                elif stage == "y2T":
                    for k in range(EK):
                        act.wait_ge(y2T_mm, EK * c + k + 1)
                        ins = nc.scalar.activation(y2T[:, k, col0(c):col0(c) + w], bank[6 + k][:, 0:w], ACT.Copy)
                    ins.then_inc(y2T_ready, 1)
                    act.wait_ge(gate_sub, c + 1)
                    nc.scalar.activation(ex[:, 0:ns], dd[:, 0:ns], ACT.Exp).then_inc(gexp_ready, 1)

            act.wait_ge(rows_mm, 1)
            nc.scalar.activation(rows[0:TILES * NEXP, :], bank[0][0:TILES * NEXP, 0:P], ACT.Copy
                                 ).then_inc(rows_ready, 1)
            nc.scalar.activation(rows_sp[:], bank[1][0:NEXP, 0:NSP], ACT.Copy).then_inc(rows_ready, 1)

            def tokens_hi(par, piece):
                c, k = piece // EK, piece % EK
                a, w = col0(c), width(c)
                nc.scalar.activation(xh[:, par, k, a:a + w], X32[:, k, a:a + w], ACT.Copy, scale=SXS
                                     ).then_inc(xs_hi, 1)

            act.wait_ge(xs_ready, 1)
            for piece in range(NCH * EK):
                tokens_hi(0, piece)

            def unit(e, par, c):
                w, j = width(c), e * NCH + c
                for m in range(HK):
                    n = j * HK + m
                    act.wait_ge(g_mm, n + 1)
                    if not isinstance(e, int) or n >= 2:
                        act.wait_ge(t_ready, n - 1)
                    i = c * HK + m
                    nc.scalar.activation(sg[:, m % 2, 0:w], bank[5 + (2 * i) % 3][:, 0:w], ACT.Silu,
                                         scale=1.0 / (SXS * SW)).then_inc(silu_ready, 1)
                    if 1 <= i <= 6 and not (isinstance(e, int) and e == NEXP - 1):
                        if i == 1:
                            act.wait_ge(xs_ready, e + 2)
                            if not isinstance(e, int) or e:
                                act.wait_ge(u_mm, e * (NCH * HK))
                        tokens_hi(1 - par, i - 1)
                    act.wait_ge(t_ready, n + 1)
                    if not isinstance(e, int) or j >= 2:
                        act.wait_ge(dn_mm, j - 1)
                    nc.scalar.activation(Hh[:, (par + c) % 2, m, 0:w], Tt[:, m % 2, 0:w], ACT.Copy
                                         ).then_inc(h_hi, 1)

            units(unit, act.Fori)

        @block.vector
        def _(dve):
            V = nc.vector
            steps = Steps(dve, dve_step)

            def low_half(out, src, scale, hi):
                return V.scalar_tensor_tensor(out=out, in0=src, scalar=scale, in1=hi, op0=ALU.mult,
                                              op1=ALU.subtract)

            def norm_stats(src, ns, eps):
                for i in range(ns):
                    steps.did(V.bn_stats(stats[:, i, :], src[:, i, :]))
                steps.wait()
                for i in range(ns):
                    steps.did(V.bn_aggr(mv[:, i, :], stats[:, i, :]))
                steps.wait()
                v, r, a, b = ve[:, 0:ns], ri[:, 0:ns], na[:, 0:ns], nb_[:, 0:ns]
                steps.then(V.tensor_scalar(v, mv[:, 0:ns, 1], eps, None, ALU.add))
                steps.then(V.tensor_scalar(sh[:, 0:ns], v.bitcast(I32), 1, None, ALU.logical_shift_right))
                steps.then(V.tensor_scalar(r.bitcast(I32), sh[:, 0:ns], -1.0, MAGIC, ALU.mult, ALU.add))
                for _ in range(3):
                    steps.then(V.tensor_tensor(a, r, r, ALU.mult))
                    steps.then(V.scalar_tensor_tensor(out=b, in0=a, scalar=-0.5, in1=v, op0=ALU.mult,
                                                      op1=ALU.mult))
                    steps.then(V.scalar_tensor_tensor(out=r, in0=b, scalar=1.5, in1=r, op0=ALU.add,
                                                      op1=ALU.mult))

            def softmax_front(logits, ns):
                steps.then(V.tensor_reduce(mx[:, 0:ns], logits, AX, ALU.max))
                return V.tensor_tensor(dd[:, 0:ns], logits, mx[:, 0:ns].unsqueeze(2).to_broadcast([P, ns, HEADS]),
                                       ALU.subtract)

            def softmax_back(out, ns):
                steps.then(V.tensor_reduce(sm[:, 0:ns], ex[:, 0:ns], AX, ALU.add))
                steps.then(V.reciprocal(sm[:, 0:ns], sm[:, 0:ns]))
                return V.tensor_tensor(out, ex[:, 0:ns], sm[:, 0:ns].unsqueeze(2).to_broadcast([P, ns, HEADS]),
                                       ALU.mult)

            dve.wait_ge(tokw_hi, 1)
            low_half(twl[:], tw[:], SW, twh[:]).then_inc(tokw_lo, 1)
            dve.wait_ge(chan_e, 1)
            steps.then(V.tensor_scalar(decay[:], ez[:], 0.5, 0.5, ALU.mult, ALU.add))
            steps.then(V.tensor_scalar(ez[:], ez[:], -0.5, 0.5, ALU.mult, ALU.add))
            steps.did(V.tensor_scalar(v_scale[:], ez[:], 1.0 / (SY * SW * SA), None, ALU.mult))
            steps.did(V.scalar_tensor_tensor(out=v_bias[:], in0=ez[:], scalar=1.0 / SA, in1=chan[:, 2, :],
                                             op0=ALU.mult, op1=ALU.mult))
            steps.did(V.tensor_scalar(bk_s[:], chan[:, 1, :], SY * SW, None, ALU.mult))
            V.tensor_scalar(chan[:, 4, :], chan[:, 4, :], 0.5, None, ALU.mult).then_inc(chan_ready, 1)
            for c in range(NCH):
                dve.wait_ge(px_hi, c + 1)
                low_half(pxl[:, c], px[:, c], SX, pxh[:, c]).then_inc(px_lo, 1)

            for stage, c in ORDER:
                w, sl = width(c), slots_of(c)
                ns, s0 = len(sl), sl[0]
                if stage == "tok":
                    if c == 0:
                        dve.wait_ge(slot0_in, 16 * 8)
                        steps.did(V.tensor_tensor(H[:, 0, :], H[:, 0, :], Y[:, 0, :], ALU.add))
                        dve.wait_ge(vec_in, 16 * 5)
                    for s in sl:
                        if s:
                            n = s - 1
                            dve.wait_ge(posb_ready, s)
                            dve.wait_ge(tok_mm, n + 1)
                            V.scalar_tensor_tensor(out=H[:, s, :], in0=bank[n % 6][:, 0:E],
                                                   scalar=1.0 / (SX * SW), in1=Y[:, s, :], op0=ALU.mult,
                                                   op1=ALU.add).then_inc(tok_read, 1)
                    dve.wait_ge(tok_read, sl[-1])
                    steps.wait()
                    norm_stats(H[:, s0:s0 + ns], ns, 1e-5)
                    for i, s in enumerate(sl):
                        steps.did(V.scalar_tensor_tensor(out=H[:, s, :], in0=H[:, s, :], scalar=mv[:, i, 0:1],
                                                         in1=gam[:], op0=ALU.subtract, op1=ALU.mult))
                    steps.wait()
                    for i, s in enumerate(sl):
                        steps.did(V.scalar_tensor_tensor(out=H[:, s, :], in0=H[:, s, :], scalar=ri[:, i:i + 1],
                                                         in1=bet[:], op0=ALU.mult, op1=ALU.add))
                    steps.wait()
                    if c == 0:
                        steps.then(V.tensor_copy(H[0:1, 0, :], cls_sb[0:1, :]))
                    norm_stats(H[:, s0:s0 + ns], ns, 1e-5)
                    for i, s in enumerate(sl):
                        V.tensor_scalar(Y[:, s, :], H[:, s, :], mv[:, i, 0:1], ri[:, i:i + 1], ALU.subtract,
                                        ALU.mult).then_inc(y_ready, 1)
                    for s in sl:
                        steps.did(V.tensor_tensor(H[:, s, :], H[:, s, :], lnb[:], ALU.add))
                    if c == 0:
                        dve.wait_ge(qkvw_hi, 1)
                        low_half(qwl[:], qw[:], SW, qwh[:]).then_inc(qkvw_lo, 1)
                    if c == 1:
                        dve.wait_ge(wo_hi, 1)
                        low_half(owl[:], ow[:], SW, owh[:]).then_inc(wo_lo, 1)
                elif stage == "yT":
                    for k in range(EK):
                        dve.wait_ge(yT_hi, EK * c + k + 1)
                        low_half(yTl[:, k, 0:w], bank[6 + k][:, 0:w], SY, yTh[:, k, 0:w]).then_inc(yT_lo, 1)
                elif stage == "qkv":
                    if c == 0:
                        steps.then(V.tensor_copy(DECs, decay[:].unsqueeze(2).unsqueeze(3)
                                                 .to_broadcast([P, MK, B, SEG])))
                        steps.did(V.memset(DECs[:, :, :, 0], 0.0))
                    for m in range(MK):
                        n = MK * c + m
                        dve.wait_ge(k_mm, n + 1)
                        dve.wait_ge(q_read, n + 1)
                        if c and m == 0:
                            dve.wait_ge(o_lo, c)
                            dve.wait_ge(logit_mm, c)
                        V.scalar_tensor_tensor(out=qk[:, m, 0:w], in0=bank[1][:, 0:w], scalar=bk_s[:, m:m + 1],
                                               in1=q[:, m, 0:w], op0=ALU.add, op1=ALU.mult).then_inc(qk_ready, 1)
                elif stage == "soft":
                    dve.wait_ge(logit_mm, c + 1)
                    lg = bank[5][:, 0:ns * HEADS].rearrange("p (s h) -> p s h", h=HEADS)
                    softmax_front(lg, ns).then_inc(logit_sub, 1)
                    dve.wait_ge(exp_ready, c + 1)
                    steps.then(softmax_back(attn[:, 0:ns], ns))
                    steps.then(V.tensor_scalar(attn_hl[:, 0:ns, 0], attn[:, 0:ns], SA, None, ALU.mult))
                    low_half(attn_hl[:, 0:ns, 1], attn[:, 0:ns], SA, attn_hl[:, 0:ns, 0]).then_inc(attn_ready, 1)
                elif stage == "state":
                    off = NSP if c == 0 else 0
                    if c:
                        steps.then(V.tensor_copy(Us[:, :, :, 0], STs[:, :, :, SEG - 1]))
                    dve.wait_ge(v_read, MK * (c + 1))
                    for m in range(MK):
                        dve.wait_ge(aB_mm, MK * c + m + 1)
                        aB = bank[3 + m % 2]
                        if c == 0:
                            steps.did(V.tensor_tensor(us2[:, m, :], aB[:, 0:NSP], vp[:, m, 0:NSP], ALU.mult))
                        V.tensor_tensor(Us[:, m, :, 1:].rearrange("p b t -> p t b"),
                                        aB[:, off:off + CW].rearrange("p (t b) -> p t b", b=B),
                                        vp[:, m, off:off + CW].rearrange("p (t b) -> p t b", b=B),
                                        ALU.mult).then_inc(u_ready, 1)
                    if c == 0:
                        steps.wait()
                        steps.did(V.tensor_copy(sp_state[:, :, 0], us2[:, :, 0]))
                        steps.then(V.tensor_tensor(sp_tmp[:], us2[:, :, 0], decay[:], ALU.mult))
                        steps.then(V.tensor_tensor(sp_state[:, :, 1], us2[:, :, 1], sp_tmp[:], ALU.add))
                        steps.then(V.tensor_copy(Us[:, :, :, 0], sp_state[:, :, 1:2].to_broadcast([P, MK, B])))
                    dve.wait_ge(u_ready, MK * (c + 1))
                    steps.then(V.tensor_tensor_scan(STt, DEC, U, 0.0, ALU.mult, ALU.add))
                    for m in range(MK):
                        steps.did(V.scalar_tensor_tensor(
                            out=qk[:, m, off:off + CW].rearrange("p (t b) -> p t b", b=B),
                            in0=q[:, m, off:off + CW].rearrange("p (t b) -> p t b", b=B), scalar=SO,
                            in1=STs[:, m, :, 1:].rearrange("p b t -> p t b"), op0=ALU.mult, op1=ALU.mult))
                    if c == 0:
                        steps.did(V.scalar_tensor_tensor(out=qk[:, :, 0:NSP], in0=q[:, :, 0:NSP], scalar=SO,
                                                         in1=sp_state[:], op0=ALU.mult, op1=ALU.mult))
                    steps.wait()
                    dve.wait_ge(th_ready, MK * (c + 1))
                    V.scalar_tensor_tensor(out=qk[:, :, 0:w], in0=th[:, :, 0:w], scalar=SO / 2,
                                           in1=qk[:, :, 0:w], op0=ALU.mult, op1=ALU.add).then_inc(o_ready, 1)
                    dve.wait_ge(o_hi, c + 1)
                    V.scalar_tensor_tensor(out=oTl[:, :, 0:w], in0=qk[:, :, 0:w], scalar=SO / 2,
                                           in1=oTh[:, :, 0:w], op0=ALU.add, op1=ALU.subtract).then_inc(o_lo, 1)
                elif stage == "out":
                    for i, s in enumerate(sl):
                        dve.wait_ge(wo_mm, s + 1)
                        V.scalar_tensor_tensor(out=Y[:, s, :], in0=bank[3 + s % 2][:, 0:E],
                                               scalar=1.0 / (SO * SW), in1=bob[:], op0=ALU.mult,
                                               op1=ALU.add).then_inc(wo_read, 1)
                    dve.wait_ge(wo_read, sl[-1] + 1)
                    norm_stats(Y[:, s0:s0 + ns], ns, 1e-6)
                    for i, s in enumerate(sl):
                        steps.did(V.scalar_tensor_tensor(out=Y[:, s, :], in0=Y[:, s, :], scalar=mv[:, i, 0:1],
                                                         in1=lns[:], op0=ALU.subtract, op1=ALU.mult))
                    steps.wait()
                    for i, s in enumerate(sl):
                        steps.did(V.scalar_tensor_tensor(out=H[:, s, :], in0=Y[:, s, :], scalar=ri[:, i:i + 1],
                                                         in1=H[:, s, :], op0=ALU.mult, op1=ALU.add))
                    steps.wait()
                    norm_stats(H[:, s0:s0 + ns], ns, 1e-5)
                    for i, s in enumerate(sl):
                        V.tensor_scalar(Y[:, s, :], H[:, s, :], mv[:, i, 0:1], ri[:, i:i + 1], ALU.subtract,
                                        ALU.mult).then_inc(y2_ready, 1)
                elif stage == "y2T":
                    dve.wait_ge(gate_mm, c + 1)
                    lg = bank[5][:, 0:ns * NEXP].rearrange("p (s h) -> p s h", h=NEXP)
                    softmax_front(lg, ns).then_inc(gate_sub, 1)
                    dve.wait_ge(gexp_ready, c + 1)
                    steps.then(softmax_back(SC[:, s0:s0 + ns], ns))

            for e in (0,):
                dve.wait_ge(ew_hi, 1)
                for i in range(6):
                    a = i * HID
                    low_half(wl[:, 0, a:a + HID], wst[:, 0, a:a + HID], SW, wh[:, 0, a:a + HID]).then_inc(ew_lo, 1)
            dve.wait_ge(const_in, 48)
            dve.wait_ge(zeroed, 5)
            first_round = steps.n
            with dve.Fori(0, ROUNDS) as r:
                def did(k):
                    dve.wait_ge(dve_step, r * 6 + (first_round + k))

                V.tensor_tensor(mid[:], lo[:].unsqueeze(1).to_broadcast([P, NCAND, NEXP]),
                                cand[:].unsqueeze(2).to_broadcast([P, NCAND, NEXP]),
                                ALU.bitwise_or).then_inc(dve_step, 1)
                did(1)
                for i in range(NCAND):
                    ins = V.tensor_tensor(ge[:, :, i, :], SC[:],
                                          mid[:, i].bitcast(F32).unsqueeze(1).to_broadcast([P, SLOTS, NEXP]), ALU.is_ge)
                ins.then_inc(ge_ready, 1)
                V.tensor_scalar(cand[:], cand[:], 2, None, ALU.logical_shift_right).then_inc(dve_step, 1)
                dve.wait_ge(count_mm, r + 1)
                V.tensor_scalar(fl[:], bank[0][:, 0:NCAND * NEXP].rearrange("p (c e) -> p c e", e=NEXP),
                                float(CAP), bit, ALU.is_ge, ALU.mult).then_inc(dve_step, 1)
                did(3)
                with nc.allow_low_precision(reason="at most three equal powers of two: exact in int32"):
                    V.tensor_reduce(inc[:], fl[:].rearrange("p c e -> p e c"), AX, ALU.add).then_inc(dve_step, 1)
                V.tensor_scalar(bit, bit, 0.25, None, ALU.mult).then_inc(dve_step, 1)
                did(5)
                V.tensor_tensor(lo[:], lo[:], inc[:], ALU.bitwise_or).then_inc(dve_step, 1)
                did(6)
            steps.n += ROUNDS * 6

            cut = lo[:].bitcast(F32).unsqueeze(1).to_broadcast([P, SLOTS, NEXP])
            steps.did(V.tensor_tensor(gt[:], SC[:], cut, ALU.is_gt))
            steps.then(V.tensor_tensor(eq[:], SC[:], cut, ALU.is_equal))
            with nc.allow_low_precision(reason="a count up to nine: exact in float16"):
                steps.then(V.tensor_reduce(esum[:], eq[:, 1:].rearrange("p s e -> p e s"), AX, ALU.add))
            tri = k16[:, K_TRI:K_TRI + B]
            coef = k16[:, K_COEF:K_COEF + 2 * B].rearrange("p (b t) -> p b t", t=2)
            for t in range(2):
                steps.did(V.tensor_tensor(tri_e[:, :, t], tri.unsqueeze(2).to_broadcast([P, B, NEXP]),
                                          esum[:].unsqueeze(1).to_broadcast([P, B, NEXP]), ALU.mult))
                ins = V.tensor_tensor(sp_e[:, :, t], coef[:, :, t:t + 1].to_broadcast([P, B, NEXP]),
                                      eq[:, 0:1].to_broadcast([P, B, NEXP]), ALU.mult)
            ins.then_inc(tie_ready, 1)
            dve.wait_ge(rank_mm, 1)
            steps.then(V.tensor_scalar(room[:], bank[2][:, 0:NEXP], -1.0, float(CAP), ALU.mult, ALU.add))
            steps.then(V.tensor_tensor(allow[:], eq[:], room[:].unsqueeze(1).to_broadcast([P, SLOTS, NEXP]),
                                       ALU.mult))
            steps.then(V.scalar_tensor_tensor(out=allow[:], in0=gt[:], scalar=TIE_BIG, in1=allow[:],
                                              op0=ALU.mult, op1=ALU.add))
            for t in range(2):
                ins = V.tensor_tensor(allow_sp[:, t], allow[:, 0],
                                      k16[:, K_SPSEL + t:K_SPSEL + t + 1].to_broadcast([P, NEXP]), ALU.mult)
            ins.then_inc(tie_ready, 1)
            steps.then(V.tensor_tensor(keep[:], bank[3][:, 0:TILES * NEXP].rearrange("p (s e) -> p s e", e=NEXP),
                                       allow[:, 1:], ALU.is_lt))
            steps.did(V.tensor_copy(SM[:, 0], SC[:, 0]))
            V.tensor_tensor(SM[:, 1:], SC[:, 1:], keep[:], ALU.mult).then_inc(sm_ready, 1)
            dve.wait_ge(rank_mm, 2)
            steps.then(V.tensor_copy(asp[:], bank[5][:, 0:2 * NEXP].rearrange("p (t e) -> p t e", e=NEXP)))
            for t in range(2):
                steps.did(V.tensor_tensor(msp[:, :, t], bank[4][:, :].rearrange("p (b t e) -> p b t e", b=B, t=2)[:, :, t],
                                          asp[:, t:t + 1].to_broadcast([P, B, NEXP]), ALU.is_lt))
            dve.wait_ge(rows_mm, 1)
            V.tensor_copy(h2sp[:], bank[6][:, 0:EK * NSP].rearrange("p (k t) -> p k t", t=NSP)
                          ).then_inc(cut_ready, 1)

            def tokens_lo(par, piece):
                c, k = piece // EK, piece % EK
                a, w = col0(c), width(c)
                low_half(xl[:, par, k, a:a + w], X32[:, k, a:a + w], SXS, xh[:, par, k, a:a + w]
                         ).then_inc(xs_lo, 1)

            for piece in range(NCH * EK):
                dve.wait_ge(xs_hi, piece + 1)
                tokens_lo(0, piece)

            def unit(e, par, c):
                static = isinstance(e, int)
                w, j = width(c), e * NCH + c
                for m in range(HK):
                    n, i = j * HK + m, c * HK + m
                    dve.wait_ge(u_mm, n + 1)
                    dve.wait_ge(silu_ready, n + 1)
                    if not static or n >= 2:
                        dve.wait_ge(h_lo, n - 1)
                    V.scalar_tensor_tensor(out=Tt[:, m % 2, 0:w], in0=bank[5 + (2 * i + 1) % 3][:, 0:w],
                                           scalar=ST_ / (SXS * SW), in1=sg[:, m % 2, 0:w], op0=ALU.mult,
                                           op1=ALU.mult).then_inc(t_ready, 1)
                    if not (static and e == NEXP - 1):
                        if 1 <= i <= 6:
                            dve.wait_ge(xs_hi, (e + 1) * (NCH * EK) + i)
                            tokens_lo(1 - par, i - 1)
                        if 6 <= i:
                            if i == 6:
                                dve.wait_ge(ew_hi, e + 2)
                            a = (i - 6) * HID
                            low_half(wl[:, 1 - par, a:a + HID], wst[:, 1 - par, a:a + HID], SW,
                                     wh[:, 1 - par, a:a + HID]).then_inc(ew_lo, 1)
                    dve.wait_ge(h_hi, n + 1)
                    V.tensor_tensor(Hl[:, (par + c) % 2, m, 0:w], Tt[:, m % 2, 0:w],
                                    Hh[:, (par + c) % 2, m, 0:w], ALU.subtract).then_inc(h_lo, 1)

            units(unit, dve.Fori)

            dve.wait_ge(dn_mm, NEXP * NCH)
            bias2 = 1.0 / (ST_ * SW)
            for i in range(TILES):
                V.scalar_tensor_tensor(out=OUT[:, i, :], in0=bank[i // 2][:, (i % 2) * E:][:, 0:E], scalar=bias2,
                                       in1=H[:, 1 + i, :], op0=ALU.mult, op1=ALU.add).then_inc(out_ready, 1)
            steps.then(V.tensor_scalar(ysp[:], bank[4][:, E:E + EK * NEXP * NSP].rearrange(
                "p (k e t) -> p k e t", k=EK, e=NEXP), bias2, None, ALU.mult))
            for k in range(EK):
                for t in range(NSP):
                    steps.then(V.tensor_tensor(prod[:], msp[:, :, t],
                                               ysp[:, k, :, t].unsqueeze(1).to_broadcast([P, B, NEXP]), ALU.mult))
                    steps.then(V.tensor_reduce(osp[:, k, t], prod[:], AX, ALU.add))
                    V.tensor_scalar(osp[:, k, t], osp[:, k, t], h2sp[:, k, t:t + 1], None, ALU.add
                                    ).then_inc(osp_ready, 1)

        @block.tensor
        def _(pe):
            mm = nc.tensor.matmul

            def cut_products(out, pairs, start=True, stop=True):
                for i, ((ah, al), (bh, bl)) in enumerate(pairs):
                    mm(out, ah, bh, start=start and i == 0, stop=False, skip_group_check=not start)
                    mm(out, ah, bl, start=False, stop=False, skip_group_check=not start)
                    ins = mm(out, al, bh, start=False, stop=stop and i == len(pairs) - 1,
                             skip_group_check=not start)
                return ins

            pe.wait_ge(tokw_lo, 1)
            pe.wait_ge(const_in, 48)
            for stage, c in ORDER:
                w, sl = width(c), slots_of(c)
                ns, s0 = len(sl), sl[0]
                if stage == "tok":
                    pe.wait_ge(px_lo, c + 1)
                    for s in sl:
                        if s:
                            n = s - 1
                            if n >= 6:
                                pe.wait_ge(tok_read, n - 5)
                            a = (n - TPC * c) * P
                            cut_products(bank[n % 6][:, 0:E],
                                         [((pxh[:, c, k, a:a + P], pxl[:, c, k, a:a + P]),
                                           (twh[:, k, :], twl[:, k, :])) for k in range(DK)]).then_inc(tok_mm, 1)
                elif stage == "yT":
                    for k in range(EK):
                        if c:
                            pe.wait_ge(yT_lo, EK * (c - 1) + k + 1)
                        for s in sl:
                            pe.wait_ge(y_ready, s + 1)
                            a, n = slot_cols(s, c)
                            ins = nc.tensor.transpose(bank[6 + k][:, a:a + n], Y[0:n, s, k * P:(k + 1) * P],
                                                      ident[0:n, 0:n])
                        ins.then_inc(yT_mm, 1)
                elif stage == "qkv":
                    if c == 0:
                        pe.wait_ge(qkvw_lo, 1)
                    pe.wait_ge(yT_lo, EK * (c + 1))
                    for m in range(MK):
                        n = MK * c + m
                        for which, done, free in ((0, q_mm, q_read), (1, k_mm, qk_ready), (2, v_mm, v_read)):
                            if n:
                                pe.wait_ge(free, n)
                            cut_products(bank[which][:, 0:w],
                                         [((qwh[:, which, k, m * P:(m + 1) * P], qwl[:, which, k, m * P:(m + 1) * P]),
                                           (yTh[:, k, 0:w], yTl[:, k, 0:w])) for k in range(EK)]).then_inc(done, 1)
                elif stage == "soft":
                    pe.wait_ge(qk_ready, MK * (c + 1))
                    if c == 0:
                        pe.wait_ge(tok_read, TILES)
                    else:
                        pe.wait_ge(attn_T_ready, c)
                    if c == 2:
                        pe.wait_ge(gate_sub, 1)
                    for i, s in enumerate(sl):
                        a, _ = slot_cols(s, c)
                        for m in range(MK):
                            ins = mm(bank[5][:, i * HEADS:(i + 1) * HEADS], qk[:, m, a:a + P],
                                     blk[:, m, :], start=m == 0, stop=m == MK - 1)
                    ins.then_inc(logit_mm, 1)
                elif stage == "state":
                    pe.wait_ge(attn_ready, c + 1)
                    for i, s in enumerate(sl):
                        a, cnt = slot_cols(s, c)
                        ins = nc.tensor.transpose(
                            bank[5][0:2 * HEADS, :].bitcast(F16)[:, a:a + cnt],
                            attn_hl[0:cnt, i].rearrange("p t h -> p (t h)"), k16[0:cnt, K_ID16:K_ID16 + cnt])
                    ins.then_inc(attn_T_mm, 1)
                    pe.wait_ge(attn_T_ready, c + 1)
                    for m in range(MK):
                        n = MK * c + m
                        if n >= 2:
                            pe.wait_ge(u_ready, n - 1)
                        if c and m == 0:
                            pe.wait_ge(wo_read, s0)
                        mm(bank[3 + m % 2][:, 0:w], k16[0:2 * HEADS, K_SPREAD + m * P:K_SPREAD + (m + 1) * P],
                           attn_T[:, 0:w], start=True, stop=True).then_inc(aB_mm, 1)
                elif stage == "out":
                    if c == 0:
                        pe.wait_ge(wo_lo, 1)
                    pe.wait_ge(o_lo, c + 1)
                    pe.wait_ge(u_ready, MK * (c + 1))
                    for s in sl:
                        if s >= 2:
                            pe.wait_ge(wo_read, s - 1)
                        a, _ = slot_cols(s, c)
                        cut_products(bank[3 + s % 2][:, 0:E],
                                     [((oTh[:, m, a:a + P], oTl[:, m, a:a + P]), (owh[:, m, :], owl[:, m, :]))
                                      for m in range(MK)]).then_inc(wo_mm, 1)
                elif stage == "y2T":
                    for k in range(EK):
                        if c:
                            pe.wait_ge(y2T_ready, c)
                        if c == 0:
                            pe.wait_ge(yT_lo, EK * NCH)
                        for s in sl:
                            pe.wait_ge(y2_ready, s + 1)
                            a, n = slot_cols(s, c)
                            ins = nc.tensor.transpose(bank[6 + k][:, a:a + n], Y[0:n, s, k * P:(k + 1) * P],
                                                      ident[0:n, 0:n])
                        ins.then_inc(y2T_mm, 1)
                    pe.wait_ge(y2T_ready, c + 1)
                    pe.wait_ge(attn_T_ready, 2 if c == 0 else 3)
                    if c:
                        pe.wait_ge(gate_sub, c)
                    for i, s in enumerate(sl):
                        a, _ = slot_cols(s, c)
                        for k in range(EK):
                            ins = mm(bank[5][:, i * NEXP:(i + 1) * NEXP], y2T[:, k, col0(c) + a:col0(c) + a + P],
                                     wg_sb[:, k, :], start=k == 0, stop=k == EK - 1)
                    ins.then_inc(gate_mm, 1)

            def const(at_):
                return k16[:, at_:at_ + P]

            with pe.Fori(0, ROUNDS) as r:
                pe.wait_ge(ge_ready, r + 1)
                for s in range(SLOTS):
                    ins = mm(bank[0][:, 0:NCAND * NEXP], const(K_ONES) if s else const(K_W32),
                             ge[:, s].rearrange("p c e -> p (c e)"), start=s == 0, stop=s == SLOTS - 1)
                ins.then_inc(count_mm, 1)

            pe.wait_ge(tie_ready, 1)
            for s in range(SLOTS):
                mm(bank[2][:, 0:NEXP], const(K_ONES) if s else const(K_W32), gt[:, s], start=s == 0,
                   stop=s == SLOTS - 1)
            rank = bank[3][:, 0:TILES * NEXP]
            mm(rank, const(K_EARLIER), esum[:].unsqueeze(1).to_broadcast([P, TILES, NEXP]), start=True, stop=False)
            for s in range(1, TILES):
                mm(bank[3][:, s * NEXP:TILES * NEXP], const(K_SAME),
                   eq[:, s:s + 1].to_broadcast([P, TILES - s, NEXP]), start=False, stop=False)
            mm(rank, const(K_LOWER), eq[:, 1:].rearrange("p s e -> p (s e)"), start=False, stop=False)
            mm(rank, const(K_SPEC), eq[:, 0:1].to_broadcast([P, TILES, NEXP]), start=False, stop=True)
            mm(bank[4][:, :], const(K_ONES), tri_e[:].rearrange("p b t e -> p (b t e)"), start=True, stop=False)
            mm(bank[4][:, :], const(K_ONES), sp_e[:].rearrange("p b t e -> p (b t e)"), start=False,
               stop=True).then_inc(rank_mm, 1)
            pe.wait_ge(tie_ready, 2)
            mm(bank[5][:, 0:2 * NEXP], const(K_ONES), allow_sp[:].rearrange("p t e -> p (t e)"),
               start=True, stop=True).then_inc(rank_mm, 1)
            pe.wait_ge(sm_ready, 1)
            nc.tensor.transpose(bank[0][0:TILES * NEXP, 0:P], SM[:, 1:].rearrange("p s e -> p (s e)"), ident)
            nc.tensor.transpose(bank[1][0:NEXP, 0:NSP], SM[0:NSP, 0], ident[0:NSP, 0:NSP])
            for k in range(EK):
                ins = nc.tensor.transpose(bank[6][:, k * NSP:(k + 1) * NSP],
                                          H[0:NSP, 0, k * P:(k + 1) * P], ident[0:NSP, 0:NSP])
            ins.then_inc(rows_mm, 1)

            pe.wait_ge(cut_ready, 1)
            pe.wait_ge(rows_ready, 2)
            for b_ in range(5):
                mm(bank[b_][:, :], zero16[:], k16[:, 0:BANK], start=True, stop=False, skip_group_check=True)

            def down(e, par, c):
                static = isinstance(e, int)
                j = e * NCH + c
                pe.wait_ge(h_lo, (j + 1) * HK)
                pe.wait_ge(h_hi, (j + 1) * HK)
                if c == 0:
                    pe.wait_ge(ew_lo, (e + 1) * 6)
                jb = (par + c) % 2
                off = NSP if c == 0 else 0
                for i in range(TPC):
                    tile = TPC * c + i
                    a = off + i * P
                    ins = cut_products(bank[tile // 2][:, (tile % 2) * E:][:, 0:E],
                                       [((Hh[:, jb, m, a:a + P], Hl[:, jb, m, a:a + P]),
                                         (w2_of(wh, par, m), w2_of(wl, par, m))) for m in range(HK)], start=False,
                                       stop=False)
                if c == 0:
                    for k in range(EK):
                        if static:
                            o = E + (k * NEXP + e) * NSP
                            dst = bank[4][:, o:o + NSP]
                        else:
                            dst = bank[4][:, bass.ds(e * NSP + (E + k * NEXP * NSP), NSP)]
                        ins = cut_products(dst, [((w2_of(wh, par, m)[:, k * P:(k + 1) * P],
                                                   w2_of(wl, par, m)[:, k * P:(k + 1) * P]),
                                                  (Hh[:, jb, m, 0:NSP], Hl[:, jb, m, 0:NSP]))
                                                 for m in range(HK)], start=False, stop=False)
                ins.then_inc(dn_mm, 1)

            before = [None]

            def unit(e, par, c):
                static = isinstance(e, int)
                w, j, a = width(c), e * NCH + c, col0(c)
                if c == 0:
                    pe.wait_ge(xs_lo, (e + 1) * (NCH * EK))
                    pe.wait_ge(ew_lo, e * 6 + 4)
                for m in range(HK):
                    n, i = j * HK + m, c * HK + m
                    for which, done in ((0, g_mm), (1, u_mm)):
                        if which == 0 and (not static or n >= 2):
                            pe.wait_ge(t_ready, n - 1)
                        if which == 1 and (not static or n >= 1):
                            pe.wait_ge(silu_ready, n)
                        cut_products(bank[5 + (2 * i + which) % 3][:, 0:w],
                                     [((w13_of(wh, par, which, k, m), w13_of(wl, par, which, k, m)),
                                       (xh[:, par, k, a:a + w], xl[:, par, k, a:a + w])) for k in range(EK)]
                                     ).then_inc(done, 1)
                if not (static and e == 0 and c == 0):
                    if c:
                        down(e, par, c - 1)
                    else:
                        down(e - 1, 1 - par, NCH - 1)

            units(unit, pe.Fori)
            down(NEXP - 1, (NEXP - 1) % 2, NCH - 1)


def shape_constants():
    import numpy as np
    p = np.arange(P)
    j, b = p // B, p % B
    k16 = np.zeros((P, K16), np.float16)
    k16[:, K_ONES:K_ONES + P] = 1
    k16[0:2, K_W32:K_W32 + P] = B
    k16[:, K_EARLIER:K_EARLIER + P] = b[:, None] < b[None, :]
    same = b[:, None] == b[None, :]
    k16[:, K_SAME:K_SAME + P] = same
    k16[:, K_LOWER:K_LOWER + P] = same & (j[:, None] < j[None, :])
    k16[0:2, K_SPEC:K_SPEC + P] = b[None, :] + 1
    k16[:, K_TRI:K_TRI + B] = b[:, None] < np.arange(B)[None, :]
    coef = np.zeros((P, B, 2))
    coef[0] = np.arange(B)[:, None] + np.arange(2)[None, :]
    coef[1] = np.arange(B)[:, None]
    k16[:, K_COEF:K_COEF + 2 * B] = coef.reshape(P, -1)
    k16[:, K_ID16:K_ID16 + P] = np.eye(P)
    spread = np.arange(INNER)[None, :] // HDIM == (np.arange(2 * HEADS) % HEADS)[:, None]
    k16[0:2 * HEADS, K_SPREAD:] = spread
    k16[0, K_SPSEL] = k16[1, K_SPSEL + 1] = 1
    k32 = np.zeros((P, K32), np.float32)
    k32[:, K_IDENT:K_IDENT + P] = np.eye(P)
    for m in range(MK):
        for h in range(HEADS):
            k32[:, K_BLK + m * HEADS + h] = (P * m + p) // HDIM == h
    k32[:, K_BIT] = 2.0 ** 28
    cand = np.tile((np.arange(NCAND, dtype=np.int32) + 1) << 28, (P, 1)).astype(np.int32)
    return k16, k32, cand


def kernel(x, cls_tok, L0_tok_W, L0_tok_b, L0_tok_cls_token, L0_tok_pos_embedding, L0_tok_gamma, L0_tok_beta,
           L0_attn_Wq, L0_attn_bq, L0_attn_Wk, L0_attn_bk, L0_attn_Wv, L0_attn_bv, L0_attn_Wo, L0_attn_bo,
           L0_attn_alpha, L0_attn_aug_param, L0_attn_ln_scale, L0_attn_ln_bias, L0_ffn_wg, L0_ffn_w1, L0_ffn_w3,
           L0_ffn_w2):
    import numpy as np
    import concourse.bacc as bacc
    from concourse.bass_utils import run_bass_kernel_spmd

    def rows(w, k):
        w = np.asarray(w)
        return w.reshape(k, P, -1).transpose(1, 0, 2)

    def channels(*vs):
        return np.stack([np.asarray(v).reshape(MK, P).T for v in vs], 1)

    g = SIDE // PATCH
    px = np.asarray(x).reshape(B, C, g, PATCH, g, PATCH).transpose(1, 3, 5, 2, 4, 0).reshape(D, T)
    k16, k32, cand = shape_constants()
    w1 = np.stack([rows(w, EK) for w in np.asarray(L0_ffn_w1)])
    w3 = np.stack([rows(w, EK) for w in np.asarray(L0_ffn_w3)])
    w2 = np.stack([rows(w, HK) for w in np.asarray(L0_ffn_w2)])
    ins = dict(
        xT=px.reshape(DK, P, NCH, CW).transpose(1, 2, 0, 3),
        cls_tok=np.asarray(cls_tok).reshape(1, E), tok_w=rows(L0_tok_W, DK), tok_b=np.asarray(L0_tok_b).reshape(1, E),
        cls_token=np.asarray(L0_tok_cls_token).reshape(1, E), pos=np.asarray(L0_tok_pos_embedding)[0],
        gamma=np.asarray(L0_tok_gamma).reshape(1, E), beta=np.asarray(L0_tok_beta).reshape(1, E),
        wqkv=np.stack([rows(w, EK) for w in (L0_attn_Wq, L0_attn_Wk, L0_attn_Wv)], 1),
        bqkv=channels(L0_attn_bq, L0_attn_bk, L0_attn_bv), wo=rows(L0_attn_Wo, MK),
        bo=np.asarray(L0_attn_bo).reshape(1, E), alpha=channels(L0_attn_alpha), aug=channels(L0_attn_aug_param),
        ln_scale=np.asarray(L0_attn_ln_scale).reshape(1, E), ln_bias=np.asarray(L0_attn_ln_bias).reshape(1, E),
        wg=rows(L0_ffn_wg, EK), w13=np.stack([w1, w3], 2).reshape(NEXP, P, 2 * EK * HID),
        w2=w2.reshape(NEXP, P, HK * E), k16_in=k16, k32_in=k32, cand_in=cand)
    nc = bacc.Bacc("TRN2", target_bir_lowering=False, num_devices=1)
    arrays, args = {}, {}
    for name, a in ins.items():
        a = np.ascontiguousarray(a)
        arrays[name] = a
        args[name] = nc.dram_tensor(name, a.shape, mybir.dt.from_np(a.dtype), kind="ExternalInput").ap()
    args["out_patch"] = nc.dram_tensor("out_patch", (P, TILES, E), F32, kind="ExternalOutput").ap()
    args["out_spec"] = nc.dram_tensor("out_spec", (P, EK, NSP, B), F32, kind="ExternalOutput").ap()
    vit_tower(nc, **args)
    r = run_bass_kernel_spmd(nc, [arrays], core_ids=[0]).results[0]
    out = np.empty((B, S, E), np.float32)
    out[:, NSP:] = np.asarray(r["out_patch"]).transpose(1, 0, 2).reshape(NPATCH, B, E).transpose(1, 0, 2)
    out[:, :NSP] = np.asarray(r["out_spec"]).transpose(3, 2, 1, 0).reshape(B, NSP, E)
    return out
```

```python
from contextlib import ExitStack

import concourse.bass as bass
from concourse import mybir

F32 = mybir.dt.float32
F16 = mybir.dt.float16
I32 = mybir.dt.int32
ALU = mybir.AluOpType
ACT = mybir.ActivationFunctionType
AX = mybir.AxisListType.X

P = 128
B = 32
C, SIDE, PATCH = 3, 96, 16
NPATCH = (SIDE // PATCH) ** 2
T = B * NPATCH
NSP = 2
S = NPATCH + NSP
E = 256
EK = E // P
D = C * PATCH * PATCH
DK = D // P
HEADS, HDIM = 8, 64
INNER = HEADS * HDIM
MK = INNER // P
NEXP = 8
HID = 512
HK = HID // P
CAP = 1024

TILES = T // P
SLOTS = TILES + 1
NCH = 3
TPC = TILES // NCH
CW = TPC * P
TC = NPATCH // NCH
COLS = NSP + T
SEG = TC + 1
BANK = 512

SX, SW, SY, SO, SXS, ST_ = 64.0, 256.0, 256.0, 64.0, 1024.0, 16.0
SA = 4096.0
TIE_BIG = 2048.0
ROUNDS = 15
NCAND = 3
RAW = 3

K_ONES, K_W32, K_EARLIER, K_SAME, K_LOWER, K_SPEC = (i * P for i in range(6))
K_TRI = 6 * P
K_COEF = K_TRI + B
K_SPSEL = K_COEF + 2 * B
K_ID16 = K_SPSEL + 2
K_SPREAD = K_ID16 + P
K16 = K_SPREAD + INNER
K_IDENT = 0
K_BLK = K_IDENT + P
K_CHAN = K_BLK + MK * HEADS
K_WG = K_CHAN + 5 * MK
K32 = K_WG + EK * NEXP
V_TOKB, V_GAMMA, V_BETA, V_BO, V_LNS, V_LNB = (i * E for i in range(6))


def slots_of(c):
    return list(range(0 if c == 0 else 1 + TPC * c, 1 + TPC * (c + 1)))


def col0(c):
    return 0 if c == 0 else NSP + CW * c


def width(c):
    return CW + (NSP if c == 0 else 0)


def slot_cols(s, c):
    if s == 0:
        return 0, NSP
    return (NSP if c == 0 else 0) + (s - 1 - TPC * c) * P, P


def vit_tower(nc, xT, cls_tok, tok_w, cls_token, pos, vectors, small, wqkv, wo, w13, w2, k16_in, cand_in,
              out_patch, out_spec):
    with ExitStack() as ctx:
        def sb(name, shape, dt=F32):
            return ctx.enter_context(nc.sbuf_tensor(name, shape, dt))

        def sem(name):
            return ctx.enter_context(nc.semaphore(name))

        bank = [ctx.enter_context(nc.psum_tensor(f"bank{i}", [P, BANK], F32)) for i in range(8)]
        raw_rows = nc.dram_tensor("raw_rows", (NEXP, T), F32, kind="Internal").ap()
        raw_rows_sp = nc.dram_tensor("raw_rows_sp", (NEXP, NSP), F32, kind="Internal").ap()
        score_rows = nc.dram_tensor("score_rows", (NEXP, T), F32, kind="Internal").ap()

        k16 = sb("k16", [P, K16], F16)
        k32 = sb("k32", [P, K32])
        cand = sb("cand", [P, ROUNDS, NCAND], I32)
        ident = k32[:, K_IDENT:K_IDENT + P]
        blk = k32[:, K_BLK:K_BLK + MK * HEADS].rearrange("p (m h) -> p m h", m=MK)
        bq, bk, bv, alpha, aug = (k32[:, K_CHAN + i * MK:K_CHAN + (i + 1) * MK] for i in range(5))
        wg = k32[:, K_WG:K_WG + EK * NEXP].rearrange("p (k e) -> p k e", k=EK)
        vec = sb("vec", [P, 6 * E])
        tokb, gam, bet, bob, lns, lnb = (vec[:, v:v + E] for v in (V_TOKB, V_GAMMA, V_BETA, V_BO, V_LNS, V_LNB))
        bk_s, v_scale, v_bias, decay, aug_h, ez = (sb(n, [P, MK]) for n in
                                                   ("bk_s", "v_scale", "v_bias", "decay", "aug_h", "ez"))
        half32 = sb("half32", [P, 1])
        minus_half = sb("minus_half", [P, 4])
        eps_of = [sb("eps5", [P, 4]), sb("eps6", [P, 4])]
        zero16 = sb("zero16", [P, P], F16)
        cls_sb = sb("cls_sb", [1, E])

        wst = sb("wst", [P, 2, 3 * EK * HID])
        wh = sb("wh", [P, 2, 3 * EK * HID], F16)
        wl = sb("wl", [P, 2, 3 * EK * HID], F16)
        staged = wst[:].rearrange("p a n -> p (a n)")
        n_tw, n_qw, n_ow = DK * E, 3 * EK * INNER, MK * E
        tw = staged[:, 0:n_tw]
        qw = staged[:, n_tw:n_tw + n_qw]
        ow = staged[:, n_tw + n_qw:n_tw + n_qw + n_ow]
        def region(name, words):
            t, place = sb(name, [P, words]), [0]

            def at(shape, dt=F32, start=None):
                if start is not None:
                    place[0] = start
                n = 1
                for x in shape:
                    n *= x
                w = n if dt != F16 else (n + 1) // 2
                v = t[:, place[0]:place[0] + w]
                place[0] += w
                assert place[0] <= words, (name, place[0])
                if dt == F16:
                    v = v.bitcast(F16)
                if len(shape) == 1:
                    return v
                names = [f"a{i}" for i in range(len(shape))]
                return v.rearrange(f"p ({' '.join(names)}) -> p {' '.join(names)}",
                                   **{a: x for a, x in zip(names[1:], shape[1:])})
            return at

        at = region("front_weights", n_tw + n_qw + n_ow)
        twh, twl = at([n_tw], F16), at([n_tw], F16)
        qwh, qwl = at([n_qw], F16), at([n_qw], F16)
        owh, owl = at([n_ow], F16), at([n_ow], F16)
        rows = at([2, P], start=0)
        tri_e, sp_e = at([B, 2, NEXP], F16), at([B, 2, NEXP], F16)
        rank_sp = at([B, 2, NEXP])
        msp = at([B, 2, NEXP])
        ysp = at([EK, NEXP, NSP])
        prod = at([EK * NSP, B, NEXP])
        osum, osp = at([EK, NSP, B]), at([EK, NSP, B])

        def w13_of(w, par, which, k, m):
            o = (which * EK + k) * HID + m * P
            return w[:, par, o:o + P]

        def w2_of(w, par, m):
            o = 2 * EK * HID + m * E
            return w[:, par, o:o + E]

        def qkv_of(w, which, k, m):
            o = (which * EK + k) * INNER + m * P
            return w[:, o:o + P]

        H = sb("H", [P, SLOTS, E])
        Y = sb("Y", [P, SLOTS, E])
        y2T = sb("y2T", [P, EK, COLS])

        WMAX = CW + NSP
        at = region("front", 16200)
        px = at([NCH, DK, CW])
        pxh, pxl = at([NCH, DK, CW], F16), at([NCH, DK, CW], F16)
        yTh, yTl = at([EK, WMAX], F16), at([EK, WMAX], F16)
        oTh, oTl = at([MK, WMAX], F16), at([MK, WMAX], F16)
        q0 = at([4, MK, WMAX], start=0)
        U, STt, DEC = (at([MK * B * SEG], start=NCH * DK * CW + i * MK * B * SEG) for i in range(3))
        Us, STs, DECs = (t.rearrange("p (m b t) -> p m b t", m=MK, b=B) for t in (U, STt, DEC))
        sB = at([2, COLS], start=0)
        sg = at([2, WMAX])
        Tt = at([2, WMAX])
        Hh, Hl = at([2, HK, WMAX], F16), at([2, HK, WMAX], F16)
        OUT = at([TILES, E])
        xh1, xl1 = at([EK, COLS], F16), at([EK, COLS], F16)

        at = region("odd_chunk", 4 * MK * WMAX)
        q1 = at([4, MK, WMAX])
        X32 = at([EK, COLS], start=0)
        xh0, xl0 = at([EK, COLS], F16), at([EK, COLS], F16)
        q_, qk_, vp_, th_ = ([t[:, i] for t in (q0, q1)] for i in range(4))
        xh, xl = [xh0, xh1], [xl0, xl1]

        stats = sb("stats", [P, 4, 6])
        mean = [[sb(f"mean{k}{c}", [P, 4, 2]) for c in range(NCH)] for k in range(4)]
        rstd = [[sb(f"rstd{k}{c}", [P, 4]) for c in range(NCH)] for k in range(4)]
        shift = [[sb(f"shift{k}{c}", [P, 4]) for c in range(NCH)] for k in range(4)]
        var_eps = sb("var_eps", [P, 4])
        mx = sb("mx", [P, 4])
        dd = sb("dd", [P, 4, HEADS])
        ex = sb("ex", [P, 4, HEADS])
        sm = sb("sm", [P, 4])
        attn = sb("attn", [P, 4, HEADS])
        attn_hl = sb("attn_hl", [P, 4, 2, HEADS], F16)
        attn_T = sb("attn_T", [2 * HEADS, WMAX], F16)
        us2 = sb("us2", [P, MK, NSP])
        sp_state = sb("sp_state", [P, MK, NSP])
        sp_tmp = sb("sp_tmp", [P, MK])
        SC = sb("SC", [P, SLOTS, NEXP])
        SM = sb("SM", [P, TILES, NEXP])
        lo = sb("lo", [P, NEXP], I32)
        mid = sb("mid", [P, NCAND, NEXP], I32)
        ge = sb("ge", [P, SLOTS, NCAND, NEXP], F16)
        fl = sb("fl", [P, NCAND, NEXP])
        inc = sb("inc", [P, NEXP], I32)
        gt = sb("gt", [P, SLOTS, NEXP], F16)
        eq = sb("eq", [P, SLOTS, NEXP], F16)
        esum = sb("esum", [P, NEXP], F16)
        room = sb("room", [P, NEXP])
        allow = sb("allow", [P, SLOTS, NEXP])
        allow_sp = sb("allow_sp", [P, 2, NEXP], F16)
        asp = sb("asp", [P, 2, NEXP])
        keep = sb("keep", [P, TILES, NEXP])
        keep_s = sb("keep_s", [P, RAW, TILES])
        rows_sp = sb("rows_sp", [NEXP, NSP])
        h2sp = sb("h2sp", [P, EK, NSP])

        px_in = [sem(f"px_in{c}") for c in range(NCH)]
        tokw_in, rows01_in, pos_in, vec_in, k16_dma, small_in = (sem(n) for n in (
            "tokw_in", "rows01_in", "pos_in", "vec_in", "k16_dma", "small_in"))
        qw_in, ow_in = sem("qw_in"), sem("ow_in")
        ew_in = [sem("ew_in0"), sem("ew_in1")]
        sB_in = [sem("sB_in0"), sem("sB_in1")]
        rows_out, out_done = sem("rows_out"), sem("out_done")
        filled, posb_ready = sem("filled"), sem("posb_ready")
        tokw_hi, qw_hi, ow_hi = sem("tokw_hi"), sem("qw_hi"), sem("ow_hi")
        tokw_lo, qw_lo, ow_lo = sem("tokw_lo"), sem("qw_lo"), sem("ow_lo")
        px_hi, px_lo = sem("px_hi"), sem("px_lo")
        dve_step, act_step, pool_step = sem("dve_step"), sem("act_step"), sem("pool_step")
        tok_mm, tok_read = sem("tok_mm"), sem("tok_read")
        mean_ready, rstd_ready = sem("mean_ready"), sem("rstd_ready")
        h_ready, y_ready, bias_in = sem("h_ready"), sem("y_ready"), sem("bias_in")
        yT_mm, yT_hi, yT_lo = sem("yT_mm"), sem("yT_hi"), sem("yT_lo")
        q_mm, k_mm, v_mm = sem("q_mm"), sem("k_mm"), sem("v_mm")
        q_read, qk_ready, v_read = sem("q_read"), sem("qk_ready"), sem("v_read")
        chan_ready, chan_e = sem("chan_ready"), sem("chan_e")
        logit_mm, logit_sub, exp_ready, attn_ready = (sem("logit_mm"), sem("logit_sub"), sem("exp_ready"),
                                                      sem("attn_ready"))
        attn_T_mm, attn_T_ready = sem("attn_T_mm"), sem("attn_T_ready")
        aB_mm, u_ready = sem("aB_mm"), sem("u_ready")
        th_ready, sig_ready, qs_ready = sem("th_ready"), sem("sig_ready"), sem("qs_ready")
        o_ready, o_hi, o_lo = sem("o_ready"), sem("o_hi"), sem("o_lo")
        wo_mm, wo_read = sem("wo_mm"), sem("wo_read")
        h2_ready, y2_ready, y2T_mm, y2T_ready = sem("h2_ready"), sem("y2_ready"), sem("y2T_mm"), sem("y2T_ready")
        gate_mm, gate_sub, gexp_ready, sc_ready = (sem("gate_mm"), sem("gate_sub"), sem("gexp_ready"),
                                                   sem("sc_ready"))
        s0_mm, raw_mm, raw_ready = sem("s0_mm"), sem("raw_mm"), sem("raw_ready")
        x0_ready, h2sp_ready = sem("x0_ready"), sem("h2sp_ready")
        ge_ready, count_mm, flags_read = sem("ge_ready"), sem("count_mm"), sem("flags_read")
        tie_ready, rank_mm, rank_read, rank_sp_mm, rank_sp_read = (sem(n) for n in (
            "tie_ready", "rank_mm", "rank_read", "rank_sp_mm", "rank_sp_read"))
        sm_ready, rows_mm, rows_ready, bank7_free = (sem("sm_ready"), sem("rows_mm"), sem("rows_ready"),
                                                     sem("bank7_free"))
        ew_hi, ew_lo = sem("ew_hi"), sem("ew_lo")
        xs_ready, xs_hi, xs_lo = sem("xs_ready"), sem("xs_hi"), sem("xs_lo")
        g_mm, u_mm, silu_ready, t_ready = sem("g_mm"), sem("u_mm"), sem("silu_ready"), sem("t_ready")
        h_hi, h_lo, dn_mm, sums_read = sem("h_hi"), sem("h_lo"), sem("dn_mm"), sem("sums_read")
        out_ready, osp_ready = sem("out_ready"), sem("osp_ready")

        block = ctx.enter_context(nc.Block())

        class Steps:

            def __init__(self, eng, s):
                self.eng, self.s, self.n = eng, s, 0

            def did(self, ins):
                self.n += 1
                ins.then_inc(self.s, 1)

            def wait(self):
                self.eng.wait_ge(self.s, self.n)

            def then(self, ins):
                self.did(ins)
                self.wait()

        ORDER = """A0 B0 T0 A1 Q00 B1 Q01 A2 Q02 B2 Q03 T1 S0 Q10 Q11 R0 Q12 P0 Q13 T2 S1 O0 Q20 N0 Q21 R1
                   Q22 P1 Q23 G0 S2 O1 X0 N1 R2 G1 P2 X1 O2 N2 G2 X2""".split()
        NORMS = [({"A": 0, "B": 1, "O": 2, "N": 3}[x[0]], int(x[1])) for x in ORDER if x[0] in "ABON"]

        def norm_count(which, c):
            return NORMS.index((which, c)) + 1

        def slots_until(c):
            return slots_of(c)[-1] + 1

        def units(unit, loop):
            for j in range(NCH * RAW + 1):
                unit(j // NCH, j // NCH % 2, j % NCH)
            with loop(0, (NEXP - 1 - RAW) // 2) as pair:
                for i in range(2):
                    e, par = pair * 2 + (RAW + i), (RAW + i) % 2
                    unit(e, par, 1)
                    unit(e, par, 2)
                    unit(e + 1, 1 - par, 0)
            for c in (1, 2):
                unit(NEXP - 1, (NEXP - 1) % 2, c)

        def hidden_bank(static, e, i, which):
            if static and e < 2:
                return bank[5 + which]
            return bank[5 + (2 * i + which) % 3]

        @block.sync
        def _(sp):
            sp.dma_start(tw, tok_w).then_inc(tokw_in, 16)
            for c in range(NCH):
                sp.dma_start(px[:, c], xT[:, c]).then_inc(px_in[c], 16)
                if c == 1:
                    sp.dma_start(vec[:], vectors.to_broadcast([P, 6 * E])).then_inc(vec_in, 16)
            sp.dma_start(qw, wqkv).then_inc(qw_in, 16)
            sp.dma_start(ow, wo).then_inc(ow_in, 16)

            def load_expert(e, par):
                sp.dma_start(wst[:, par, 0:2 * EK * HID], w13[e]).then_inc(ew_in[par], 16)
                sp.dma_start(wst[:, par, 2 * EK * HID:], w2[e]).then_inc(ew_in[par], 16)

            for s in (tokw_lo, tokw_hi, qw_lo, qw_hi, ow_lo, ow_hi):
                sp.wait_ge(s, 1)
            load_expert(0, 0)
            load_expert(1, 1)
            sp.wait_ge(raw_ready, 2)
            sp.dma_start(raw_rows.rearrange("e (s n) -> s e n", n=P), rows[0:TILES * NEXP, 0, :]
                         ).then_inc(rows_out, 16)
            sp.dma_start(raw_rows_sp, rows_sp[:]).then_inc(rows_out, 16)
            sp.wait_ge(rows_out, 32)
            for par in (1, 0):
                sp.dma_start(sB[:, par, NSP:], raw_rows[2 - par:3 - par, :].to_broadcast([P, T])
                             ).then_inc(sB_in[par], 16)
                sp.dma_start(sB[:, par, 0:NSP], raw_rows_sp[2 - par:3 - par, :].to_broadcast([P, NSP])
                             ).then_inc(sB_in[par], 16)

            def load_weights(e, par):
                sp.wait_ge(ew_lo, (e - 1) * 6)
                sp.dma_start(wst[:, par, 0:2 * EK * HID], w13[e]).then_inc(ew_in[par], 16)
                sp.dma_start(wst[:, par, 2 * EK * HID:], w2[e]).then_inc(ew_in[par], 16)

            load_weights(2, 0)
            load_weights(3, 1)
            sp.wait_ge(rows_ready, 1)
            sp.dma_start(score_rows.rearrange("e (s n) -> s e n", n=P), rows[0:TILES * NEXP, 1, :]
                         ).then_inc(rows_out, 16)
            sp.wait_ge(rows_out, 48)

            def load_scores(e, par):
                sp.wait_ge(xs_ready, e - 2)
                sp.dma_start(sB[:, par, NSP:], score_rows[bass.ds(e, 1), :].to_broadcast([P, T])
                             ).then_inc(sB_in[par], 16)
                sp.dma_start(sB[:, par, 0:NSP], raw_rows_sp[bass.ds(e, 1), :].to_broadcast([P, NSP])
                             ).then_inc(sB_in[par], 16)

            load_scores(3, 1)
            with sp.Fori(2, NEXP // 2) as pair:
                for par in range(2):
                    e = pair * 2 + par
                    load_weights(e, par)
                    load_scores(e, par)
            for i in range(TILES // 3):
                sp.wait_ge(out_ready, 3 * (i + 1))
                sp.dma_start(out_patch[:, 3 * i:3 * i + 3], OUT[:, 3 * i:3 * i + 3]).then_inc(out_done, 16)
            sp.wait_ge(osp_ready, 1)
            sp.dma_start(out_spec, osp).then_inc(out_done, 16)
            sp.wait_ge(out_done, 16 * (1 + TILES // 3))

        @block.gpsimd
        def _(pool):
            G = nc.gpsimd
            steps = Steps(pool, pool_step)
            G.memset(H[:, 0, :], 0.0).then_inc(filled, 1)
            G.memset(Y[:, 0, :], 0.0).then_inc(filled, 1)
            pool.wait_ge(filled, 2)
            for j in range(P // B):
                pool.dma_start(Y[B * j:B * (j + 1), 1:, :],
                               pos[1 + j:1 + j + (P // B) * (TILES - 1) + 1:P // B, :].unsqueeze(0)
                               .to_broadcast([B, TILES, E])).then_inc(pos_in, 16)
            pool.dma_start(k32[:], small).then_inc(small_in, 16)
            pool.dma_start(H[1:2, 0, :], cls_token).then_inc(rows01_in, 16)
            pool.dma_start(Y[1:2, 0, :], pos[0:1, :]).then_inc(rows01_in, 16)
            pool.dma_start(cls_sb[:], cls_tok).then_inc(rows01_in, 16)
            pool.dma_start(k16[:], k16_in).then_inc(k16_dma, 16)
            pool.dma_start(cand[:], cand_in).then_inc(k16_dma, 16)
            G.memset(lo[:], 0).then_inc(filled, 1)
            G.memset(half32[:], SO / 2).then_inc(filled, 1)
            G.memset(zero16[:], 0.0).then_inc(filled, 1)
            G.memset(minus_half[:], -0.5).then_inc(filled, 1)
            G.memset(eps_of[0][:], 1e-5).then_inc(filled, 1)
            G.memset(eps_of[1][:], 1e-6).then_inc(filled, 1)
            pool.wait_ge(filled, 8)
            pool.wait_ge(pos_in, 16 * (P // B))
            pool.wait_ge(vec_in, 16)
            for c in range(NCH):
                a = 1 + TPC * c
                G.tensor_tensor(Y[:, a:a + TPC, :], Y[:, a:a + TPC, :],
                                tokb.unsqueeze(1).to_broadcast([P, TPC, E]), ALU.add).then_inc(posb_ready, 1)

            def norm(which, c):
                ns = len(slots_of(c))
                m, r, b = mean[which][c], rstd[which][c], shift[which][c]
                pool.wait_ge(mean_ready, norm_count(which, c))
                steps.then(G.tensor_tensor(var_eps[:, 0:ns], m[:, 0:ns, 1], eps_of[which == 2][:, 0:ns], ALU.add))
                steps.then(G.tensor_tensor(r[:, 0:ns], var_eps[:, 0:ns], minus_half[:, 0:ns], ALU.pow))
                if which % 2 == 0:
                    G.tensor_copy(var_eps[:, 0:ns], r[:, 0:ns]).then_inc(rstd_ready, 1)
                else:
                    steps.then(G.tensor_tensor(b[:, 0:ns], m[:, 0:ns, 0], r[:, 0:ns], ALU.mult))
                    G.tensor_scalar(b[:, 0:ns], b[:, 0:ns], -1.0, 0.0, ALU.mult, ALU.add).then_inc(rstd_ready, 1)

            def weights_hi(e, par):
                if isinstance(e, int):
                    pool.wait_ge(ew_in[par], 32 * (e // 2 + 1))
                else:
                    pool.wait_ge(ew_in[par], (e - par) * 16 + 32)
                    pool.sem_inc(pool_step, 1)
                G.tensor_scalar(wh[:, par], wst[:, par], SW, 0.0, ALU.mult, ALU.add).then_inc(ew_hi, 1)

            for stage in ORDER:
                c = int(stage[1])
                sl = slots_of(c)
                ns, s0, w = len(sl), sl[0], width(c)
                if stage[0] in "ABON":
                    norm({"A": 0, "B": 1, "O": 2, "N": 3}[stage[0]], c)
                elif stage[0] == "T":
                    pool.wait_ge(y_ready, slots_until(c))
                    G.tensor_tensor(H[:, s0:s0 + ns, :], H[:, s0:s0 + ns, :],
                                    lnb.unsqueeze(1).to_broadcast([P, ns, E]), ALU.add).then_inc(bias_in, 1)
                elif stage[0] == "P":
                    pool.wait_ge(sig_ready, c + 1)
                    for m in range(MK):
                        pool.wait_ge(qs_ready, MK * c + m + 1)
                        G.tensor_tensor(qk_[c % 2][:, m, 0:w], qk_[c % 2][:, m, 0:w], th_[c % 2][:, m, 0:w],
                                        ALU.add).then_inc(o_ready, 1)
                if stage == "S1":
                    weights_hi(0, 0)
                if stage == "O1":
                    weights_hi(1, 1)

            def scaled_tokens(e, par):
                pool.wait_ge(sB_in[par], (32 * (e // 2) + (32 if par else 0)) if isinstance(e, int)
                             else (e - par) * 16 + (32 if par else 0))
                for k in range(EK):
                    ins = G.tensor_tensor(X32[:, k], y2T[:, k], sB[:, par], ALU.mult)
                ins.then_inc(xs_ready, 1)

            def next_expert(e, par):
                pool.wait_ge(xs_hi, e * (NCH * EK))
                pool.wait_ge(xs_lo, e * (NCH * EK))
                scaled_tokens(e, par)
                pool.wait_ge(dn_mm, (e - 1) * NCH)
                weights_hi(e, par)

            pool.wait_ge(xs_hi, NCH * EK)
            pool.wait_ge(xs_lo, NCH * EK)
            scaled_tokens(1, 1)
            next_expert(2, 0)
            next_expert(3, 1)
            with pool.Fori(2, NEXP // 2) as pair:
                for par in range(2):
                    next_expert(pair * 2 + par, par)

        @block.scalar
        def _(act):
            A = nc.scalar
            act.wait_ge(tokw_in, 16)
            A.activation(twh, tw, ACT.Copy, scale=SW).then_inc(tokw_hi, 1)
            for c in range(NCH):
                act.wait_ge(px_in[c], 16)
                A.activation(pxh[:, c], px[:, c], ACT.Copy, scale=SX).then_inc(px_hi, 1)
            act.wait_ge(qw_in, 16)
            A.activation(qwh, qw, ACT.Copy, scale=SW).then_inc(qw_hi, 1)
            act.wait_ge(ow_in, 16)
            A.activation(owh, ow, ACT.Copy, scale=SW).then_inc(ow_hi, 1)
            act.wait_ge(small_in, 16)
            A.activation(ez[:], alpha, ACT.Tanh, scale=0.5).then_inc(chan_e, 1)
            act.wait_ge(filled, 8)

            def tokens_hi(par, piece):
                c, k = piece // EK, piece % EK
                a, w = col0(c), width(c)
                A.activation(xh[par][:, k, a:a + w], X32[:, k, a:a + w], ACT.Copy, scale=SXS).then_inc(xs_hi, 1)

            for stage in ORDER:
                c, par = int(stage[1]), int(stage[1]) % 2
                w, sl = width(c), slots_of(c)
                ns, s0 = len(sl), sl[0]
                q, vp, th = q_[par], vp_[par], th_[par]
                if stage[0] in "BN":
                    which, done = (1, y_ready) if stage[0] == "B" else (3, y2_ready)
                    act.wait_ge(rstd_ready, norm_count(which, c))
                    for i, s in enumerate(sl):
                        A.activation(Y[:, s, :], H[:, s, :], ACT.Identity, bias=shift[which][c][:, i:i + 1],
                                     scale=rstd[which][c][:, i:i + 1]).then_inc(done, 1)
                elif stage[0] == "T":
                    for k in range(EK):
                        act.wait_ge(yT_mm, EK * c + k + 1)
                        if c:
                            act.wait_ge(v_mm, MK * c)
                        A.activation(yTh[:, k, 0:w], bank[6 + k][:, 0:w], ACT.Copy, scale=SY).then_inc(yT_hi, 1)
                elif stage[0] == "Q":
                    m = int(stage[2])
                    n = MK * c + m
                    if n == 0:
                        act.wait_ge(chan_ready, 1)
                        act.wait_ge(tok_mm, TILES)
                        act.wait_ge(px_lo, NCH)
                        act.wait_ge(px_hi, NCH)
                    act.wait_ge(q_mm, n + 1)
                    if c == 2 and m == 0:
                        act.wait_ge(o_lo, 1)
                    A.activation(q[:, m, 0:w], bank[0][:, 0:w], ACT.Identity, bias=bq[:, m:m + 1],
                                 scale=1.0 / (SY * SW)).then_inc(q_read, 1)
                    act.wait_ge(v_mm, n + 1)
                    A.activation(vp[:, m, 0:w], bank[2][:, 0:w], ACT.Identity, bias=v_bias[:, m:m + 1],
                                 scale=v_scale[:, m:m + 1]).then_inc(v_read, 1)
                    act.wait_ge(q_read, n + 1)
                    A.activation(th[:, m, 0:w], q[:, m, 0:w], ACT.Tanh, scale=aug_h[:, m:m + 1]
                                 ).then_inc(th_ready, 1)
                    if m == MK - 1:
                        act.wait_ge(th_ready, n + 1)
                        A.activation(th[:, :, 0:w], th[:, :, 0:w], ACT.Identity, bias=half32[:], scale=SO / 2
                                     ).then_inc(sig_ready, 1)
                elif stage[0] == "S":
                    act.wait_ge(logit_sub, c + 1)
                    A.activation(ex[:, 0:ns], dd[:, 0:ns], ACT.Exp, scale=HDIM ** -0.5 / (SY * SW)
                                 ).then_inc(exp_ready, 1)
                elif stage[0] == "R":
                    act.wait_ge(attn_T_mm, c + 1)
                    if c:
                        act.wait_ge(aB_mm, MK * c)
                    A.activation(attn_T[:, 0:w], bank[5][0:2 * HEADS, :].bitcast(F16)[:, 0:w], ACT.Copy
                                 ).then_inc(attn_T_ready, 1)
                elif stage[0] == "P":
                    if c:
                        act.wait_ge(wo_mm, s0)
                    for m in range(MK):
                        act.wait_ge(o_ready, MK * c + m + 1)
                        A.activation(oTh[:, m, 0:w], qk_[par][:, m, 0:w], ACT.Copy).then_inc(o_hi, 1)
                elif stage[0] == "G":
                    for k in range(EK):
                        act.wait_ge(y2T_mm, EK * c + k + 1)
                        A.activation(y2T[:, k, col0(c):col0(c) + w], bank[6 + k][:, 0:w], ACT.Copy
                                     ).then_inc(y2T_ready, 1)
                    act.wait_ge(gate_sub, c + 1)
                    A.activation(ex[:, 0:ns], dd[:, 0:ns], ACT.Exp).then_inc(gexp_ready, 1)
                elif stage[0] == "X":
                    act.wait_ge(x0_ready, EK * (c + 1))
                    for k in range(EK):
                        tokens_hi(0, EK * c + k)

            act.wait_ge(raw_mm, 1)
            A.activation(rows[0:TILES * NEXP, 0, :], bank[0][0:TILES * NEXP, 0:P], ACT.Copy).then_inc(raw_ready, 1)
            A.activation(rows_sp[:], bank[1][0:NEXP, 0:NSP], ACT.Copy).then_inc(raw_ready, 1)

            def unit(e, par, c):
                static = isinstance(e, int)
                w, j = width(c), e * NCH + c
                for m in range(HK):
                    n, i = j * HK + m, c * HK + m
                    act.wait_ge(g_mm, n + 1)
                    if not static or n >= 2:
                        act.wait_ge(t_ready, n - 1)
                    A.activation(sg[:, m % 2, 0:w], hidden_bank(static, e, i, 0)[:, 0:w], ACT.Silu,
                                 scale=1.0 / (SXS * SW)).then_inc(silu_ready, 1)
                    if 4 <= i <= 9 and not (static and e == NEXP - 1):
                        if i == 4:
                            act.wait_ge(xs_ready, e + 1)
                            if not static or e:
                                act.wait_ge(u_mm, e * (NCH * HK))
                        tokens_hi(1 - par, i - 4)
                    act.wait_ge(t_ready, n + 1)
                    if not static or j >= 2:
                        act.wait_ge(dn_mm, j - 1)
                    A.activation(Hh[:, (par + c) % 2, m, 0:w], Tt[:, m % 2, 0:w], ACT.Copy).then_inc(h_hi, 1)
                    if static and n == 18:
                        act.wait_ge(rows_mm, 1)
                        A.activation(rows[0:TILES * NEXP, 1, :], bank[7][0:TILES * NEXP, 0:P], ACT.Copy
                                     ).then_inc(rows_ready, 1)
                        A.activation(asp[:], bank[7][:, P:P + 2 * NEXP].rearrange("p (t e) -> p t e", e=NEXP),
                                     ACT.Copy).then_inc(bank7_free, 1)

            units(unit, act.Fori)

        @block.vector
        def _(dve):
            V = nc.vector
            steps = Steps(dve, dve_step)

            def low_half(out, src, scale, hi):
                return V.scalar_tensor_tensor(out=out, in0=src, scalar=scale, in1=hi, op0=ALU.mult,
                                              op1=ALU.subtract)

            def norm_stats(src, which, c):
                ns = len(slots_of(c))
                for i in range(ns):
                    steps.did(V.bn_stats(stats[:, i, :], src[:, i, :]))
                steps.wait()
                for i in range(ns):
                    ins = V.bn_aggr(mean[which][c][:, i, :], stats[:, i, :])
                ins.then_inc(mean_ready, 1)
                dve.wait_ge(mean_ready, norm_count(which, c))

            def softmax_front(logits, ns):
                steps.then(V.tensor_reduce(mx[:, 0:ns], logits, AX, ALU.max))
                return V.tensor_tensor(dd[:, 0:ns], logits, mx[:, 0:ns].unsqueeze(2).to_broadcast([P, ns, HEADS]),
                                       ALU.subtract)

            def softmax_back(out, ns):
                steps.then(V.tensor_reduce(sm[:, 0:ns], ex[:, 0:ns], AX, ALU.add))
                steps.then(V.reciprocal(sm[:, 0:ns], sm[:, 0:ns]))
                return V.tensor_tensor(out, ex[:, 0:ns], sm[:, 0:ns].unsqueeze(2).to_broadcast([P, ns, HEADS]),
                                       ALU.mult)

            def tokens_lo(par, piece):
                c, k = piece // EK, piece % EK
                a, w = col0(c), width(c)
                low_half(xl[par][:, k, a:a + w], X32[:, k, a:a + w], SXS, xh[par][:, k, a:a + w]
                         ).then_inc(xs_lo, 1)

            def weights_lo(par, i):
                a = i * HID
                low_half(wl[:, par, a:a + HID], wst[:, par, a:a + HID], SW, wh[:, par, a:a + HID]
                         ).then_inc(ew_lo, 1)

            dve.wait_ge(tokw_hi, 1)
            low_half(twl, tw, SW, twh).then_inc(tokw_lo, 1)
            for c in range(NCH):
                dve.wait_ge(px_hi, c + 1)
                low_half(pxl[:, c], px[:, c], SX, pxh[:, c]).then_inc(px_lo, 1)
            dve.wait_ge(qw_hi, 1)
            low_half(qwl, qw, SW, qwh).then_inc(qw_lo, 1)
            dve.wait_ge(chan_e, 1)
            steps.then(V.tensor_scalar(decay[:], ez[:], 0.5, 0.5, ALU.mult, ALU.add))
            steps.then(V.tensor_scalar(ez[:], ez[:], -0.5, 0.5, ALU.mult, ALU.add))
            steps.did(V.tensor_scalar(v_scale[:], ez[:], 1.0 / (SY * SW * SA), None, ALU.mult))
            steps.did(V.scalar_tensor_tensor(out=v_bias[:], in0=ez[:], scalar=1.0 / SA, in1=bv,
                                             op0=ALU.mult, op1=ALU.mult))
            steps.did(V.tensor_scalar(bk_s[:], bk, SY * SW, None, ALU.mult))
            V.tensor_scalar(aug_h[:], aug, 0.5, None, ALU.mult).then_inc(chan_ready, 1)

            for stage in ORDER:
                c, par = int(stage[1]), int(stage[1]) % 2
                w, sl = width(c), slots_of(c)
                ns, s0 = len(sl), sl[0]
                q, qk, vp, th = q_[par], qk_[par], vp_[par], th_[par]
                if stage[0] == "A":
                    if c == 0:
                        dve.wait_ge(rows01_in, 48)
                        dve.wait_ge(filled, 2)
                        steps.did(V.tensor_tensor(H[:, 0, :], H[:, 0, :], Y[:, 0, :], ALU.add))
                    dve.wait_ge(posb_ready, c + 1)
                    for s in sl:
                        if s:
                            n = s - 1
                            i = n - TPC * c
                            dve.wait_ge(tok_mm, TPC * c + (2 if i < 2 else 3))
                            V.scalar_tensor_tensor(out=H[:, s, :], in0=bank[2 * c + i // 2][:, (i % 2) * E:][:, 0:E],
                                                   scalar=1.0 / (SX * SW), in1=Y[:, s, :], op0=ALU.mult,
                                                   op1=ALU.add).then_inc(tok_read, 1)
                    dve.wait_ge(tok_read, sl[-1])
                    steps.wait()
                    norm_stats(H[:, s0:s0 + ns], 0, c)
                elif stage[0] == "B":
                    dve.wait_ge(vec_in, 16)
                    for i, s in enumerate(sl):
                        steps.did(V.scalar_tensor_tensor(out=H[:, s, :], in0=H[:, s, :],
                                                         scalar=mean[0][c][:, i, 0:1], in1=gam, op0=ALU.subtract,
                                                         op1=ALU.mult))
                    steps.wait()
                    dve.wait_ge(rstd_ready, norm_count(0, c))
                    for i, s in enumerate(sl):
                        steps.did(V.scalar_tensor_tensor(out=H[:, s, :], in0=H[:, s, :],
                                                         scalar=rstd[0][c][:, i:i + 1], in1=bet, op0=ALU.mult,
                                                         op1=ALU.add))
                    steps.wait()
                    if c == 0:
                        steps.then(V.tensor_copy(H[0:1, 0, :], cls_sb[0:1, :]))
                    norm_stats(H[:, s0:s0 + ns], 1, c)
                elif stage[0] == "T":
                    for k in range(EK):
                        dve.wait_ge(yT_hi, EK * c + k + 1)
                        low_half(yTl[:, k, 0:w], bank[6 + k][:, 0:w], SY, yTh[:, k, 0:w]).then_inc(yT_lo, 1)
                elif stage[0] == "Q":
                    m = int(stage[2])
                    n = MK * c + m
                    if n == 1:
                        dve.wait_ge(ow_hi, 1)
                        low_half(owl, ow, SW, owh).then_inc(ow_lo, 1)
                    dve.wait_ge(k_mm, n + 1)
                    dve.wait_ge(q_read, n + 1)
                    if c == 2 and m == 0:
                        dve.wait_ge(o_lo, 1)
                    V.scalar_tensor_tensor(out=qk[:, m, 0:w], in0=bank[1][:, 0:w], scalar=bk_s[:, m:m + 1],
                                           in1=q[:, m, 0:w], op0=ALU.add, op1=ALU.mult).then_inc(qk_ready, 1)
                    if n == 2:
                        steps.then(V.tensor_copy(DECs, decay[:].unsqueeze(2).unsqueeze(3)
                                                 .to_broadcast([P, MK, B, SEG])))
                        steps.did(V.memset(DECs[:, :, :, 0], 0.0))
                elif stage[0] == "S":
                    dve.wait_ge(logit_mm, c + 1)
                    lg = bank[5][:, 0:ns * HEADS].rearrange("p (s h) -> p s h", h=HEADS)
                    softmax_front(lg, ns).then_inc(logit_sub, 1)
                    dve.wait_ge(exp_ready, c + 1)
                    steps.then(softmax_back(attn[:, 0:ns], ns))
                    steps.then(V.tensor_scalar(attn_hl[:, 0:ns, 0], attn[:, 0:ns], SA, None, ALU.mult))
                    low_half(attn_hl[:, 0:ns, 1], attn[:, 0:ns], SA, attn_hl[:, 0:ns, 0]).then_inc(attn_ready, 1)
                elif stage[0] == "R":
                    off = NSP if c == 0 else 0
                    if c:
                        steps.did(V.tensor_copy(Us[:, :, :, 0], STs[:, :, :, SEG - 1]))
                    dve.wait_ge(v_read, MK * (c + 1))
                    for m in range(MK):
                        dve.wait_ge(aB_mm, MK * c + m + 1)
                        aB = bank[3 + m % 2]
                        if c == 0:
                            steps.did(V.tensor_tensor(us2[:, m, :], aB[:, 0:NSP], vp[:, m, 0:NSP], ALU.mult))
                        V.tensor_tensor(Us[:, m, :, 1:].rearrange("p b t -> p t b"),
                                        aB[:, off:off + CW].rearrange("p (t b) -> p t b", b=B),
                                        vp[:, m, off:off + CW].rearrange("p (t b) -> p t b", b=B),
                                        ALU.mult).then_inc(u_ready, 1)
                    if c == 0:
                        steps.wait()
                        steps.did(V.tensor_copy(sp_state[:, :, 0], us2[:, :, 0]))
                        steps.then(V.tensor_tensor(sp_tmp[:], us2[:, :, 0], decay[:], ALU.mult))
                        steps.then(V.tensor_tensor(sp_state[:, :, 1], us2[:, :, 1], sp_tmp[:], ALU.add))
                        steps.did(V.tensor_copy(Us[:, :, :, 0], sp_state[:, :, 1:2].to_broadcast([P, MK, B])))
                    steps.wait()
                    dve.wait_ge(u_ready, MK * (c + 1))
                    steps.then(V.tensor_tensor_scan(STt, DEC, U, 0.0, ALU.mult, ALU.add))
                    if c == 0:
                        steps.did(V.scalar_tensor_tensor(out=qk[:, :, 0:NSP], in0=q[:, :, 0:NSP], scalar=SO,
                                                         in1=sp_state[:], op0=ALU.mult, op1=ALU.mult))
                    for m in range(MK):
                        V.scalar_tensor_tensor(
                            out=qk[:, m, off:off + CW].rearrange("p (t b) -> p t b", b=B),
                            in0=q[:, m, off:off + CW].rearrange("p (t b) -> p t b", b=B), scalar=SO,
                            in1=STs[:, m, :, 1:].rearrange("p b t -> p t b"), op0=ALU.mult,
                            op1=ALU.mult).then_inc(qs_ready, 1)
                    dve.wait_ge(qs_ready, MK * (c + 1))
                elif stage[0] == "P":
                    for m in range(MK):
                        dve.wait_ge(o_hi, MK * c + m + 1)
                        ins = V.tensor_tensor(oTl[:, m, 0:w], qk[:, m, 0:w], oTh[:, m, 0:w], ALU.subtract)
                    ins.then_inc(o_lo, 1)
                elif stage[0] == "O":
                    for s in sl:
                        dve.wait_ge(wo_mm, s + 1)
                        V.scalar_tensor_tensor(out=Y[:, s, :], in0=bank[3 + s % 2][:, 0:E],
                                               scalar=1.0 / (SO * SW), in1=bob, op0=ALU.mult,
                                               op1=ALU.add).then_inc(wo_read, 1)
                    dve.wait_ge(wo_read, slots_until(c))
                    norm_stats(Y[:, s0:s0 + ns], 2, c)
                elif stage[0] == "N":
                    for i, s in enumerate(sl):
                        steps.did(V.scalar_tensor_tensor(out=Y[:, s, :], in0=Y[:, s, :],
                                                         scalar=mean[2][c][:, i, 0:1], in1=lns, op0=ALU.subtract,
                                                         op1=ALU.mult))
                    steps.wait()
                    dve.wait_ge(rstd_ready, norm_count(2, c))
                    dve.wait_ge(bias_in, c + 1)
                    for i, s in enumerate(sl):
                        steps.did(V.scalar_tensor_tensor(out=H[:, s, :], in0=Y[:, s, :],
                                                         scalar=rstd[2][c][:, i:i + 1], in1=H[:, s, :],
                                                         op0=ALU.mult, op1=ALU.add))
                    steps.wait()
                    norm_stats(H[:, s0:s0 + ns], 3, c)
                elif stage[0] == "G":
                    dve.wait_ge(gate_mm, c + 1)
                    lg = bank[5][:, 0:ns * NEXP].rearrange("p (s h) -> p s h", h=NEXP)
                    softmax_front(lg, ns).then_inc(gate_sub, 1)
                    dve.wait_ge(gexp_ready, c + 1)
                    softmax_back(SC[:, s0:s0 + ns], ns).then_inc(sc_ready, 1)
                elif stage[0] == "X":
                    dve.wait_ge(s0_mm, c + 1)
                    for k in range(EK):
                        V.tensor_tensor(X32[:, k, col0(c):col0(c) + w], y2T[:, k, col0(c):col0(c) + w],
                                        bank[5][:, 0:w], ALU.mult).then_inc(x0_ready, 1)
                    dve.wait_ge(x0_ready, EK * (c + 1))
                    for k in range(EK):
                        dve.wait_ge(xs_hi, EK * c + k + 1)
                        tokens_lo(0, EK * c + k)
                if stage == "P0":
                    dve.wait_ge(ew_hi, 1)
                if stage in ("Q13", "Q20", "Q21", "Q22", "Q23", "G0"):
                    weights_lo(0, ["Q13", "Q20", "Q21", "Q22", "Q23", "G0"].index(stage))

            dve.wait_ge(sc_ready, NCH)
            dve.wait_ge(k16_dma, 32)
            dve.wait_ge(raw_mm, 1)
            V.tensor_copy(h2sp[:], bank[2][:, 0:EK * NSP].rearrange("p (k t) -> p k t", t=NSP)
                          ).then_inc(h2sp_ready, 1)

            def round_front(r):
                steps.then(V.tensor_tensor(mid[:], lo[:].unsqueeze(1).to_broadcast([P, NCAND, NEXP]),
                                           cand[:, r].unsqueeze(2).to_broadcast([P, NCAND, NEXP]), ALU.bitwise_or))
                V.tensor_tensor(ge[:].rearrange("p s c e -> p c s e"),
                                SC[:].unsqueeze(1).to_broadcast([P, NCAND, SLOTS, NEXP]),
                                mid[:].bitcast(F32).unsqueeze(2).to_broadcast([P, NCAND, SLOTS, NEXP]),
                                ALU.is_ge).then_inc(ge_ready, 1)

            def round_back(r):
                dve.wait_ge(count_mm, r + 1)
                V.tensor_scalar(fl[:], bank[7][:, 0:NCAND * NEXP].rearrange("p (c e) -> p c e", e=NEXP),
                                float(CAP), 2.0 ** (2 * (ROUNDS - 1 - r)), ALU.is_ge, ALU.mult
                                ).then_inc(flags_read, 1)
                dve.wait_ge(flags_read, r + 1)
                with nc.allow_low_precision(reason="at most three equal powers of two: exact in int32"):
                    steps.then(V.tensor_reduce(inc[:], fl[:].rearrange("p c e -> p e c"), AX, ALU.add))
                steps.then(V.tensor_tensor(lo[:], lo[:], inc[:], ALU.bitwise_or))

            def find_ties():
                cut = lo[:].bitcast(F32).unsqueeze(1).to_broadcast([P, SLOTS, NEXP])
                steps.did(V.tensor_tensor(gt[:], SC[:], cut, ALU.is_gt))
                steps.then(V.tensor_tensor(eq[:], SC[:], cut, ALU.is_equal))
                with nc.allow_low_precision(reason="a count up to nine: exact in float16"):
                    V.tensor_reduce(esum[:], eq[:, 1:].rearrange("p s e -> p e s"), AX, ALU.add
                                    ).then_inc(tie_ready, 1)

            def find_special_ties():
                dve.wait_ge(tie_ready, 1)
                tri = k16[:, K_TRI:K_TRI + B]
                coef = k16[:, K_COEF:K_COEF + 2 * B].rearrange("p (b t) -> p b t", t=2)
                for t in range(2):
                    V.tensor_tensor(tri_e[:, :, t], tri.unsqueeze(2).to_broadcast([P, B, NEXP]),
                                    esum[:].unsqueeze(1).to_broadcast([P, B, NEXP]), ALU.mult)
                    ins = V.tensor_tensor(sp_e[:, :, t], coef[:, :, t:t + 1].to_broadcast([P, B, NEXP]),
                                          eq[:, 0:1].to_broadcast([P, B, NEXP]), ALU.mult)
                ins.then_inc(tie_ready, 1)

            def take():
                dve.wait_ge(rank_mm, 1)
                steps.then(V.tensor_scalar(room[:], bank[7][:, 0:NEXP], -1.0, float(CAP), ALU.mult, ALU.add))
                steps.then(V.tensor_tensor(allow[:], eq[:], room[:].unsqueeze(1).to_broadcast([P, SLOTS, NEXP]),
                                           ALU.mult))
                steps.then(V.scalar_tensor_tensor(out=allow[:], in0=gt[:], scalar=TIE_BIG, in1=allow[:],
                                                  op0=ALU.mult, op1=ALU.add))
                V.tensor_tensor(keep[:], bank[7][:, 128:128 + TILES * NEXP].rearrange("p (s e) -> p s e", e=NEXP),
                                allow[:, 1:], ALU.is_lt).then_inc(rank_read, 1)
                for t in range(2):
                    steps.did(V.tensor_tensor(allow_sp[:, t], allow[:, 0],
                                              k16[:, K_SPSEL + t:K_SPSEL + t + 1].to_broadcast([P, NEXP]), ALU.mult))
                dve.wait_ge(rank_read, 1)
                for e in range(RAW):
                    steps.did(V.tensor_scalar(keep_s[:, e], keep[:, :, e], 1.0 / (ST_ * SW), None, ALU.mult))
                V.tensor_tensor(SM[:], SC[:, 1:], keep[:], ALU.mult).then_inc(sm_ready, 1)

            def copy_special_ranks():
                dve.wait_ge(rank_sp_mm, 1)
                V.tensor_copy(rank_sp, bank[7][:, :].rearrange("p (b t e) -> p b t e", b=B, t=2)
                              ).then_inc(rank_sp_read, 1)

            def take_specials():
                dve.wait_ge(bank7_free, 1)
                dve.wait_ge(rank_sp_read, 1)
                for t in range(2):
                    steps.did(V.tensor_tensor(msp[:, :, t], rank_sp[:, :, t], asp[:, t:t + 1].to_broadcast([P, B, NEXP]),
                                              ALU.is_lt))

            def sum_tile(e, i):
                if i in (0, 2, 6):
                    last = {0: 1, 2: 2, 6: 3}[i]
                    dve.wait_ge(dn_mm, NCH * (NEXP - 1 if e is None else e) + last)
                    steps.wait()
                src = bank[i // 2][:, (i % 2) * E:][:, 0:E]
                dst = OUT[:, i, :]
                if e == 0:
                    ins = V.scalar_tensor_tensor(out=dst, in0=src, scalar=keep_s[:, 0, i:i + 1],
                                                 in1=H[:, 1 + i, :], op0=ALU.mult, op1=ALU.add)
                elif e is not None:
                    ins = V.scalar_tensor_tensor(out=dst, in0=src, scalar=keep_s[:, e, i:i + 1], in1=dst,
                                                 op0=ALU.mult, op1=ALU.add)
                else:
                    ins = V.scalar_tensor_tensor(out=dst, in0=src, scalar=1.0 / (ST_ * SW), in1=dst,
                                                 op0=ALU.mult, op1=ALU.add)
                ins.then_inc(out_ready if e is None else sums_read, 1)

            def special_sums(first, count, done):
                spec = bank[4][:, E:E + EK * NEXP * NSP].rearrange("p (k e t) -> p k e t", k=EK, e=NEXP)
                V.tensor_scalar(ysp[:, :, first:first + count], spec[:, :, first:first + count], 1.0 / (ST_ * SW),
                                None, ALU.mult).then_inc(done, 1)

            def beside(n):
                if n < ROUNDS:
                    round_back(n)
                if n + 1 < ROUNDS:
                    round_front(n + 1)
                if n == ROUNDS - 1:
                    find_ties()
                if n == ROUNDS:
                    find_special_ties()
                if n == 16:
                    take()
                if n == 17:
                    copy_special_ranks()
                if n == 19:
                    take_specials()
                for e, at_ in ((0, {16: (0, 3), 17: (3, 6), 18: (6, 9)}),
                               (1, {24: (0, 2), 26: (2, 4), 27: (4, 6), 28: (6, 9)}),
                               (2, {34: (0, 2), 37: (2, 4), 38: (4, 6), 39: (6, 9)})):
                    if n in at_:
                        for i in range(*at_[n]):
                            sum_tile(e, i)
                        if i == TILES - 1:
                            special_sums(e, 1, sums_read)

            round_front(0)

            def unit(e, par, c):
                static = isinstance(e, int)
                w, j = width(c), e * NCH + c
                for m in range(HK):
                    n, i = j * HK + m, c * HK + m
                    dve.wait_ge(u_mm, n + 1)
                    dve.wait_ge(silu_ready, n + 1)
                    if not static or n >= 2:
                        dve.wait_ge(h_lo, n - 1)
                    V.scalar_tensor_tensor(out=Tt[:, m % 2, 0:w], in0=hidden_bank(static, e, i, 1)[:, 0:w],
                                           scalar=ST_ / (SXS * SW), in1=sg[:, m % 2, 0:w], op0=ALU.mult,
                                           op1=ALU.mult).then_inc(t_ready, 1)
                    if not (static and e == NEXP - 1):
                        if 4 <= i <= 9:
                            dve.wait_ge(xs_hi, (e + 1) * (NCH * EK) + (i - 3))
                            tokens_lo(1 - par, i - 4)
                        if 6 <= i:
                            if i == 6:
                                dve.wait_ge(ew_hi, e + 2)
                            weights_lo(1 - par, i - 6)
                    dve.wait_ge(h_hi, n + 1)
                    V.tensor_tensor(Hl[:, (par + c) % 2, m, 0:w], Tt[:, m % 2, 0:w],
                                    Hh[:, (par + c) % 2, m, 0:w], ALU.subtract).then_inc(h_lo, 1)
                    if static:
                        beside(n)

            units(unit, dve.Fori)

            dve.wait_ge(sums_read, RAW * (TILES + 1))
            for i in range(TILES):
                sum_tile(None, i)
            special_sums(RAW, NEXP - RAW, dve_step)
            steps.n += 1
            steps.wait()
            for k in range(EK):
                for t in range(NSP):
                    steps.did(V.tensor_tensor(prod[:, k * NSP + t], msp[:, :, t],
                                              ysp[:, k, :, t].unsqueeze(1).to_broadcast([P, B, NEXP]), ALU.mult))
            steps.wait()
            steps.then(V.tensor_reduce(osum.rearrange("p k t b -> p (k t b)"),
                                       prod.rearrange("p x b e -> p (x b) e"), AX, ALU.add))
            V.tensor_tensor(osp, osum, h2sp[:].unsqueeze(3).to_broadcast([P, EK, NSP, B]), ALU.add
                            ).then_inc(osp_ready, 1)

        @block.tensor
        def _(pe):
            mm = nc.tensor.matmul

            def cut_products(out, pairs, start=True, stop=True):
                for i, ((ah, al), (bh, bl)) in enumerate(pairs):
                    mm(out, ah, bh, start=start and i == 0, stop=False, skip_group_check=not start)
                    mm(out, ah, bl, start=False, stop=False, skip_group_check=not start)
                    ins = mm(out, al, bh, start=False, stop=stop and i == len(pairs) - 1,
                             skip_group_check=not start)
                return ins

            pe.wait_ge(tokw_lo, 1)
            for c in range(NCH):
                pe.wait_ge(px_lo, c + 1)
                for i in range(TPC):
                    a = i * P
                    cut_products(bank[2 * c + i // 2][:, (i % 2) * E:][:, 0:E],
                                 [((pxh[:, c, k, a:a + P], pxl[:, c, k, a:a + P]),
                                   (twh[:, k * E:(k + 1) * E], twl[:, k * E:(k + 1) * E])) for k in range(DK)]
                                 ).then_inc(tok_mm, 1)
            pe.wait_ge(small_in, 16)
            for stage in ORDER:
                c, par = int(stage[1]), int(stage[1]) % 2
                w, sl = width(c), slots_of(c)
                ns, s0 = len(sl), sl[0]
                if stage[0] == "T":
                    for k in range(EK):
                        if c:
                            pe.wait_ge(yT_lo, EK * (c - 1) + k + 1)
                        for s in sl:
                            pe.wait_ge(y_ready, s + 1)
                            a, n = slot_cols(s, c)
                            ins = nc.tensor.transpose(bank[6 + k][:, a:a + n], Y[0:n, s, k * P:(k + 1) * P],
                                                      ident[0:n, 0:n])
                        ins.then_inc(yT_mm, 1)
                elif stage[0] == "Q":
                    m = int(stage[2])
                    n = MK * c + m
                    if n == 0:
                        pe.wait_ge(qw_lo, 1)
                        pe.wait_ge(tok_read, TPC * 2)
                    pe.wait_ge(yT_lo, EK * (c + 1))
                    for which, done, free in ((0, q_mm, q_read), (1, k_mm, qk_ready), (2, v_mm, v_read)):
                        if n:
                            pe.wait_ge(free, n)
                        cut_products(bank[which][:, 0:w],
                                     [((qkv_of(qwh, which, k, m), qkv_of(qwl, which, k, m)),
                                       (yTh[:, k, 0:w], yTl[:, k, 0:w])) for k in range(EK)]).then_inc(done, 1)
                elif stage[0] == "S":
                    pe.wait_ge(qk_ready, MK * (c + 1))
                    if c == 0:
                        pe.wait_ge(tok_read, TILES)
                    else:
                        pe.wait_ge(attn_T_ready, c)
                    if c == 2:
                        pe.wait_ge(gate_sub, 1)
                    for i, s in enumerate(sl):
                        a, _ = slot_cols(s, c)
                        for m in range(MK):
                            ins = mm(bank[5][:, i * HEADS:(i + 1) * HEADS], qk_[par][:, m, a:a + P],
                                     blk[:, m, :], start=m == 0, stop=m == MK - 1)
                    ins.then_inc(logit_mm, 1)
                elif stage[0] == "R":
                    if c == 0:
                        pe.wait_ge(k16_dma, 32)
                    pe.wait_ge(attn_ready, c + 1)
                    if c == 2:
                        pe.wait_ge(x0_ready, EK)
                    for i, s in enumerate(sl):
                        a, cnt = slot_cols(s, c)
                        ins = nc.tensor.transpose(
                            bank[5][0:2 * HEADS, :].bitcast(F16)[:, a:a + cnt],
                            attn_hl[0:cnt, i].rearrange("p t h -> p (t h)"), k16[0:cnt, K_ID16:K_ID16 + cnt])
                    ins.then_inc(attn_T_mm, 1)
                    pe.wait_ge(attn_T_ready, c + 1)
                    for m in range(MK):
                        n = MK * c + m
                        if n >= 2:
                            pe.wait_ge(u_ready, n - 1)
                        if c and m == 0:
                            pe.wait_ge(wo_read, s0)
                        mm(bank[3 + m % 2][:, 0:w], k16[0:2 * HEADS, K_SPREAD + m * P:K_SPREAD + (m + 1) * P],
                           attn_T[:, 0:w], start=True, stop=True).then_inc(aB_mm, 1)
                elif stage[0] == "O":
                    if c == 0:
                        pe.wait_ge(ow_lo, 1)
                    pe.wait_ge(o_lo, c + 1)
                    pe.wait_ge(u_ready, MK * (c + 1))
                    for s in sl:
                        if s >= 2:
                            pe.wait_ge(wo_read, s - 1)
                        a, _ = slot_cols(s, c)
                        cut_products(bank[3 + s % 2][:, 0:E],
                                     [((oTh[:, m, a:a + P], oTl[:, m, a:a + P]),
                                       (owh[:, m * E:(m + 1) * E], owl[:, m * E:(m + 1) * E]))
                                      for m in range(MK)]).then_inc(wo_mm, 1)
                elif stage[0] == "G":
                    for k in range(EK):
                        if c:
                            pe.wait_ge(y2T_ready, EK * c)
                        else:
                            pe.wait_ge(yT_lo, EK * NCH)
                        for s in sl:
                            pe.wait_ge(y2_ready, s + 1)
                            a, n = slot_cols(s, c)
                            ins = nc.tensor.transpose(bank[6 + k][:, a:a + n], Y[0:n, s, k * P:(k + 1) * P],
                                                      ident[0:n, 0:n])
                        ins.then_inc(y2T_mm, 1)
                    pe.wait_ge(y2T_ready, EK * (c + 1))
                    pe.wait_ge(attn_T_ready, sum(x[0] == "R" for x in ORDER[:ORDER.index(stage)]))
                    if c:
                        pe.wait_ge(x0_ready, EK * sum(x[0] == "X" for x in ORDER[:ORDER.index(stage)]))
                    for i, s in enumerate(sl):
                        a, _ = slot_cols(s, c)
                        for k in range(EK):
                            ins = mm(bank[5][:, i * NEXP:(i + 1) * NEXP], y2T[:, k, col0(c) + a:col0(c) + a + P],
                                     wg[:, k, :], start=k == 0, stop=k == EK - 1)
                    ins.then_inc(gate_mm, 1)
                elif stage[0] == "X":
                    pe.wait_ge(sc_ready, c + 1)
                    pe.wait_ge(attn_T_ready, sum(x[0] == "R" for x in ORDER[:ORDER.index(stage)]))
                    pe.wait_ge(logit_sub, sum(x[0] == "S" for x in ORDER[:ORDER.index(stage)]))
                    if c:
                        pe.wait_ge(x0_ready, EK * c)
                    for s in sl:
                        a, n = slot_cols(s, c)
                        ins = mm(bank[5][:, a:a + n], SC[:, s, 0:1].to_broadcast([P, P]), ident[:, 0:n],
                                 start=True, stop=True)
                    ins.then_inc(s0_mm, 1)

            def const(at_):
                return k16[:, at_:at_ + P]

            pe.wait_ge(qk_ready, MK * NCH)
            pe.wait_ge(v_read, MK * NCH)
            pe.wait_ge(wo_read, SLOTS)
            nc.tensor.transpose(bank[0][0:TILES * NEXP, 0:P], SC[:, 1:].rearrange("p s e -> p (s e)"), ident)
            nc.tensor.transpose(bank[1][0:NEXP, 0:NSP], SC[0:NSP, 0], ident[0:NSP, 0:NSP])
            for k in range(EK):
                ins = nc.tensor.transpose(bank[2][:, k * NSP:(k + 1) * NSP], H[0:NSP, 0, k * P:(k + 1) * P],
                                          ident[0:NSP, 0:NSP])
            ins.then_inc(raw_mm, 1)

            def beside(n):
                if n < ROUNDS:
                    pe.wait_ge(ge_ready, n + 1)
                    if n:
                        pe.wait_ge(flags_read, n)
                    for s in range(SLOTS):
                        ins = mm(bank[7][:, 0:NCAND * NEXP], const(K_ONES) if s else const(K_W32),
                                 ge[:, s].rearrange("p c e -> p (c e)"), start=s == 0, stop=s == SLOTS - 1)
                    ins.then_inc(count_mm, 1)
                if n == ROUNDS:
                    pe.wait_ge(tie_ready, 1)
                    pe.wait_ge(flags_read, ROUNDS)
                    for s in range(SLOTS):
                        mm(bank[7][:, 0:NEXP], const(K_ONES) if s else const(K_W32), gt[:, s], start=s == 0,
                           stop=s == SLOTS - 1)
                    rank = bank[7][:, 128:128 + TILES * NEXP]
                    mm(rank, const(K_EARLIER), esum[:].unsqueeze(1).to_broadcast([P, TILES, NEXP]), start=True,
                       stop=False)
                    for s in range(1, TILES):
                        mm(bank[7][:, 128 + s * NEXP:128 + TILES * NEXP], const(K_SAME),
                           eq[:, s:s + 1].to_broadcast([P, TILES - s, NEXP]), start=False, stop=False)
                    mm(rank, const(K_LOWER), eq[:, 1:].rearrange("p s e -> p (s e)"), start=False, stop=False)
                    mm(rank, const(K_SPEC), eq[:, 0:1].to_broadcast([P, TILES, NEXP]), start=False, stop=True
                       ).then_inc(rank_mm, 1)
                if n == 17:
                    pe.wait_ge(tie_ready, 2)
                    pe.wait_ge(rank_read, 1)
                    mm(bank[7][:, :], const(K_ONES), tri_e.rearrange("p b t e -> p (b t e)"), start=True,
                       stop=False)
                    mm(bank[7][:, :], const(K_ONES), sp_e.rearrange("p b t e -> p (b t e)"), start=False,
                       stop=True).then_inc(rank_sp_mm, 1)
                if n == 18:
                    pe.wait_ge(rank_sp_read, 1)
                    pe.wait_ge(sm_ready, 1)
                    nc.tensor.transpose(bank[7][0:TILES * NEXP, 0:P], SM[:].rearrange("p s e -> p (s e)"), ident)
                    mm(bank[7][:, P:P + 2 * NEXP], const(K_ONES), allow_sp[:].rearrange("p t e -> p (t e)"),
                       start=True, stop=True).then_inc(rows_mm, 1)

            def zero_sums():
                for b_ in range(5):
                    mm(bank[b_][:, :], zero16[:], k16[:, 0:BANK], start=True, stop=False,
                       skip_group_check=True)

            def down(e, par, c):
                static = isinstance(e, int)
                j = e * NCH + c
                pe.wait_ge(h_lo, (j + 1) * HK)
                pe.wait_ge(h_hi, (j + 1) * HK)
                if c == 0:
                    pe.wait_ge(ew_lo, (e + 1) * 6)
                if static and e < RAW and c == 0:
                    if e == 0:
                        pe.wait_ge(raw_ready, 2)
                        pe.wait_ge(h2sp_ready, 1)
                    else:
                        pe.wait_ge(sums_read, e * (TILES + 1))
                    zero_sums()
                jb = (par + c) % 2
                off = NSP if c == 0 else 0
                for i in range(TPC):
                    tile = TPC * c + i
                    a = off + i * P
                    ins = cut_products(bank[tile // 2][:, (tile % 2) * E:][:, 0:E],
                                       [((Hh[:, jb, m, a:a + P], Hl[:, jb, m, a:a + P]),
                                         (w2_of(wh, par, m), w2_of(wl, par, m))) for m in range(HK)], start=False,
                                       stop=False)
                if c == 0:
                    for k in range(EK):
                        o = E + k * NEXP * NSP
                        dst = (bank[4][:, o + e * NSP:o + (e + 1) * NSP] if static
                               else bank[4][:, bass.ds(e * NSP + o, NSP)])
                        ins = cut_products(dst, [((w2_of(wh, par, m)[:, k * P:(k + 1) * P],
                                                   w2_of(wl, par, m)[:, k * P:(k + 1) * P]),
                                                  (Hh[:, jb, m, 0:NSP], Hl[:, jb, m, 0:NSP]))
                                                 for m in range(HK)], start=False, stop=False)
                ins.then_inc(dn_mm, 1)

            def unit(e, par, c):
                static = isinstance(e, int)
                w, j, a = width(c), e * NCH + c, col0(c)
                if c == 0:
                    pe.wait_ge(ew_lo, e * 6 + 4)
                    if not (static and e == 0):
                        pe.wait_ge(xs_lo, (e + 1) * (NCH * EK))
                if static and e == 0:
                    pe.wait_ge(xs_lo, EK * (c + 1))
                    if c == 0:
                        pe.wait_ge(x0_ready, EK * NCH)
                if static and (e, c) == (2, 0):
                    pe.wait_ge(bank7_free, 1)
                for m in range(HK):
                    n, i = j * HK + m, c * HK + m
                    for which, done in ((0, g_mm), (1, u_mm)):
                        if static and e < 2:
                            if n:
                                pe.wait_ge((silu_ready, t_ready)[which], n)
                        elif static and (e, n) == (2, 24):
                            pe.wait_ge((silu_ready, t_ready)[which], n)
                        elif which == 0:
                            pe.wait_ge(t_ready, n - 1)
                        else:
                            pe.wait_ge(silu_ready, n)
                        cut_products(hidden_bank(static, e, i, which)[:, 0:w],
                                     [((w13_of(wh, par, which, k, m), w13_of(wl, par, which, k, m)),
                                       (xh[par][:, k, a:a + w], xl[par][:, k, a:a + w])) for k in range(EK)]
                                     ).then_inc(done, 1)
                    if static:
                        beside(n)
                if not (static and e == 0 and c == 0):
                    if c:
                        down(e, par, c - 1)
                    else:
                        down(e - 1, 1 - par, NCH - 1)
                if static and (e, c) == (RAW, 0):
                    pe.wait_ge(sums_read, RAW * (TILES + 1))
                    zero_sums()

            units(unit, pe.Fori)
            down(NEXP - 1, (NEXP - 1) % 2, NCH - 1)


def shape_constants():
    import numpy as np
    p = np.arange(P)
    j, b = p // B, p % B
    k16 = np.zeros((P, K16), np.float16)
    k16[:, K_ONES:K_ONES + P] = 1
    k16[0:2, K_W32:K_W32 + P] = B
    k16[:, K_EARLIER:K_EARLIER + P] = b[:, None] < b[None, :]
    same = b[:, None] == b[None, :]
    k16[:, K_SAME:K_SAME + P] = same
    k16[:, K_LOWER:K_LOWER + P] = same & (j[:, None] < j[None, :])
    k16[0:2, K_SPEC:K_SPEC + P] = b[None, :] + 1
    k16[:, K_TRI:K_TRI + B] = b[:, None] < np.arange(B)[None, :]
    coef = np.zeros((P, B, 2))
    coef[0] = np.arange(B)[:, None] + np.arange(2)[None, :]
    coef[1] = np.arange(B)[:, None]
    k16[:, K_COEF:K_COEF + 2 * B] = coef.reshape(P, -1)
    k16[:, K_ID16:K_ID16 + P] = np.eye(P)
    spread = np.arange(INNER)[None, :] // HDIM == (np.arange(2 * HEADS) % HEADS)[:, None]
    k16[0:2 * HEADS, K_SPREAD:] = spread
    k16[0, K_SPSEL] = k16[1, K_SPSEL + 1] = 1
    k32 = np.zeros((P, K32), np.float32)
    k32[:, K_IDENT:K_IDENT + P] = np.eye(P)
    for m in range(MK):
        for h in range(HEADS):
            k32[:, K_BLK + m * HEADS + h] = (P * m + p) // HDIM == h
    step = 2 * (ROUNDS - 1 - np.arange(ROUNDS))
    cand = np.tile(((np.arange(NCAND) + 1)[None, :] << step[:, None])[None], (P, 1, 1)).astype(np.int32)
    return k16, k32, cand


def kernel(x, cls_tok, L0_tok_W, L0_tok_b, L0_tok_cls_token, L0_tok_pos_embedding, L0_tok_gamma, L0_tok_beta,
           L0_attn_Wq, L0_attn_bq, L0_attn_Wk, L0_attn_bk, L0_attn_Wv, L0_attn_bv, L0_attn_Wo, L0_attn_bo,
           L0_attn_alpha, L0_attn_aug_param, L0_attn_ln_scale, L0_attn_ln_bias, L0_ffn_wg, L0_ffn_w1, L0_ffn_w3,
           L0_ffn_w2):
    import numpy as np
    import concourse.bacc as bacc
    from concourse.bass_utils import run_bass_kernel_spmd

    def rows(w, k):
        w = np.asarray(w)
        return w.reshape(k, P, -1).transpose(1, 0, 2)

    def channels(*vs):
        return np.stack([np.asarray(v).reshape(MK, P).T for v in vs], 1)

    g = SIDE // PATCH
    px = np.asarray(x).reshape(B, C, g, PATCH, g, PATCH).transpose(1, 3, 5, 2, 4, 0).reshape(D, T)
    k16, k32, cand = shape_constants()
    w1 = np.stack([rows(w, EK) for w in np.asarray(L0_ffn_w1)])
    w3 = np.stack([rows(w, EK) for w in np.asarray(L0_ffn_w3)])
    w2 = np.stack([rows(w, HK) for w in np.asarray(L0_ffn_w2)])
    chan = channels(L0_attn_bq, L0_attn_bk, L0_attn_bv, L0_attn_alpha, L0_attn_aug_param).reshape(P, -1)
    k32[:, K_CHAN:K_WG] = chan
    k32[:, K_WG:] = rows(L0_ffn_wg, EK).reshape(P, -1)
    ins = dict(
        xT=px.reshape(DK, P, NCH, CW).transpose(1, 2, 0, 3), cls_tok=np.asarray(cls_tok).reshape(1, E),
        tok_w=rows(L0_tok_W, DK).reshape(P, -1), cls_token=np.asarray(L0_tok_cls_token).reshape(1, E),
        pos=np.asarray(L0_tok_pos_embedding)[0],
        vectors=np.concatenate([np.asarray(v) for v in (L0_tok_b, L0_tok_gamma, L0_tok_beta, L0_attn_bo,
                                                        L0_attn_ln_scale, L0_attn_ln_bias)]).reshape(1, -1),
        small=k32, wqkv=np.stack([rows(w, EK) for w in (L0_attn_Wq, L0_attn_Wk, L0_attn_Wv)], 1).reshape(P, -1),
        wo=rows(L0_attn_Wo, MK).reshape(P, -1), w13=np.stack([w1, w3], 2).reshape(NEXP, P, 2 * EK * HID),
        w2=w2.reshape(NEXP, P, HK * E), k16_in=k16, cand_in=cand)
    nc = bacc.Bacc("TRN2", target_bir_lowering=False, num_devices=1)
    arrays, args = {}, {}
    for name, a in ins.items():
        a = np.ascontiguousarray(a)
        arrays[name] = a
        args[name] = nc.dram_tensor(name, a.shape, mybir.dt.from_np(a.dtype), kind="ExternalInput").ap()
    args["out_patch"] = nc.dram_tensor("out_patch", (P, TILES, E), F32, kind="ExternalOutput").ap()
    args["out_spec"] = nc.dram_tensor("out_spec", (P, EK, NSP, B), F32, kind="ExternalOutput").ap()
    vit_tower(nc, **args)
    r = run_bass_kernel_spmd(nc, [arrays], core_ids=[0]).results[0]
    out = np.empty((B, S, E), np.float32)
    out[:, NSP:] = np.asarray(r["out_patch"]).transpose(1, 0, 2).reshape(NPATCH, B, E).transpose(1, 0, 2)
    out[:, :NSP] = np.asarray(r["out_spec"]).transpose(3, 2, 1, 0).reshape(B, NSP, E)
    return out
```

```python
from contextlib import ExitStack

import concourse.bass as bass
from concourse import mybir

F32 = mybir.dt.float32
F16 = mybir.dt.float16
I32 = mybir.dt.int32
ALU = mybir.AluOpType
ACT = mybir.ActivationFunctionType
AX = mybir.AxisListType.X

P = 128
B = 32
C, SIDE, PATCH = 3, 96, 16
NPATCH = (SIDE // PATCH) ** 2
T = B * NPATCH
NSP = 2
S = NPATCH + NSP
E = 256
EK = E // P
D = C * PATCH * PATCH
DK = D // P
HEADS, HDIM = 8, 64
INNER = HEADS * HDIM
MK = INNER // P
NEXP = 8
HID = 512
HK = HID // P
CAP = 1024

TILES = T // P
SLOTS = TILES + 1
NCH = 3
TPC = TILES // NCH
CW = TPC * P
TC = NPATCH // NCH
COLS = NSP + T
SEG = TC + 1
BANK = 512

SX, SW, SY, SO, SXS, ST_ = 64.0, 256.0, 256.0, 64.0, 1024.0, 16.0
SA = 4096.0
SR = 128.0
TIE_BIG = 2048.0
BITS = 3
ROUNDS = 30 // BITS
NCAND = 2 ** BITS - 1
RAW = 2
LOOPED = 4

K_ONES, K_W32, K_EARLIER, K_SAME, K_LOWER, K_SPEC = (i * P for i in range(6))
K_TRI = 6 * P
K_COEF = K_TRI + B
K_SPSEL = K_COEF + 2 * B
K_ID16 = K_SPSEL + 2
K_SPREAD = K_ID16 + P
K16 = K_SPREAD + INNER
R_BIAS, R_CLS, R_POS0, R_BO = (NPATCH + i for i in range(4))
RROWS = NPATCH + 4
K_IDENT = 0
K_BLK = K_IDENT + P
K_CHAN = K_BLK + MK * HEADS
K_WG = K_CHAN + 5 * MK
K32 = K_WG + EK * NEXP
V_GAMMA, V_BETA, V_LNS, V_LNB = (i * E for i in range(4))


def slots_of(c):
    return list(range(0 if c == 0 else 1 + TPC * c, 1 + TPC * (c + 1)))


def col0(c):
    return 0 if c == 0 else NSP + CW * c


def width(c):
    return CW + (NSP if c == 0 else 0)


def slot_cols(s, c):
    if s == 0:
        return 0, NSP
    return (NSP if c == 0 else 0) + (s - 1 - TPC * c) * P, P


def vit_tower(nc, xT, cls_tok, tok_w, added, selectors, vectors, small, wqkv, wo, w13, w2, k16_in, cand_in,
              out_patch, out_spec):
    with ExitStack() as ctx:
        def sb(name, shape, dt=F32):
            return ctx.enter_context(nc.sbuf_tensor(name, shape, dt))

        def sem(name):
            return ctx.enter_context(nc.semaphore(name))

        bank = [ctx.enter_context(nc.psum_tensor(f"bank{i}", [P, BANK], F32)) for i in range(8)]
        raw_rows = nc.dram_tensor("raw_rows", (NEXP, T), F32, kind="Internal").ap()
        raw_rows_sp = nc.dram_tensor("raw_rows_sp", (NEXP, NSP), F32, kind="Internal").ap()
        score_rows = nc.dram_tensor("score_rows", (NEXP, T), F32, kind="Internal").ap()

        k16 = sb("k16", [P, K16], F16)
        k32 = sb("k32", [P, K32])
        cand = sb("cand", [P, ROUNDS, NCAND], I32)
        ident = k32[:, K_IDENT:K_IDENT + P]
        blk = k32[:, K_BLK:K_BLK + MK * HEADS].rearrange("p (m h) -> p m h", m=MK)
        bq, bk, bv, alpha, aug = (k32[:, K_CHAN + i * MK:K_CHAN + (i + 1) * MK] for i in range(5))
        wg = k32[:, K_WG:K_WG + EK * NEXP].rearrange("p (k e) -> p k e", k=EK)
        vec = sb("vec", [P, 4 * E])
        gam, bet, lns, lnb = (vec[:, v:v + E] for v in (V_GAMMA, V_BETA, V_LNS, V_LNB))
        bk_s, v_scale, v_bias, decay, aug_h, ez = (sb(n, [P, MK]) for n in
                                                   ("bk_s", "v_scale", "v_bias", "decay", "aug_h", "ez"))
        half32 = sb("half32", [P, 1])
        minus_half = sb("minus_half", [P, 4])
        zero16 = sb("zero16", [P, P], F16)
        cls_sb = sb("cls_sb", [1, E])
        add_rows = sb("add_rows", [RROWS, E])
        bo_selector = sb("bo_selector", [RROWS, P], F16)
        add_hi, add_lo = sb("add_hi", [RROWS, E], F16), sb("add_lo", [RROWS, E], F16)

        WMAX = CW + NSP

        wst = sb("wst", [P, 2, 3 * EK * HID])
        wh = sb("wh", [P, 2, 3 * EK * HID], F16)
        wl = sb("wl", [P, 2, 3 * EK * HID], F16)
        staged = wst[:].rearrange("p a n -> p (a n)")
        n_tw, n_qw, n_ow = DK * E, 3 * EK * INNER, MK * E
        tw = staged[:, 0:n_tw]
        qw = staged[:, n_tw:n_tw + n_qw]
        ow = staged[:, n_tw + n_qw:n_tw + n_qw + n_ow]
        def region(name, words):
            t, place = sb(name, [P, words]), [0]

            def at(shape, dt=F32, start=None):
                if start is not None:
                    place[0] = start
                n = 1
                for x in shape:
                    n *= x
                w = n if dt != F16 else (n + 1) // 2
                v = t[:, place[0]:place[0] + w]
                place[0] += w
                assert place[0] <= words, (name, place[0])
                if dt == F16:
                    v = v.bitcast(F16)
                if len(shape) == 1:
                    return v
                names = [f"a{i}" for i in range(len(shape))]
                return v.rearrange(f"p ({' '.join(names)}) -> p {' '.join(names)}",
                                   **{a: x for a, x in zip(names[1:], shape[1:])})
            return at

        at = region("front_weights", n_tw + n_qw + n_ow)
        twh, twl = at([n_tw], F16), at([n_tw], F16)
        qwh, qwl = at([n_qw], F16), at([n_qw], F16)
        owh, owl = at([n_ow], F16), at([n_ow], F16)
        Hh, Hl = at([2, HK, WMAX], F16, start=0), at([2, HK, WMAX], F16)
        rows = at([2, P])
        tri_e, sp_e = at([B, 2, NEXP], F16), at([B, 2, NEXP], F16)
        rank_sp = at([B, 2, NEXP])
        msp = at([B, 2, NEXP])
        ysp = at([EK, NEXP, NSP])

        def w13_of(w, par, which, k, m):
            o = (which * EK + k) * HID + m * P
            return w[:, par, o:o + P]

        def w2_of(w, par, m):
            o = 2 * EK * HID + m * E
            return w[:, par, o:o + E]

        def qkv_of(w, which, k, m):
            o = (which * EK + k) * INNER + m * P
            return w[:, o:o + P]

        H = sb("H", [P, SLOTS, E])
        Y = sb("Y", [P, SLOTS, E])
        y2T = sb("y2T", [P, EK, COLS])

        at = region("front", 16200)
        px = at([NCH, DK, CW])
        pxh, pxl = at([NCH, DK, CW], F16), at([NCH, DK, CW], F16)
        yTh, yTl = at([EK, WMAX], F16), at([EK, WMAX], F16)
        oTh, oTl = at([MK, WMAX], F16), at([MK, WMAX], F16)
        q0 = at([4, MK, WMAX], start=0)
        U, STt, DEC = (at([MK * B * SEG], start=NCH * DK * CW + i * MK * B * SEG) for i in range(3))
        Us, STs, DECs = (t.rearrange("p (m b t) -> p m b t", m=MK, b=B) for t in (U, STt, DEC))
        sB = at([2, COLS], start=0)
        OUT = at([TILES, E])
        xh1, xl1 = at([EK, COLS], F16), at([EK, COLS], F16)

        at = region("odd_chunk", 4 * MK * WMAX)
        selector = at([SLOTS * P], F16)
        q1 = at([4, MK, WMAX], start=0)
        X32 = at([EK, COLS], start=0)
        xh0, xl0 = at([EK, COLS], F16), at([EK, COLS], F16)
        sg, Tt = at([2, WMAX]), at([2, WMAX])
        prod = at([EK * NSP, B, NEXP], start=0)
        osum, osp = at([EK, NSP, B]), at([EK, NSP, B])
        q_, qk_, vp_, th_ = ([t[:, i] for t in (q0, q1)] for i in range(4))
        xh, xl = [xh0, xh1], [xl0, xl1]

        stats = sb("stats", [P, 4, 6])
        mean = [[sb(f"mean{k}{c}", [P, 4, 2]) for c in range(NCH)] for k in range(4)]
        rstd = [[sb(f"rstd{k}{c}", [P, 4]) for c in range(NCH)] for k in range(4)]
        shift = [[sb(f"shift{k}{c}", [P, 4]) for c in range(NCH)] for k in range(4)]
        var_eps = sb("var_eps", [P, 4])
        mx = sb("mx", [P, 4])
        dd = sb("dd", [P, 4, HEADS])
        ex = sb("ex", [P, 4, HEADS])
        sm = sb("sm", [P, 4])
        attn = sb("attn", [P, 4, HEADS])
        attn_hl = sb("attn_hl", [P, 4, 2, HEADS], F16)
        logits_T = sb("logits_T", [HEADS, WMAX])
        attn_T = sb("attn_T", [2 * HEADS, WMAX], F16)
        us2 = sb("us2", [P, MK, NSP])
        sp_state = sb("sp_state", [P, MK, NSP])
        sp_tmp = sb("sp_tmp", [P, MK])
        SC = sb("SC", [P, SLOTS, NEXP])
        SM = sb("SM", [P, TILES, NEXP])
        lo = sb("lo", [P, NEXP], I32)
        mid = sb("mid", [P, NCAND, NEXP], I32)
        ahead_of = sb("ahead_of", [P, NCAND, NEXP], I32)
        ge = sb("ge", [P, SLOTS, NCAND, NEXP], F16)
        fl = sb("fl", [P, NCAND, NEXP])
        inc = sb("inc", [P, NEXP], I32)
        gt = sb("gt", [P, SLOTS, NEXP], F16)
        eq = sb("eq", [P, SLOTS, NEXP], F16)
        esum = sb("esum", [P, NEXP], F16)
        room = sb("room", [P, NEXP])
        allow = sb("allow", [P, SLOTS, NEXP])
        allow_sp = sb("allow_sp", [P, 2, NEXP], F16)
        asp = sb("asp", [P, 2, NEXP])
        keep = sb("keep", [P, TILES, NEXP])
        keep_s = sb("keep_s", [P, RAW, TILES])
        rows_sp = sb("rows_sp", [NEXP, NSP])
        h2sp = sb("h2sp", [P, EK, NSP])

        px_in = [sem(f"px_in{c}") for c in range(NCH)]
        px_first_in = sem("px_first_in")
        tokw_in, added_in, selectors_in, cls_in, vec_in, k16_dma, small_in = (sem(n) for n in (
            "tokw_in", "added_in", "selectors_in", "cls_in", "vec_in", "k16_dma", "small_in"))
        qw_in, ow_in = sem("qw_in"), sem("ow_in")
        ew_in = [sem("ew_in0"), sem("ew_in1")]
        sB_in = [sem("sB_in0"), sem("sB_in1")]
        rows_out, out_done = sem("rows_out"), sem("out_done")
        bo_selector_in, sp_tie_ready = sem("bo_selector_in"), sem("sp_tie_ready")
        filled, added_hi, added_lo = sem("filled"), sem("added_hi"), sem("added_lo")
        logits_T_mm, logits_T_ready = sem("logits_T_mm"), sem("logits_T_ready")
        tokw_hi, qw_hi, ow_hi = sem("tokw_hi"), sem("qw_hi"), sem("ow_hi")
        kw_lo, vw_lo = sem("kw_lo"), sem("vw_lo")
        w_scaled, ew_scaled = sem("w_scaled"), sem("ew_scaled")
        tokw_lo, qw_lo, ow_lo = sem("tokw_lo"), sem("qw_lo"), sem("ow_lo")
        px_hi, px_lo = sem("px_hi"), sem("px_lo")
        dve_step, act_step, pool_step = sem("dve_step"), sem("act_step"), sem("pool_step")
        tok_mm, tok_read = sem("tok_mm"), sem("tok_read")
        mean_ready, rstd_ready = sem("mean_ready"), sem("rstd_ready")
        h_ready, y_ready, bias_in = sem("h_ready"), sem("y_ready"), sem("bias_in")
        yT_mm, yT_hi, yT_lo = sem("yT_mm"), sem("yT_hi"), sem("yT_lo")
        q_mm, k_mm, v_mm = sem("q_mm"), sem("k_mm"), sem("v_mm")
        q_read, qk_ready, v_read = sem("q_read"), sem("qk_ready"), sem("v_read")
        chan_ready, chan_e = sem("chan_ready"), sem("chan_e")
        logit_mm, logit_sub, exp_ready, attn_ready = (sem("logit_mm"), sem("logit_sub"), sem("exp_ready"),
                                                      sem("attn_ready"))
        attn_T_mm, attn_T_ready = sem("attn_T_mm"), sem("attn_T_ready")
        aB_mm, u_ready = sem("aB_mm"), sem("u_ready")
        th_ready, sig_ready, qs_ready = sem("th_ready"), sem("sig_ready"), sem("qs_ready")
        o_odd = sem("o_odd")
        o_ready, o_hi, o_lo = sem("o_ready"), sem("o_hi"), sem("o_lo")
        wo_mm, wo_read = sem("wo_mm"), sem("wo_read")
        h2_ready, y2_ready, y2T_mm, y2T_ready = sem("h2_ready"), sem("y2_ready"), sem("y2T_mm"), sem("y2T_ready")
        gate_mm, gate_sub, gexp_ready, sc_ready = (sem("gate_mm"), sem("gate_sub"), sem("gexp_ready"),
                                                   sem("sc_ready"))
        s0_mm, raw_mm, raw_ready = sem("s0_mm"), sem("raw_mm"), sem("raw_ready")
        x0_ready, h2sp_ready = sem("x0_ready"), sem("h2sp_ready")
        ge_ready, count_mm, flags_read = sem("ge_ready"), sem("count_mm"), sem("flags_read")
        tie_ready, rank_mm, rank_read, rank_sp_mm, rank_sp_read = (sem(n) for n in (
            "tie_ready", "rank_mm", "rank_read", "rank_sp_mm", "rank_sp_read"))
        sm_ready, rows_mm, rows_ready, asp_ready = (sem("sm_ready"), sem("rows_mm"), sem("rows_ready"),
                                                     sem("asp_ready"))
        ew_hi, ew_lo = sem("ew_hi"), sem("ew_lo")
        xs_ready, xs_hi, xs_lo = sem("xs_ready"), sem("xs_hi"), sem("xs_lo")
        g_mm, u_mm, silu_ready, t_ready = sem("g_mm"), sem("u_mm"), sem("silu_ready"), sem("t_ready")
        h_hi, h_lo, dn_mm, sums_read = sem("h_hi"), sem("h_lo"), sem("dn_mm"), sem("sums_read")
        out_ready, osp_ready = sem("out_ready"), sem("osp_ready")

        block = ctx.enter_context(nc.Block())

        class Steps:

            def __init__(self, eng, s):
                self.eng, self.s, self.n = eng, s, 0

            def did(self, ins):
                self.n += 1
                ins.then_inc(self.s, 1)

            def wait(self):
                self.eng.wait_ge(self.s, self.n)

            def then(self, ins):
                self.did(ins)
                self.wait()

        PE_ORDER = """A0 W1 A1 B0 T0 W2 W0 Q00 A2 Q01 B1 Q02 Q03 T1 S0 L0 Q10 W3 B2 Q11 R0 V0 T2 Q12 P0
                   Q13 S1 L1 O0 Q20 Q21 R1 V1 Q22 N0 G0 K0 Q23 M0 P1 O1 S2 L2 X0 N1 G1 R2 V2 H00 H01 K1
                   P2 M1 H02 X1 O2 N2 H03 H10 D0 H11 G2 H12 K2 M2 X2 H13""".split()
        ACT_ORDER = """A0 W1 W0 A1 B0 W2 T0 Q00 Q01 A2 B1 Q02 Q03 T1 S0 W3 L0 Q10 Q11 R0 B2 Q12 P0 Q13 T2
                    S1 L1 Q20 R1 Q21 O0 N0 Q22 P1 G0 Q23 S2 O1 L2 N1 X0 R2 H00 H01 G1 P2 H02 X1 H03 D0
                    O2 H10 N2 H11 G2 H12 X2 H13""".split()
        DVE_ORDER = """A0 U1 U2 W0 B0 C0 W2 A1 W1 T0 B1 C1 Q00 A2 U3 W3 Q01 Q02 Q03 T1 S0 L0 Q10 B2 C2 Q11
                    R0 V0 Y0 Q12 Q13 P0 T2 S1 L1 O0 Q20 N0 Z0 Q21 R1 V1 Y1 Q22 P1 G0 Q23 S2 O1 N1 Z1 L2
                    X0 R2 V2 Y2 H00 H01 G1 P2 H02 X1 O2 H03 N2 Z2 H10 H11 D0 G2 H12 X2 H13""".split()
        HIGH_AT = "Q10 Q21".split()
        WEIGHTS_AT = "T2 S1 L1 O0 Q20 G0".split()
        NEXT_WEIGHTS_AT = "Z1 R2 H01 P2 H10 D0".split()
        NORMS = [({"A": 0, "C": 1, "O": 2, "Z": 3}[x[0]], int(x[1])) for x in DVE_ORDER if x[0] in "ACOZ"]

        def norm_count(which, c):
            return NORMS.index((which, c)) + 1

        def before(stage, kinds):
            return sum(x[0] in kinds for x in PE_ORDER[:PE_ORDER.index(stage)])

        def slots_until(c):
            return slots_of(c)[-1] + 1

        def units(unit, loop):
            for j in range(2, NCH * RAW + 1):
                unit(j // NCH, j // NCH % 2, j % NCH)
            with loop(0, LOOPED // 2) as pair:
                for i in range(2):
                    e, par = pair * 2 + (RAW + i), (RAW + i) % 2
                    unit(e, par, 1)
                    unit(e, par, 2)
                    unit(e + 1, 1 - par, 0)
            for j in range(NCH * (RAW + LOOPED) + 1, NCH * NEXP):
                unit(j // NCH, j // NCH % 2, j % NCH)

        def rounds_at(n):
            return [r for r in (n - 2 * HK,) if 0 <= r < ROUNDS]

        def token_pieces(static, e, i):
            if static and e < RAW:
                pieces = {10: [(1, 0), (1, 1)], 11: [(1, 2), (1, 3)]}.get(i, [])
                return [(0, 4), (0, 5)] if (e, i) == (1, 0) else pieces
            if static and (e, i) == (2, 0):
                return [(0, 4), (0, 5)]
            if static and e == NEXP - 1:
                return []
            return [(1, i - 4)] if 4 <= i <= 9 else []

        def hidden_bank(static, e, i, which):
            if static and e == 0 and i < 2 * HK:
                return bank[(2, 6)[which]]
            if static and e < 2:
                return bank[5 + which]
            return bank[5 + (2 * i + which) % 3]

        TOK_PLACE = [(s // 2, s % 2) for s in range(SLOTS)]
        TOK_DONE = [max(s for s in range(SLOTS) if TOK_PLACE[s][0] == b_) + 1 for b_, _ in TOK_PLACE]

        def tok_out(s):
            b_, half = TOK_PLACE[s]
            return bank[b_][:, half * E:(half + 1) * E]

        def wo_out(i):
            return bank[3 + i // 2][:, (i % 2) * E:][:, 0:E]

        def sums(i):
            return bank[(i + 1) // 2][:, (i + 1) % 2 * E:][:, 0:E]

        @block.sync
        def _(sp):
            sp.dma_start(tw, tok_w).then_inc(tokw_in, 16)
            for c in range(NCH):
                if c:
                    sp.dma_start(px[:, c], xT[:, c]).then_inc(px_in[c], 16)
                else:
                    sp.dma_start(px[:, c, 0:DK // 2], xT[:, c, 0:DK // 2]).then_inc(px_first_in, 16)
                    sp.dma_start(px[:, c, DK // 2:], xT[:, c, DK // 2:]).then_inc(px_in[c], 16)
                    sp.dma_start(add_rows[:], added).then_inc(added_in, 16)
                    sp.dma_start(selector[0:RROWS], selectors[:, 0:SLOTS * P]).then_inc(selectors_in, 16)
                if c == 1:
                    sp.dma_start(vec[:], vectors.to_broadcast([P, 4 * E])).then_inc(vec_in, 16)
            sp.dma_start(qw, wqkv).then_inc(qw_in, 16)
            sp.dma_start(k32[:], small).then_inc(small_in, 16)
            sp.dma_start(ow, wo).then_inc(ow_in, 16)
            sp.dma_start(bo_selector[:], selectors[:, SLOTS * P:]).then_inc(bo_selector_in, 16)
            sp.dma_start(k16[:], k16_in).then_inc(k16_dma, 16)
            sp.dma_start(cand[:], cand_in).then_inc(k16_dma, 16)

            def load_expert(e, par):
                sp.dma_start(wst[:, par, 0:2 * EK * HID], w13[e]).then_inc(ew_in[par], 16)
                sp.dma_start(wst[:, par, 2 * EK * HID:], w2[e]).then_inc(ew_in[par], 16)

            for s in (tokw_lo, tokw_hi, ow_lo, ow_hi):
                sp.wait_ge(s, 1)
            for s in (qw_lo, kw_lo, vw_lo):
                sp.wait_ge(s, 1)
            load_expert(0, 0)
            load_expert(1, 1)
            sp.wait_ge(raw_ready, 2)
            sp.dma_start(raw_rows.rearrange("e (s n) -> s e n", n=P), rows[0:TILES * NEXP, 0, :]
                         ).then_inc(rows_out, 16)
            sp.dma_start(raw_rows_sp, rows_sp[:]).then_inc(rows_out, 16)
            sp.wait_ge(rows_out, 32)
            sp.dma_start(sB[:, 1, NSP:], raw_rows[1:2, :].to_broadcast([P, T])).then_inc(sB_in[1], 16)
            sp.dma_start(sB[:, 1, 0:NSP], raw_rows_sp[1:2, :].to_broadcast([P, NSP])).then_inc(sB_in[1], 16)

            def load_weights(e, par):
                sp.wait_ge(ew_lo, (e - 1) * 6)
                sp.dma_start(wst[:, par, 0:2 * EK * HID], w13[e]).then_inc(ew_in[par], 16)
                sp.dma_start(wst[:, par, 2 * EK * HID:], w2[e]).then_inc(ew_in[par], 16)

            load_weights(2, 0)
            sp.wait_ge(rows_ready, 1)
            sp.dma_start(score_rows.rearrange("e (s n) -> s e n", n=P), rows[0:TILES * NEXP, 1, :]
                         ).then_inc(rows_out, 16)
            sp.wait_ge(rows_out, 48)

            def load_scores(e, par):
                if not (isinstance(e, int) and e == 2):
                    sp.wait_ge(xs_ready, (e - 2) * NCH)
                sp.dma_start(sB[:, par, NSP:], score_rows[bass.ds(e, 1), :].to_broadcast([P, T])
                             ).then_inc(sB_in[par], 16)
                sp.dma_start(sB[:, par, 0:NSP], raw_rows_sp[bass.ds(e, 1), :].to_broadcast([P, NSP])
                             ).then_inc(sB_in[par], 16)

            load_scores(2, 0)
            load_weights(3, 1)
            load_scores(3, 1)
            with sp.Fori(2, NEXP // 2) as pair:
                for par in range(2):
                    e = pair * 2 + par
                    load_weights(e, par)
                    load_scores(e, par)
            for i in range(TILES // 3):
                sp.wait_ge(out_ready, 3 * (i + 1))
                sp.dma_start(out_patch[:, 3 * i:3 * i + 3], OUT[:, 3 * i:3 * i + 3]).then_inc(out_done, 16)
            sp.wait_ge(osp_ready, 1)
            sp.dma_start(out_spec, osp).then_inc(out_done, 16)
            sp.wait_ge(out_done, 16 * (1 + TILES // 3))

        def y2T_bank(c, k):
            return bank[7] if c else bank[6 + k]

        @block.gpsimd
        def _(pool):
            G = nc.gpsimd
            steps = Steps(pool, pool_step)
            pool.dma_start(cls_sb[:], cls_tok).then_inc(cls_in, 16)
            G.memset(lo[:], 0).then_inc(filled, 1)
            G.memset(half32[:], SO / 2).then_inc(filled, 1)
            G.memset(zero16[:], 0.0).then_inc(filled, 1)
            G.memset(minus_half[:], -0.5).then_inc(filled, 1)
            pool.wait_ge(filled, 4)
            pool.wait_ge(vec_in, 16)

            def norm(which, c):
                ns = len(slots_of(c))
                m, r, b = mean[which][c], rstd[which][c], shift[which][c]
                pool.wait_ge(mean_ready, norm_count(which, c))
                eps = (1e-5 * (SX * SW) ** 2, 1e-5, 1e-6 * (SO * SW) ** 2, 1e-5)[which]
                steps.then(G.tensor_scalar(var_eps[:, 0:ns], m[:, 0:ns, 1], eps, 0.0, ALU.add, ALU.add))
                ins = G.tensor_tensor(r[:, 0:ns], var_eps[:, 0:ns], minus_half[:, 0:ns], ALU.pow)
                if which % 2:
                    steps.then(ins)
                    steps.then(G.tensor_tensor(b[:, 0:ns], m[:, 0:ns, 0], r[:, 0:ns], ALU.mult))
                    ins = G.tensor_scalar(b[:, 0:ns], b[:, 0:ns], -1.0, 0.0, ALU.mult, ALU.add)
                ins.then_inc(rstd_ready, 1)

            def weights_hi(e, par):
                if isinstance(e, int):
                    pool.wait_ge(ew_in[par], 32 * (e // 2 + 1))
                else:
                    pool.wait_ge(ew_in[par], (e - par) * 16 + 32)
                    pool.sem_inc(pool_step, 1)
                G.tensor_scalar(wh[:, par], wst[:, par], SW, 0.0, ALU.mult, ALU.add).then_inc(ew_hi, 1)

            for stage in DVE_ORDER:
                c = int(stage[1])
                if stage[0] == "W":
                    continue
                if stage[0] == "U":
                    pool.wait_ge(w_scaled, c)
                    a = c * EK * INNER
                    if c < 3:
                        G.tensor_tensor(qwl[:, a:a + EK * INNER], qw[:, a:a + EK * INNER],
                                        qwh[:, a:a + EK * INNER], ALU.subtract).then_inc((kw_lo, vw_lo)[c - 1], 1)
                    else:
                        G.tensor_tensor(owl, ow, owh, ALU.subtract).then_inc(ow_lo, 1)
                    continue
                sl = slots_of(c)
                ns, s0, w = len(sl), sl[0], width(c)
                if stage[0] in "ACOZ":
                    norm({"A": 0, "C": 1, "O": 2, "Z": 3}[stage[0]], c)
                elif stage[0] == "T":
                    pool.wait_ge(y_ready, slots_until(c))
                    G.tensor_tensor(H[:, s0:s0 + ns, :], H[:, s0:s0 + ns, :],
                                    lnb.unsqueeze(1).to_broadcast([P, ns, E]), ALU.add).then_inc(bias_in, 1)
                elif stage[0] == "P":
                    pool.wait_ge(sig_ready, c + 1)
                    for m in range(0, MK, 2 if c == NCH - 1 else 1):
                        pool.wait_ge(qs_ready, MK * c + m + 1)
                        G.tensor_tensor(qk_[c % 2][:, m, 0:w], qk_[c % 2][:, m, 0:w], th_[c % 2][:, m, 0:w],
                                        ALU.add).then_inc(o_ready, 1)
                if stage in HIGH_AT:
                    weights_hi(HIGH_AT.index(stage), HIGH_AT.index(stage))
                for e, stages in ((0, WEIGHTS_AT), (1, NEXT_WEIGHTS_AT)):
                    if stage in stages:
                        i = stages.index(stage)
                        part = wst[:, e, i * HID:(i + 1) * HID]
                        pool.wait_ge(ew_hi, e + 1)
                        G.tensor_scalar(part, part, SW, 0.0, ALU.mult, ALU.add).then_inc(ew_scaled, 1)
                        pool.wait_ge(ew_scaled, 6 * e + i + 1)
                        G.tensor_tensor(wl[:, e, i * HID:(i + 1) * HID], part, wh[:, e, i * HID:(i + 1) * HID],
                                        ALU.subtract).then_inc(ew_lo, 1)

            def scaled_tokens(e, par):
                pool.wait_ge(sB_in[par], (32 * (e // 2) + (32 if par else 0)) if isinstance(e, int)
                             else (e - par) * 16 + (32 if par else 0))
                for c in range(NCH):
                    a, w = col0(c), width(c)
                    for k in range(EK):
                        ins = G.tensor_tensor(X32[:, k, a:a + w], y2T[:, k, a:a + w], sB[:, par, a:a + w],
                                              ALU.mult)
                    ins.then_inc(xs_ready, 1)

            def next_tokens(e, par):
                pool.wait_ge(xs_hi, e * (NCH * EK))
                pool.wait_ge(xs_lo, e * (NCH * EK))
                scaled_tokens(e, par)

            def next_weights(e, par):
                pool.wait_ge(dn_mm, (e - 1) * NCH)
                weights_hi(e, par)

            next_tokens(1, 1)
            next_weights(2, 0)
            pool.wait_ge(tie_ready, 1)
            tri = k16[:, K_TRI:K_TRI + B]
            coef = k16[:, K_COEF:K_COEF + 2 * B].rearrange("p (b t) -> p b t", t=2)
            for t in range(2):
                G.tensor_tensor(tri_e[:, :, t], tri.unsqueeze(2).to_broadcast([P, B, NEXP]),
                                esum[:].unsqueeze(1).to_broadcast([P, B, NEXP]), ALU.mult)
                ins = G.tensor_tensor(sp_e[:, :, t], coef[:, :, t:t + 1].to_broadcast([P, B, NEXP]),
                                      eq[:, 0:1].to_broadcast([P, B, NEXP]), ALU.mult)
            ins.then_inc(sp_tie_ready, 1)
            next_tokens(2, 0)
            next_tokens(3, 1)
            next_weights(3, 1)
            with pool.Fori(2, NEXP // 2) as pair:
                for par in range(2):
                    next_tokens(pair * 2 + par, par)
                    next_weights(pair * 2 + par, par)

        @block.scalar
        def _(act):
            A = nc.scalar
            act.wait_ge(tokw_in, 16)
            A.activation(twh, tw, ACT.Copy, scale=SW).then_inc(tokw_hi, 1)
            for c in range(NCH):
                for k in (0, DK // 2):
                    act.wait_ge(px_in[c] if c or k else px_first_in, 16)
                    A.activation(pxh[:, c, k:k + DK // 2], px[:, c, k:k + DK // 2], ACT.Copy, scale=SX
                                 ).then_inc(px_hi, 1)
                if c == 0:
                    act.wait_ge(added_in, 16)
                    A.activation(add_hi[:], add_rows[:], ACT.Copy, scale=SR).then_inc(added_hi, 1)
            act.wait_ge(qw_in, 16)
            for i in range(3):
                a = i * EK * INNER
                A.activation(qwh[:, a:a + EK * INNER], qw[:, a:a + EK * INNER], ACT.Copy, scale=SW
                             ).then_inc(qw_hi, 1)
                if i:
                    act.wait_ge(qw_hi, i + 1)
                    A.activation(qw[:, a:a + EK * INNER], qw[:, a:a + EK * INNER], ACT.Copy, scale=SW
                                 ).then_inc(w_scaled, 1)
            act.wait_ge(ow_in, 16)
            A.activation(owh, ow, ACT.Copy, scale=SW).then_inc(ow_hi, 1)
            act.wait_ge(ow_hi, 1)
            A.activation(ow, ow, ACT.Copy, scale=SW).then_inc(w_scaled, 1)
            act.wait_ge(small_in, 16)
            A.activation(ez[:], alpha, ACT.Tanh, scale=0.5).then_inc(chan_e, 1)
            act.wait_ge(filled, 4)

            def tokens_hi(par, piece):
                c, k = piece // EK, piece % EK
                a, w = col0(c), width(c)
                A.activation(xh[par][:, k, a:a + w], X32[:, k, a:a + w], ACT.Copy, scale=SXS).then_inc(xs_hi, 1)

            def hidden(e, par, c, m):
                static = isinstance(e, int)
                w, j = width(c), e * NCH + c
                n, i = j * HK + m, c * HK + m
                act.wait_ge(g_mm, n + 1)
                if not static or n >= 2:
                    act.wait_ge(t_ready, n - 1)
                A.activation(sg[:, m % 2, 0:w], hidden_bank(static, e, i, 0)[:, 0:w], ACT.Silu,
                             scale=1.0 / (SXS * SW)).then_inc(silu_ready, 1)
                for ahead, piece in token_pieces(static, e, i):
                    act.wait_ge(xs_ready, (e - 1 + ahead) * NCH + piece // EK + 1)
                    if piece == 0 and not (static and e == 0):
                        act.wait_ge(u_mm, e * (NCH * HK))
                    tokens_hi(1 - par if ahead else par, piece)
                act.wait_ge(t_ready, n + 1)
                if not static or j >= 2:
                    act.wait_ge(dn_mm, j - 1)
                A.activation(Hh[:, (par + c) % 2, m, 0:w], Tt[:, m % 2, 0:w], ACT.Copy).then_inc(h_hi, 1)
                if static and n == 19:
                    act.wait_ge(rows_mm, 1)
                    A.activation(rows[0:TILES * NEXP, 1, :], bank[7][0:TILES * NEXP, 0:P], ACT.Copy
                                 ).then_inc(rows_ready, 1)
                    A.activation(asp[:], bank[7][:, P:P + 2 * NEXP].rearrange("p (t e) -> p t e", e=NEXP),
                                 ACT.Copy).then_inc(asp_ready, 1)

            for stage in ACT_ORDER:
                c, par = int(stage[1]), int(stage[1]) % 2
                w, sl = width(c), slots_of(min(c, NCH - 1))
                ns, s0 = len(sl), sl[0]
                q, vp, th = q_[par], vp_[par], th_[par]
                if stage[0] in "BN":
                    which, done = (1, y_ready) if stage[0] == "B" else (3, y2_ready)
                    act.wait_ge(rstd_ready, norm_count(which, c))
                    for i, s in enumerate(sl):
                        A.activation(Y[:, s, :], H[:, s, :], ACT.Identity, bias=shift[which][c][:, i:i + 1],
                                     scale=rstd[which][c][:, i:i + 1]).then_inc(done, 1)
                elif stage[0] == "T":
                    for k in range(EK):
                        act.wait_ge(yT_mm, EK * c + k + 1)
                        if c:
                            act.wait_ge(v_mm, MK * c)
                        A.activation(yTh[:, k, 0:w], bank[6 + k][:, 0:w], ACT.Copy, scale=SY).then_inc(yT_hi, 1)
                elif stage[0] == "Q":
                    m = int(stage[2])
                    n = MK * c + m
                    if n == 0:
                        act.wait_ge(chan_ready, 1)
                        act.wait_ge(tok_mm, SLOTS)
                        act.wait_ge(px_lo, 2 * NCH)
                        act.wait_ge(px_hi, 2 * NCH)
                    act.wait_ge(q_mm, n + 1)
                    if c == 2 and m == 0:
                        act.wait_ge(o_lo, 1)
                    A.activation(q[:, m, 0:w], bank[0][:, 0:w], ACT.Identity, bias=bq[:, m:m + 1],
                                 scale=1.0 / (SY * SW)).then_inc(q_read, 1)
                    act.wait_ge(v_mm, n + 1)
                    A.activation(vp[:, m, 0:w], bank[2][:, 0:w], ACT.Identity, bias=v_bias[:, m:m + 1],
                                 scale=v_scale[:, m:m + 1]).then_inc(v_read, 1)
                    act.wait_ge(q_read, n + 1)
                    A.activation(th[:, m, 0:w], q[:, m, 0:w], ACT.Tanh, scale=aug_h[:, m:m + 1]
                                 ).then_inc(th_ready, 1)
                    if m == MK - 1:
                        act.wait_ge(th_ready, n + 1)
                        A.activation(th[:, :, 0:w], th[:, :, 0:w], ACT.Identity, bias=half32[:], scale=SO / 2
                                     ).then_inc(sig_ready, 1)
                elif stage[0] == "S":
                    act.wait_ge(logits_T_mm, c + 1)
                    if c:
                        act.wait_ge(logit_mm, c)
                    A.activation(logits_T[:, 0:w], bank[5][0:HEADS, 0:w], ACT.Copy).then_inc(logits_T_ready, 1)
                elif stage[0] == "L":
                    act.wait_ge(logit_sub, c + 1)
                    A.activation(ex[:, 0:ns], dd[:, 0:ns], ACT.Exp, scale=HDIM ** -0.5 / (SY * SW)
                                 ).then_inc(exp_ready, 1)
                elif stage[0] == "R":
                    act.wait_ge(attn_T_mm, c + 1)
                    if c:
                        act.wait_ge(aB_mm, MK * c)
                    A.activation(attn_T[:, 0:w], bank[5][0:2 * HEADS, :].bitcast(F16)[:, 0:w], ACT.Copy
                                 ).then_inc(attn_T_ready, 1)
                elif stage[0] == "P":
                    if c:
                        act.wait_ge(wo_mm, s0)
                    for m in range(MK):
                        if c < NCH - 1:
                            act.wait_ge(o_ready, MK * c + m + 1)
                        elif m % 2:
                            act.wait_ge(o_odd, m // 2 + 1)
                        else:
                            act.wait_ge(o_ready, MK * c + m // 2 + 1)
                        A.activation(oTh[:, m, 0:w], qk_[par][:, m, 0:w], ACT.Copy).then_inc(o_hi, 1)
                elif stage[0] == "G":
                    for k in range(EK):
                        act.wait_ge(y2T_mm, EK * c + k + 1)
                        A.activation(y2T[:, k, col0(c):col0(c) + w], y2T_bank(c, k)[:, 0:w], ACT.Copy
                                     ).then_inc(y2T_ready, 1)
                    act.wait_ge(gate_sub, c + 1)
                    A.activation(ex[:, 0:ns], dd[:, 0:ns], ACT.Exp).then_inc(gexp_ready, 1)
                elif stage[0] == "X":
                    act.wait_ge(x0_ready, EK * (c + 1))
                    for k in range(EK):
                        tokens_hi(0, EK * c + k)
                elif stage[0] == "H":
                    hidden(0, 0, c, int(stage[2]))

            act.wait_ge(raw_mm, 1)
            A.activation(rows[0:TILES * NEXP, 0, :], bank[7][0:TILES * NEXP, 0:P], ACT.Copy).then_inc(raw_ready, 1)
            A.activation(rows_sp[:], bank[7][0:NEXP, P:P + NSP], ACT.Copy).then_inc(raw_ready, 1)
            A.activation(h2sp[:], bank[7][:, P + NSP:P + NSP + EK * NSP].rearrange("p (k t) -> p k t", t=NSP),
                         ACT.Copy).then_inc(raw_ready, 1)

            def unit(e, par, c):
                for m in range(HK):
                    hidden(e, par, c, m)

            units(unit, act.Fori)

        @block.vector
        def _(dve):
            V = nc.vector
            steps = Steps(dve, dve_step)

            def low_half(out, src, scale, hi):
                return V.scalar_tensor_tensor(out=out, in0=src, scalar=scale, in1=hi, op0=ALU.mult,
                                              op1=ALU.subtract)

            def norm_stats(src, which, c):
                ns = len(slots_of(c))
                for i in range(ns):
                    steps.did(V.bn_stats(stats[:, i, :], src(i)))
                steps.wait()
                for i in range(ns):
                    ins = V.bn_aggr(mean[which][c][:, i, :], stats[:, i, :])
                ins.then_inc(mean_ready, 1)
                dve.wait_ge(mean_ready, norm_count(which, c))

            def softmax_front(logits, ns):
                steps.then(V.tensor_reduce(mx[:, 0:ns], logits, AX, ALU.max))
                return V.tensor_tensor(dd[:, 0:ns], logits, mx[:, 0:ns].unsqueeze(2).to_broadcast([P, ns, HEADS]),
                                       ALU.subtract)

            def softmax_back(out, ns):
                steps.then(V.tensor_reduce(sm[:, 0:ns], ex[:, 0:ns], AX, ALU.add))
                steps.then(V.reciprocal(sm[:, 0:ns], sm[:, 0:ns]))
                return V.tensor_tensor(out, ex[:, 0:ns], sm[:, 0:ns].unsqueeze(2).to_broadcast([P, ns, HEADS]),
                                       ALU.mult)

            def tokens_lo(par, piece):
                c, k = piece // EK, piece % EK
                a, w = col0(c), width(c)
                low_half(xl[par][:, k, a:a + w], X32[:, k, a:a + w], SXS, xh[par][:, k, a:a + w]
                         ).then_inc(xs_lo, 1)

            def weights_lo(par, i):
                a = i * HID
                low_half(wl[:, par, a:a + HID], wst[:, par, a:a + HID], SW, wh[:, par, a:a + HID]
                         ).then_inc(ew_lo, 1)

            dve.wait_ge(tokw_hi, 1)
            low_half(twl, tw, SW, twh).then_inc(tokw_lo, 1)
            for c in range(NCH):
                for i in range(2):
                    k = i * (DK // 2)
                    dve.wait_ge(px_hi, 2 * c + i + 1)
                    low_half(pxl[:, c, k:k + DK // 2], px[:, c, k:k + DK // 2], SX, pxh[:, c, k:k + DK // 2]
                             ).then_inc(px_lo, 1)
                if c == 0:
                    dve.wait_ge(added_hi, 1)
                    low_half(add_lo[:], add_rows[:], SR, add_hi[:]).then_inc(added_lo, 1)

            def find_ties():
                cut = lo[:].bitcast(F32).unsqueeze(1).to_broadcast([P, SLOTS, NEXP])
                steps.did(V.tensor_tensor(gt[:], SC[:], cut, ALU.is_gt))
                steps.then(V.tensor_tensor(eq[:], SC[:], cut, ALU.is_equal))
                with nc.allow_low_precision(reason="a count up to nine: exact in float16"):
                    V.tensor_reduce(esum[:], eq[:, 1:].rearrange("p s e -> p e s"), AX, ALU.add
                                    ).then_inc(tie_ready, 1)

            def take():
                dve.wait_ge(rank_mm, 1)
                steps.then(V.tensor_scalar(room[:], bank[7][:, 0:NEXP], -1.0, float(CAP), ALU.mult, ALU.add))
                steps.then(V.tensor_tensor(allow[:], eq[:], room[:].unsqueeze(1).to_broadcast([P, SLOTS, NEXP]),
                                           ALU.mult))
                steps.then(V.scalar_tensor_tensor(out=allow[:], in0=gt[:], scalar=TIE_BIG, in1=allow[:],
                                                  op0=ALU.mult, op1=ALU.add))
                V.tensor_tensor(keep[:], bank[7][:, 128:128 + TILES * NEXP].rearrange("p (s e) -> p s e", e=NEXP),
                                allow[:, 1:], ALU.is_lt).then_inc(rank_read, 1)
                for t in range(2):
                    steps.did(V.tensor_tensor(allow_sp[:, t], allow[:, 0],
                                              k16[:, K_SPSEL + t:K_SPSEL + t + 1].to_broadcast([P, NEXP]), ALU.mult))
                dve.wait_ge(rank_read, 1)
                for e in range(RAW):
                    steps.did(V.tensor_scalar(keep_s[:, e], keep[:, :, e], 1.0 / (ST_ * SW), None, ALU.mult))
                V.tensor_tensor(SM[:], SC[:, 1:], keep[:], ALU.mult).then_inc(sm_ready, 1)

            def copy_special_ranks():
                dve.wait_ge(rank_sp_mm, 1)
                V.tensor_copy(rank_sp, bank[7][:, :].rearrange("p (b t e) -> p b t e", b=B, t=2)
                              ).then_inc(rank_sp_read, 1)

            def take_specials():
                dve.wait_ge(asp_ready, 1)
                dve.wait_ge(rank_sp_read, 1)
                for t in range(2):
                    steps.did(V.tensor_tensor(msp[:, :, t], rank_sp[:, :, t], asp[:, t:t + 1].to_broadcast([P, B, NEXP]),
                                              ALU.is_lt))

            def sum_tile(e, i):
                if i in (0, 3, 5):
                    last = {0: 1, 3: 2, 5: 3}[i]
                    dve.wait_ge(dn_mm, NCH * (NEXP - 1 if e is None else e) + last)
                    steps.wait()
                src = sums(i)
                dst = OUT[:, i, :]
                if e == 0:
                    ins = V.scalar_tensor_tensor(out=dst, in0=src, scalar=keep_s[:, 0, i:i + 1],
                                                 in1=H[:, 1 + i, :], op0=ALU.mult, op1=ALU.add)
                elif e is not None:
                    ins = V.scalar_tensor_tensor(out=dst, in0=src, scalar=keep_s[:, e, i:i + 1], in1=dst,
                                                 op0=ALU.mult, op1=ALU.add)
                else:
                    ins = V.scalar_tensor_tensor(out=dst, in0=src, scalar=1.0 / (ST_ * SW), in1=dst,
                                                 op0=ALU.mult, op1=ALU.add)
                ins.then_inc(out_ready if e is None else sums_read, 1)

            def special_sums(first, count, done):
                spec = bank[0][:, 0:EK * NEXP * NSP].rearrange("p (k e t) -> p k e t", k=EK, e=NEXP)
                V.tensor_scalar(ysp[:, :, first:first + count], spec[:, :, first:first + count], 1.0 / (ST_ * SW),
                                None, ALU.mult).then_inc(done, 1)

            def special_outputs():
                special_sums(RAW, NEXP - RAW, dve_step)
                steps.n += 1
                steps.wait()
                for k in range(EK):
                    for t in range(NSP):
                        steps.did(V.tensor_tensor(prod[:, k * NSP + t], msp[:, :, t],
                                                  ysp[:, k, :, t].unsqueeze(1).to_broadcast([P, B, NEXP]),
                                                  ALU.mult))
                steps.wait()
                steps.then(V.tensor_reduce(osum.rearrange("p k t b -> p (k t b)"),
                                           prod.rearrange("p x b e -> p (x b) e"), AX, ALU.add))
                V.tensor_tensor(osp, osum, h2sp[:].unsqueeze(3).to_broadcast([P, EK, NSP, B]), ALU.add
                                ).then_inc(osp_ready, 1)

            def beside(n):
                if n == 22:
                    copy_special_ranks()
                if n == 23:
                    take_specials()
                if n == (NEXP * NCH - 1) * HK + 1:
                    special_outputs()

            def sums_beside(n):
                if n == (NEXP * NCH - 1) * HK:
                    dve.wait_ge(sums_read, RAW * (TILES + 1))
                    for i in range(3):
                        sum_tile(None, i)
                for e, at_ in ((0, {18: (0, 3), 20: (3, 5), 21: (5, 7), 22: (7, 9)}),
                               (1, {22: (0, 2), 23: (2, 3), 24: (3, 5), 28: (5, 9)})):
                    if n in at_:
                        for i in range(*at_[n]):
                            sum_tile(e, i)
                            if i == 0:
                                special_sums(e, 1, sums_read)

            def reached(candidates):
                V.tensor_tensor(ge[:].rearrange("p s c e -> p c s e"),
                                SC[:].unsqueeze(1).to_broadcast([P, NCAND, SLOTS, NEXP]),
                                candidates[:].bitcast(F32).unsqueeze(2).to_broadcast([P, NCAND, SLOTS, NEXP]),
                                ALU.is_ge).then_inc(ge_ready, 1)

            def with_bits(out, base, r):
                steps.did(V.tensor_tensor(out[:], base[:].unsqueeze(1).to_broadcast([P, NCAND, NEXP]),
                                          cand[:, r].unsqueeze(2).to_broadcast([P, NCAND, NEXP]), ALU.bitwise_or))

            def search_round(r):
                if r + 1 < ROUNDS:
                    steps.wait()
                    with_bits(ahead_of, lo, r + 1)
                dve.wait_ge(count_mm, r + 1)
                V.tensor_scalar(fl[:], bank[7][:, 0:NCAND * NEXP].rearrange("p (c e) -> p c e", e=NEXP),
                                float(CAP), 2.0 ** (BITS * (ROUNDS - 1 - r)), ALU.is_ge, ALU.mult
                                ).then_inc(flags_read, 1)
                dve.wait_ge(flags_read, r + 1)
                with nc.allow_low_precision(reason="a few equal powers of two: exact in int32"):
                    steps.then(V.tensor_reduce(inc[:], fl[:].rearrange("p c e -> p e c"), AX, ALU.add))
                if r + 1 < ROUNDS:
                    steps.then(V.tensor_tensor(mid[:], ahead_of[:],
                                               inc[:].unsqueeze(1).to_broadcast([P, NCAND, NEXP]),
                                               ALU.bitwise_or))
                    reached(mid)
                steps.did(V.tensor_tensor(lo[:], lo[:], inc[:], ALU.bitwise_or))

            def hidden(e, par, c, m):
                static = isinstance(e, int)
                w, j = width(c), e * NCH + c
                n, i = j * HK + m, c * HK + m
                dve.wait_ge(u_mm, n + 1)
                dve.wait_ge(silu_ready, n + 1)
                if not static or n >= 2:
                    dve.wait_ge(h_lo, n - 1)
                V.scalar_tensor_tensor(out=Tt[:, m % 2, 0:w], in0=hidden_bank(static, e, i, 1)[:, 0:w],
                                       scalar=ST_ / (SXS * SW), in1=sg[:, m % 2, 0:w], op0=ALU.mult,
                                       op1=ALU.mult).then_inc(t_ready, 1)
                if static:
                    for r in rounds_at(n):
                        search_round(r)
                        if r + 1 == ROUNDS:
                            steps.wait()
                            find_ties()
                    if n == 18:
                        take()
                    sums_beside(n)
                for ahead, piece in token_pieces(static, e, i):
                    dve.wait_ge(xs_hi, (e + ahead) * (NCH * EK) + piece + 1)
                    tokens_lo(1 - par if ahead else par, piece)
                if not (static and e in (0, NEXP - 1)):
                    if 6 <= i:
                        if i == 6:
                            dve.wait_ge(ew_hi, e + 2)
                            if static and e == 1:
                                dve.wait_ge(ew_lo, 12)
                        weights_lo(1 - par, i - 6)
                dve.wait_ge(h_hi, n + 1)
                V.tensor_tensor(Hl[:, (par + c) % 2, m, 0:w], Tt[:, m % 2, 0:w],
                                Hh[:, (par + c) % 2, m, 0:w], ALU.subtract).then_inc(h_lo, 1)
                if static:
                    beside(n)

            for stage in DVE_ORDER:
                c, par = int(stage[1]), int(stage[1]) % 2
                w, sl = width(c), slots_of(min(c, NCH - 1))
                ns, s0 = len(sl), sl[0]
                q, qk, vp, th = q_[par], qk_[par], vp_[par], th_[par]
                if stage == "W0":
                    a = EK * INNER
                    dve.wait_ge(qw_hi, 1)
                    low_half(qwl[:, 0:a], qw[:, 0:a], SW, qwh[:, 0:a]).then_inc(qw_lo, 1)
                elif stage == "W1":
                    dve.wait_ge(chan_e, 1)
                    steps.then(V.tensor_scalar(decay[:], ez[:], 0.5, 0.5, ALU.mult, ALU.add))
                    steps.then(V.tensor_scalar(ez[:], ez[:], -0.5, 0.5, ALU.mult, ALU.add))
                    steps.did(V.tensor_scalar(v_scale[:], ez[:], 1.0 / (SY * SW * SA), None, ALU.mult))
                    steps.did(V.scalar_tensor_tensor(out=v_bias[:], in0=ez[:], scalar=1.0 / SA, in1=bv,
                                                     op0=ALU.mult, op1=ALU.mult))
                    steps.did(V.tensor_scalar(bk_s[:], bk, SY * SW, None, ALU.mult))
                    V.tensor_scalar(aug_h[:], aug, 0.5, None, ALU.mult).then_inc(chan_ready, 1)
                elif stage[0] == "A":
                    dve.wait_ge(tok_mm, max(TOK_DONE[s] for s in sl))
                    norm_stats(lambda i: tok_out(s0 + i), 0, c)
                elif stage[0] == "B":
                    dve.wait_ge(vec_in, 16)
                    for i, s in enumerate(sl):
                        V.scalar_tensor_tensor(out=H[:, s, :], in0=tok_out(s), scalar=mean[0][c][:, i, 0:1],
                                               in1=gam, op0=ALU.subtract, op1=ALU.mult).then_inc(tok_read, 1)
                elif stage[0] == "C":
                    dve.wait_ge(tok_read, slots_until(c))
                    dve.wait_ge(rstd_ready, norm_count(0, c))
                    for i, s in enumerate(sl):
                        steps.did(V.scalar_tensor_tensor(out=H[:, s, :], in0=H[:, s, :],
                                                         scalar=rstd[0][c][:, i:i + 1], in1=bet, op0=ALU.mult,
                                                         op1=ALU.add))
                    steps.wait()
                    if c == 0:
                        dve.wait_ge(cls_in, 16)
                        steps.then(V.tensor_copy(H[0:1, 0, :], cls_sb[0:1, :]))
                    norm_stats(lambda i: H[:, s0 + i, :], 1, c)
                elif stage[0] == "T":
                    for k in range(EK):
                        dve.wait_ge(yT_hi, EK * c + k + 1)
                        low_half(yTl[:, k, 0:w], bank[6 + k][:, 0:w], SY, yTh[:, k, 0:w]).then_inc(yT_lo, 1)
                elif stage[0] == "Q":
                    m = int(stage[2])
                    n = MK * c + m
                    dve.wait_ge(k_mm, n + 1)
                    dve.wait_ge(q_read, n + 1)
                    if c == 2 and m == 0:
                        dve.wait_ge(o_lo, 1)
                    V.scalar_tensor_tensor(out=qk[:, m, 0:w], in0=bank[1][:, 0:w], scalar=bk_s[:, m:m + 1],
                                           in1=q[:, m, 0:w], op0=ALU.add, op1=ALU.mult).then_inc(qk_ready, 1)
                    if n == 2:
                        steps.then(V.tensor_copy(DECs, decay[:].unsqueeze(2).unsqueeze(3)
                                                 .to_broadcast([P, MK, B, SEG])))
                        steps.did(V.memset(DECs[:, :, :, 0], 0.0))
                elif stage[0] == "L":
                    dve.wait_ge(logit_mm, c + 1)
                    lg = bank[5][:, 0:ns * HEADS].rearrange("p (s h) -> p s h", h=HEADS)
                    softmax_front(lg, ns).then_inc(logit_sub, 1)
                    dve.wait_ge(exp_ready, c + 1)
                    steps.then(softmax_back(attn[:, 0:ns], ns))
                    steps.then(V.tensor_scalar(attn_hl[:, 0:ns, 0], attn[:, 0:ns], SA, None, ALU.mult))
                    low_half(attn_hl[:, 0:ns, 1], attn[:, 0:ns], SA, attn_hl[:, 0:ns, 0]).then_inc(attn_ready, 1)
                elif stage[0] == "R":
                    off = NSP if c == 0 else 0
                    if c:
                        steps.did(V.tensor_copy(Us[:, :, :, 0], STs[:, :, :, SEG - 1]))
                    dve.wait_ge(v_read, MK * (c + 1))
                    for m in range(MK):
                        dve.wait_ge(aB_mm, MK * c + m + 1)
                        aB = bank[3 + m % 2]
                        if c == 0:
                            steps.did(V.tensor_tensor(us2[:, m, :], aB[:, 0:NSP], vp[:, m, 0:NSP], ALU.mult))
                        V.tensor_tensor(Us[:, m, :, 1:].rearrange("p b t -> p t b"),
                                        aB[:, off:off + CW].rearrange("p (t b) -> p t b", b=B),
                                        vp[:, m, off:off + CW].rearrange("p (t b) -> p t b", b=B),
                                        ALU.mult).then_inc(u_ready, 1)
                    if c == 0:
                        steps.wait()
                        steps.did(V.tensor_copy(sp_state[:, :, 0], us2[:, :, 0]))
                        steps.then(V.tensor_tensor(sp_tmp[:], us2[:, :, 0], decay[:], ALU.mult))
                        steps.then(V.tensor_tensor(sp_state[:, :, 1], us2[:, :, 1], sp_tmp[:], ALU.add))
                        steps.did(V.tensor_copy(Us[:, :, :, 0], sp_state[:, :, 1:2].to_broadcast([P, MK, B])))
                elif stage[0] == "V":
                    steps.wait()
                    dve.wait_ge(u_ready, MK * (c + 1))
                    steps.then(V.tensor_tensor_scan(STt, DEC, U, 0.0, ALU.mult, ALU.add))
                elif stage[0] == "Y":
                    off = NSP if c == 0 else 0
                    if c == 0:
                        steps.did(V.scalar_tensor_tensor(out=qk[:, :, 0:NSP], in0=q[:, :, 0:NSP], scalar=SO,
                                                         in1=sp_state[:], op0=ALU.mult, op1=ALU.mult))
                    for m in range(MK):
                        V.scalar_tensor_tensor(
                            out=qk[:, m, off:off + CW].rearrange("p (t b) -> p t b", b=B),
                            in0=q[:, m, off:off + CW].rearrange("p (t b) -> p t b", b=B), scalar=SO,
                            in1=STs[:, m, :, 1:].rearrange("p b t -> p t b"), op0=ALU.mult,
                            op1=ALU.mult).then_inc(qs_ready, 1)
                    dve.wait_ge(qs_ready, MK * (c + 1))
                elif stage[0] == "P":
                    if c == NCH - 1:
                        dve.wait_ge(sig_ready, c + 1)
                        for m in range(1, MK, 2):
                            V.tensor_tensor(qk[:, m, 0:w], qk[:, m, 0:w], th[:, m, 0:w], ALU.add
                                            ).then_inc(o_odd, 1)
                        dve.wait_ge(o_odd, MK // 2)
                    for m in range(MK):
                        dve.wait_ge(o_hi, MK * c + m + 1)
                        ins = V.tensor_tensor(oTl[:, m, 0:w], qk[:, m, 0:w], oTh[:, m, 0:w], ALU.subtract)
                    ins.then_inc(o_lo, 1)
                elif stage[0] == "O":
                    dve.wait_ge(wo_mm, slots_until(c))
                    norm_stats(lambda i: wo_out(i), 2, c)
                elif stage[0] == "N":
                    for i, s in enumerate(sl):
                        V.scalar_tensor_tensor(out=Y[:, s, :], in0=wo_out(i), scalar=mean[2][c][:, i, 0:1],
                                               in1=lns, op0=ALU.subtract, op1=ALU.mult).then_inc(wo_read, 1)
                elif stage[0] == "Z":
                    dve.wait_ge(wo_read, slots_until(c))
                    dve.wait_ge(rstd_ready, norm_count(2, c))
                    dve.wait_ge(bias_in, c + 1)
                    for i, s in enumerate(sl):
                        steps.did(V.scalar_tensor_tensor(out=H[:, s, :], in0=Y[:, s, :],
                                                         scalar=rstd[2][c][:, i:i + 1], in1=H[:, s, :],
                                                         op0=ALU.mult, op1=ALU.add))
                    steps.wait()
                    norm_stats(lambda i: H[:, s0 + i, :], 3, c)
                elif stage[0] == "G":
                    dve.wait_ge(gate_mm, c + 1)
                    lg = bank[5][:, 0:ns * NEXP].rearrange("p (s h) -> p s h", h=NEXP)
                    softmax_front(lg, ns).then_inc(gate_sub, 1)
                    dve.wait_ge(gexp_ready, c + 1)
                    softmax_back(SC[:, s0:s0 + ns], ns).then_inc(sc_ready, 1)
                elif stage[0] == "X":
                    dve.wait_ge(s0_mm, c + 1)
                    for k in range(EK):
                        V.tensor_tensor(X32[:, k, col0(c):col0(c) + w], y2T[:, k, col0(c):col0(c) + w],
                                        bank[5][:, 0:w], ALU.mult).then_inc(x0_ready, 1)
                    dve.wait_ge(x0_ready, EK * (c + 1))
                    for k in range(EK):
                        dve.wait_ge(xs_hi, EK * c + k + 1)
                        tokens_lo(0, EK * c + k)
                elif stage[0] == "H":
                    hidden(0, 0, c, int(stage[2]))

            def unit(e, par, c):
                for m in range(HK):
                    hidden(e, par, c, m)
                if isinstance(e, int) and (e, c) == (RAW, 0):
                    sums_beside((RAW * NCH + 1) * HK)

            dve.wait_ge(k16_dma, 32)
            with_bits(mid, lo, 0)
            steps.wait()
            reached(mid)
            units(unit, dve.Fori)

            for i in range(3, TILES):
                sum_tile(None, i)

        @block.tensor
        def _(pe):
            mm = nc.tensor.matmul

            def cut_products(out, pairs, start=True, stop=True, free=False):
                for i, ((ah, al), (bh, bl)) in enumerate(pairs):
                    mm(out, ah, bh, start=start and i == 0, stop=False, skip_group_check=free)
                    mm(out, ah, bl, start=False, stop=False, skip_group_check=free)
                    ins = mm(out, al, bh, start=False, stop=stop and i == len(pairs) - 1,
                             skip_group_check=free)
                return ins

            def const(at_):
                return k16[:, at_:at_ + P]

            def count(r):
                if r:
                    pe.wait_ge(flags_read, r)
                else:
                    pe.wait_ge(raw_ready, 3)
                pe.wait_ge(ge_ready, r + 1)
                for s in range(SLOTS):
                    ins = mm(bank[7][:, 0:NCAND * NEXP], const(K_ONES) if s else const(K_W32),
                             ge[:, s].rearrange("p c e -> p (c e)"), start=s == 0, stop=s == SLOTS - 1)
                ins.then_inc(count_mm, 1)

            def beside(n):
                if n == 18:
                    pe.wait_ge(tie_ready, 1)
                    pe.wait_ge(flags_read, ROUNDS)
                    for s in range(SLOTS):
                        mm(bank[7][:, 0:NEXP], const(K_ONES) if s else const(K_W32), gt[:, s], start=s == 0,
                           stop=s == SLOTS - 1)
                    rank = bank[7][:, 128:128 + TILES * NEXP]
                    mm(rank, const(K_EARLIER), esum[:].unsqueeze(1).to_broadcast([P, TILES, NEXP]), start=True,
                       stop=False)
                    for s in range(1, TILES):
                        mm(bank[7][:, 128 + s * NEXP:128 + TILES * NEXP], const(K_SAME),
                           eq[:, s:s + 1].to_broadcast([P, TILES - s, NEXP]), start=False, stop=False)
                    mm(rank, const(K_LOWER), eq[:, 1:].rearrange("p s e -> p (s e)"), start=False, stop=False)
                    mm(rank, const(K_SPEC), eq[:, 0:1].to_broadcast([P, TILES, NEXP]), start=False, stop=True
                       ).then_inc(rank_mm, 1)
                if n == 19:
                    pe.wait_ge(rank_read, 1)
                    pe.wait_ge(sm_ready, 1)
                    nc.tensor.transpose(bank[7][0:TILES * NEXP, 0:P], SM[:].rearrange("p s e -> p (s e)"), ident)
                    mm(bank[7][:, P:P + 2 * NEXP], const(K_ONES), allow_sp[:].rearrange("p t e -> p (t e)"),
                       start=True, stop=True).then_inc(rows_mm, 1)
                if n == 22:
                    pe.wait_ge(sp_tie_ready, 1)
                    pe.wait_ge(asp_ready, 1)
                    mm(bank[7][:, :], const(K_ONES), tri_e.rearrange("p b t e -> p (b t e)"), start=True,
                       stop=False)
                    mm(bank[7][:, :], const(K_ONES), sp_e.rearrange("p b t e -> p (b t e)"), start=False,
                       stop=True).then_inc(rank_sp_mm, 1)

            ZEROED = [(0, 1), (2, 3), (4,)]

            def zero_sums(banks):
                for b_ in banks:
                    mm(bank[b_][:, :], zero16[:], k16[:, 0:BANK], start=True, stop=False,
                       skip_group_check=True)

            def down(e, par, c):
                static = isinstance(e, int)
                j = e * NCH + c
                pe.wait_ge(h_lo, (j + 1) * HK)
                pe.wait_ge(h_hi, (j + 1) * HK)
                if c == 0:
                    pe.wait_ge(ew_lo, (e + 1) * 6)
                if static and e < RAW:
                    if e == 0:
                        for s_ in (q_read, qk_ready, v_read, u_ready):
                            pe.wait_ge(s_, MK * NCH)
                        if c:
                            pe.wait_ge(wo_read, SLOTS)
                    else:
                        pe.wait_ge(sums_read, (e - 1) * (TILES + 1) + (4, 8, 10)[c])
                    zero_sums(ZEROED[c])
                jb = (par + c) % 2
                off = NSP if c == 0 else 0
                for i in range(TPC):
                    a = off + i * P
                    ins = cut_products(sums(TPC * c + i),
                                       [((Hh[:, jb, m, a:a + P], Hl[:, jb, m, a:a + P]),
                                         (w2_of(wh, par, m), w2_of(wl, par, m))) for m in range(HK)], start=False,
                                       stop=False, free=True)
                if c == 0:
                    for k in range(EK):
                        o = k * NEXP * NSP
                        dst = (bank[0][:, o + e * NSP:o + (e + 1) * NSP] if static
                               else bank[0][:, bass.ds(e * NSP + o, NSP)])
                        ins = cut_products(dst, [((w2_of(wh, par, m)[:, k * P:(k + 1) * P],
                                                   w2_of(wl, par, m)[:, k * P:(k + 1) * P]),
                                                  (Hh[:, jb, m, 0:NSP], Hl[:, jb, m, 0:NSP]))
                                                 for m in range(HK)], start=False, stop=False, free=True)
                ins.then_inc(dn_mm, 1)

            def hidden(e, par, c, m):
                static = isinstance(e, int)
                w, j, a = width(c), e * NCH + c, col0(c)
                n, i = j * HK + m, c * HK + m
                if m == 0:
                    if c == 0:
                        pe.wait_ge(ew_lo, e * 6 + 4)
                    pe.wait_ge(xs_lo, e * (NCH * EK) + EK * (c + 1))
                    if static and j == 0:
                        pe.wait_ge(v_read, MK * NCH)
                        pe.wait_ge(yT_lo, EK * NCH)
                        pe.wait_ge(y2T_ready, EK)
                    if static and j == 2:
                        pe.wait_ge(x0_ready, EK * NCH)
                        pe.wait_ge(silu_ready, n)
                        pe.wait_ge(t_ready, n)
                    if static and (e, c) == (2, 0):
                        pe.wait_ge(rank_sp_read, 1)
                for which, done in ((0, g_mm), (1, u_mm)):
                    if static and e < 2:
                        if n:
                            pe.wait_ge((silu_ready, t_ready)[which], n)
                    elif static and (e, n) == (2, 24):
                        pe.wait_ge((silu_ready, t_ready)[which], n)
                    elif which == 0:
                        pe.wait_ge(t_ready, n - 1)
                    else:
                        pe.wait_ge(silu_ready, n)
                    cut_products(hidden_bank(static, e, i, which)[:, 0:w],
                                 [((w13_of(wh, par, which, k, m), w13_of(wl, par, which, k, m)),
                                   (xh[par][:, k, a:a + w], xl[par][:, k, a:a + w])) for k in range(EK)]
                                 ).then_inc(done, 1)
                if static:
                    for r in rounds_at(n):
                        count(r)
                    beside(n)

            def spread(c, ms):
                for m in ms:
                    n = MK * c + m
                    if n >= 2:
                        pe.wait_ge(u_ready, n - 1)
                    mm(bank[3 + m % 2][:, 0:width(c)], k16[0:2 * HEADS, K_SPREAD + m * P:K_SPREAD + (m + 1) * P],
                       attn_T[:, 0:width(c)], start=True, stop=True).then_inc(aB_mm, 1)

            def bank5_free(stage):
                for kind, read, each in (("S", logits_T_ready, 1), ("L", logit_sub, 1), ("R", attn_T_ready, 1),
                                         ("M", gate_sub, 1), ("X", x0_ready, EK)):
                    if before(stage, kind):
                        pe.wait_ge(read, each * before(stage, kind))

            pe.wait_ge(filled, 4)
            pe.wait_ge(tokw_lo, 1)
            for _ in range(24):
                mm(bank[7][:, 0:P], zero16[:], zero16[:], start=True, stop=True)
            pe.wait_ge(selectors_in, 16)
            pe.wait_ge(added_lo, 1)
            for c in range(NCH):
                pe.wait_ge(px_lo, 2 * (c + 1))
                for s in slots_of(c):
                    sel = selector[0:RROWS, s * P:(s + 1) * P]
                    mm(tok_out(s), sel, add_hi[:], start=True, stop=False)
                    ins = mm(tok_out(s), sel, add_lo[:], start=False, stop=s == 0)
                    if s:
                        a = (s - 1 - TPC * c) * P
                        ins = cut_products(tok_out(s),
                                           [((pxh[:, c, k, a:a + P], pxl[:, c, k, a:a + P]),
                                             (twh[:, k * E:(k + 1) * E], twl[:, k * E:(k + 1) * E]))
                                            for k in range(DK)], start=False, stop=True)
                    ins.then_inc(tok_mm, 1)
            pe.wait_ge(small_in, 16)
            for stage in PE_ORDER:
                c, par = int(stage[1]), int(stage[1]) % 2
                w, sl = width(c), slots_of(min(c, NCH - 1))
                ns, s0 = len(sl), sl[0]
                if stage[0] == "T":
                    for k in range(EK):
                        if c:
                            pe.wait_ge(yT_lo, EK * (c - 1) + k + 1)
                        if before(stage, "GK"):
                            pe.wait_ge(y2T_ready, before(stage, "GK"))
                        for s in sl:
                            pe.wait_ge(y_ready, s + 1)
                            a, n = slot_cols(s, c)
                            ins = nc.tensor.transpose(bank[6 + k][:, a:a + n], Y[0:n, s, k * P:(k + 1) * P],
                                                      ident[0:n, 0:n])
                        ins.then_inc(yT_mm, 1)
                elif stage[0] == "Q":
                    m = int(stage[2])
                    n = MK * c + m
                    if n == 0:
                        pe.wait_ge(tok_read, TOK_DONE[3])
                    pe.wait_ge(yT_lo, EK * (c + 1))
                    for which, done, free in ((0, q_mm, q_read), (1, k_mm, qk_ready), (2, v_mm, v_read)):
                        if n:
                            pe.wait_ge(free, n)
                        else:
                            pe.wait_ge((qw_lo, kw_lo, vw_lo)[which], 1)
                        if n == 0 and which == 2:
                            pe.wait_ge(tok_read, TOK_DONE[5])
                        cut_products(bank[which][:, 0:w],
                                     [((qkv_of(qwh, which, k, m), qkv_of(qwl, which, k, m)),
                                       (yTh[:, k, 0:w], yTl[:, k, 0:w])) for k in range(EK)]).then_inc(done, 1)
                elif stage[0] == "S":
                    pe.wait_ge(qk_ready, MK * (c + 1))
                    bank5_free(stage)
                    for m in range(MK):
                        ins = mm(bank[5][0:HEADS, 0:w], blk[:, m, :], qk_[par][:, m, 0:w], start=m == 0,
                                 stop=m == MK - 1)
                    ins.then_inc(logits_T_mm, 1)
                elif stage[0] == "L":
                    pe.wait_ge(logits_T_ready, c + 1)
                    bank5_free(stage)
                    for i, s in enumerate(sl):
                        a, _ = slot_cols(s, c)
                        ins = nc.tensor.transpose(bank[5][:, i * HEADS:(i + 1) * HEADS], logits_T[:, a:a + P],
                                                  ident[0:HEADS, 0:HEADS])
                    ins.then_inc(logit_mm, 1)
                elif stage[0] == "R":
                    if c == 0:
                        pe.wait_ge(k16_dma, 32)
                    pe.wait_ge(attn_ready, c + 1)
                    bank5_free(stage)
                    pe.wait_ge(tok_read, SLOTS)
                    if before(stage, "O"):
                        pe.wait_ge(wo_read, slots_until(before(stage, "O") - 1))
                    for i, s in enumerate(sl):
                        a, cnt = slot_cols(s, c)
                        ins = nc.tensor.transpose(
                            bank[5][0:2 * HEADS, :].bitcast(F16)[:, a:a + cnt],
                            attn_hl[0:cnt, i].rearrange("p t h -> p (t h)"), k16[0:cnt, K_ID16:K_ID16 + cnt])
                    ins.then_inc(attn_T_mm, 1)
                    pe.wait_ge(attn_T_ready, c + 1)
                    spread(c, (0, 1))
                elif stage[0] == "V":
                    spread(c, (2, 3))
                elif stage[0] == "O":
                    if c == 0:
                        pe.wait_ge(ow_lo, 1)
                        pe.wait_ge(bo_selector_in, 16)
                    pe.wait_ge(o_lo, c + 1)
                    pe.wait_ge(u_ready, MK * before(stage, "V"))
                    if c:
                        pe.wait_ge(wo_read, s0)
                    for i, s in enumerate(sl):
                        a, _ = slot_cols(s, c)
                        mm(wo_out(i), bo_selector[:], add_hi[:], start=True, stop=False)
                        mm(wo_out(i), bo_selector[:], add_lo[:], start=False, stop=False)
                        cut_products(wo_out(i), [((oTh[:, m, a:a + P], oTl[:, m, a:a + P]),
                                                  (owh[:, m * E:(m + 1) * E], owl[:, m * E:(m + 1) * E]))
                                                 for m in range(MK)], start=False).then_inc(wo_mm, 1)
                elif stage[0] in "GK":
                    k = "GK".index(stage[0])
                    pe.wait_ge(yT_lo, EK * before(stage, "T"))
                    if c:
                        pe.wait_ge(y2T_ready, EK * c + k)
                    for s in sl:
                        pe.wait_ge(y2_ready, s + 1)
                        a, n = slot_cols(s, c)
                        ins = nc.tensor.transpose(y2T_bank(c, k)[:, a:a + n], Y[0:n, s, k * P:(k + 1) * P],
                                                  ident[0:n, 0:n])
                    ins.then_inc(y2T_mm, 1)
                elif stage[0] == "M":
                    pe.wait_ge(y2T_ready, EK * (c + 1))
                    bank5_free(stage)
                    for i, s in enumerate(sl):
                        a, _ = slot_cols(s, c)
                        for k in range(EK):
                            ins = mm(bank[5][:, i * NEXP:(i + 1) * NEXP], y2T[:, k, col0(c) + a:col0(c) + a + P],
                                     wg[:, k, :], start=k == 0, stop=k == EK - 1)
                    ins.then_inc(gate_mm, 1)
                elif stage[0] == "H":
                    hidden(0, 0, c, int(stage[2]))
                elif stage[0] == "D":
                    down(0, 0, c)
                elif stage[0] == "X":
                    pe.wait_ge(sc_ready, c + 1)
                    bank5_free(stage)
                    for s in sl:
                        a, n = slot_cols(s, c)
                        ins = mm(bank[5][:, a:a + n], SC[:, s, 0:1].to_broadcast([P, P]), ident[:, 0:n],
                                 start=True, stop=True)
                    ins.then_inc(s0_mm, 1)

            nc.tensor.transpose(bank[7][0:TILES * NEXP, 0:P], SC[:, 1:].rearrange("p s e -> p (s e)"), ident)
            nc.tensor.transpose(bank[7][0:NEXP, P:P + NSP], SC[0:NSP, 0], ident[0:NSP, 0:NSP])
            for k in range(EK):
                a = P + NSP + k * NSP
                ins = nc.tensor.transpose(bank[7][:, a:a + NSP], H[0:NSP, 0, k * P:(k + 1) * P],
                                          ident[0:NSP, 0:NSP])
            ins.then_inc(raw_mm, 1)

            def unit(e, par, c):
                for m in range(HK):
                    hidden(e, par, c, m)
                if c:
                    down(e, par, c - 1)
                else:
                    down(e - 1, 1 - par, NCH - 1)
                if isinstance(e, int) and (e, c) == (RAW, 0):
                    pe.wait_ge(sums_read, RAW * (TILES + 1))
                    zero_sums(range(5))

            units(unit, pe.Fori)
            down(NEXP - 1, (NEXP - 1) % 2, NCH - 1)


def shape_constants():
    import numpy as np
    p = np.arange(P)
    j, b = p // B, p % B
    k16 = np.zeros((P, K16), np.float16)
    k16[:, K_ONES:K_ONES + P] = 1
    k16[0:2, K_W32:K_W32 + P] = B
    k16[:, K_EARLIER:K_EARLIER + P] = b[:, None] < b[None, :]
    same = b[:, None] == b[None, :]
    k16[:, K_SAME:K_SAME + P] = same
    k16[:, K_LOWER:K_LOWER + P] = same & (j[:, None] < j[None, :])
    k16[0:2, K_SPEC:K_SPEC + P] = b[None, :] + 1
    k16[:, K_TRI:K_TRI + B] = b[:, None] < np.arange(B)[None, :]
    coef = np.zeros((P, B, 2))
    coef[0] = np.arange(B)[:, None] + np.arange(2)[None, :]
    coef[1] = np.arange(B)[:, None]
    k16[:, K_COEF:K_COEF + 2 * B] = coef.reshape(P, -1)
    k16[:, K_ID16:K_ID16 + P] = np.eye(P)
    spread = np.arange(INNER)[None, :] // HDIM == (np.arange(2 * HEADS) % HEADS)[:, None]
    k16[0:2 * HEADS, K_SPREAD:] = spread
    k16[0, K_SPSEL] = k16[1, K_SPSEL + 1] = 1
    selectors = np.zeros((RROWS, SLOTS + 1, P), np.float16)
    for s in range(1, SLOTS):
        selectors[p // B + (P // B) * (s - 1), s, p] = SX * SW / SR
        selectors[R_BIAS, s] = SX * SW / SR
    selectors[R_BO, SLOTS] = SO * SW / SR
    selectors[R_CLS:R_POS0 + 1, 0, 1] = SX * SW / SR
    k32 = np.zeros((P, K32), np.float32)
    k32[:, K_IDENT:K_IDENT + P] = np.eye(P)
    for m in range(MK):
        for h in range(HEADS):
            k32[:, K_BLK + m * HEADS + h] = (P * m + p) // HDIM == h
    step = BITS * (ROUNDS - 1 - np.arange(ROUNDS))
    cand = np.tile(((np.arange(NCAND) + 1)[None, :] << step[:, None])[None], (P, 1, 1)).astype(np.int32)
    return k16, k32, cand, selectors.reshape(RROWS, -1)


def kernel(x, cls_tok, L0_tok_W, L0_tok_b, L0_tok_cls_token, L0_tok_pos_embedding, L0_tok_gamma, L0_tok_beta,
           L0_attn_Wq, L0_attn_bq, L0_attn_Wk, L0_attn_bk, L0_attn_Wv, L0_attn_bv, L0_attn_Wo, L0_attn_bo,
           L0_attn_alpha, L0_attn_aug_param, L0_attn_ln_scale, L0_attn_ln_bias, L0_ffn_wg, L0_ffn_w1, L0_ffn_w3,
           L0_ffn_w2):
    import numpy as np
    import concourse.bacc as bacc
    from concourse.bass_utils import run_bass_kernel_spmd

    def rows(w, k):
        w = np.asarray(w)
        return w.reshape(k, P, -1).transpose(1, 0, 2)

    def channels(*vs):
        return np.stack([np.asarray(v).reshape(MK, P).T for v in vs], 1)

    g = SIDE // PATCH
    px = np.asarray(x).reshape(B, C, g, PATCH, g, PATCH).transpose(1, 3, 5, 2, 4, 0).reshape(D, T)
    k16, k32, cand, selectors = shape_constants()
    w1 = np.stack([rows(w, EK) for w in np.asarray(L0_ffn_w1)])
    w3 = np.stack([rows(w, EK) for w in np.asarray(L0_ffn_w3)])
    w2 = np.stack([rows(w, HK) for w in np.asarray(L0_ffn_w2)])
    chan = channels(L0_attn_bq, L0_attn_bk, L0_attn_bv, L0_attn_alpha, L0_attn_aug_param).reshape(P, -1)
    k32[:, K_CHAN:K_WG] = chan
    k32[:, K_WG:] = rows(L0_ffn_wg, EK).reshape(P, -1)
    pos = np.asarray(L0_tok_pos_embedding)[0]
    ins = dict(
        xT=px.reshape(DK, P, NCH, CW).transpose(1, 2, 0, 3), cls_tok=np.asarray(cls_tok).reshape(1, E),
        tok_w=rows(L0_tok_W, DK).reshape(P, -1), selectors=selectors,
        added=np.concatenate([pos[1:], np.asarray(L0_tok_b).reshape(1, E),
                              np.asarray(L0_tok_cls_token).reshape(1, E), pos[0:1],
                              np.asarray(L0_attn_bo).reshape(1, E)]),
        vectors=np.concatenate([np.asarray(v) for v in (L0_tok_gamma, L0_tok_beta,
                                                        L0_attn_ln_scale, L0_attn_ln_bias)]).reshape(1, -1),
        small=k32, wqkv=np.stack([rows(w, EK) for w in (L0_attn_Wq, L0_attn_Wk, L0_attn_Wv)], 1).reshape(P, -1),
        wo=rows(L0_attn_Wo, MK).reshape(P, -1), w13=np.stack([w1, w3], 2).reshape(NEXP, P, 2 * EK * HID),
        w2=w2.reshape(NEXP, P, HK * E), k16_in=k16, cand_in=cand)
    nc = bacc.Bacc("TRN2", target_bir_lowering=False, num_devices=1)
    arrays, args = {}, {}
    for name, a in ins.items():
        a = np.ascontiguousarray(a)
        arrays[name] = a
        args[name] = nc.dram_tensor(name, a.shape, mybir.dt.from_np(a.dtype), kind="ExternalInput").ap()
    args["out_patch"] = nc.dram_tensor("out_patch", (P, TILES, E), F32, kind="ExternalOutput").ap()
    args["out_spec"] = nc.dram_tensor("out_spec", (P, EK, NSP, B), F32, kind="ExternalOutput").ap()
    vit_tower(nc, **args)
    r = run_bass_kernel_spmd(nc, [arrays], core_ids=[0]).results[0]
    out = np.empty((B, S, E), np.float32)
    out[:, NSP:] = np.asarray(r["out_patch"]).transpose(1, 0, 2).reshape(NPATCH, B, E).transpose(1, 0, 2)
    out[:, :NSP] = np.asarray(r["out_spec"]).transpose(3, 2, 1, 0).reshape(B, NSP, E)
    return out
```
